# Optimizing a Trainium2 kernel written in Bass

```python
import numpy as np
import jax
import jax.numpy as jnp

def _softmax(x, axis=-1):
    return jax.nn.softmax(x, axis=axis)

def _gelu(x):
    return jax.nn.gelu(x, approximate=True)

def _silu(x):
    return jax.nn.silu(x)

def _sigmoid(x):
    return jax.nn.sigmoid(x)

def _layernorm(x, axis=-1, eps=1e-05):
    m = jnp.mean(x, axis=axis, keepdims=True)
    v = jnp.var(x, axis=axis, keepdims=True)
    return (x - m) / jnp.sqrt(v + eps)

def _scatter_add(tgt, idx, src, axis=0):
    return tgt.at[idx].add(src)

def _segment_sum(src, seg, n):
    return jax.ops.segment_sum(src, seg, n)
kernel_name = 'mk_cond_seq_d4_seqx_r4_5c7849'

def setup_inputs(seed: int=0):
    np.random.seed(seed)
    _w = jnp.asarray

    def _rec_inputs():
        import jax
        import jax.numpy as jnp
        _rk = jax.random.key(seed)
        x = -0.0003929 + 0.9999 * jax.random.normal(jax.random.fold_in(_rk, 1), (16, 256, 256), jnp.float32)
        _lenS = 256 - jax.random.randint(jax.random.fold_in(_rk, 7), (16,), 0, max(1, 256 // 4) + 1, jnp.int32)
        _lenS2 = 256 - jax.random.randint(jax.random.fold_in(_rk, 8), (16,), 0, max(1, 256 // 4) + 1, jnp.int32)
        cond_1024 = 0.00782532 + 1.00527 * jax.random.normal(jax.random.fold_in(_rk, 11), (16, 256), jnp.float32)
        _validS = jnp.arange(256)[None, :] < _lenS[:, None]
        _validS2 = jnp.arange(256)[None, :] < _lenS2[:, None]
        _causal = jnp.tril(jnp.ones((256, 256), dtype=bool))
        mask_BxSxSx11_ik0 = jnp.where(jnp.ones((16, 256, 256, 11), dtype=bool), 0, 1).astype(jnp.int32)
        return (x, cond_1024, mask_BxSxSx11_ik0)
    x, cond_1024, mask_BxSxSx11_ik0 = _rec_inputs()

    def _L0_cond_setup():
        import jax, jax.numpy as jnp
        import numpy as np
        B, L, D, P = (8, 512, 256, 64)

        def _ln(x):
            m = x.mean(-1, keepdims=True)
            v = x.var(-1, keepdims=True)
            return (x - m) * jax.lax.rsqrt(v + 1e-05)

        def _s5(u, Lam_re, Lam_im, B_re, B_im, C_re, C_im, D_diag, log_step):
            Lam = Lam_re + 1j * Lam_im
            dt = jnp.exp(log_step)
            Lam_bar = jnp.exp(Lam * dt)
            Bc = B_re + 1j * B_im
            B_bar = ((Lam_bar - 1.0) / Lam)[:, None] * Bc
            Bu = jnp.einsum('bld,pd->blp', u.astype(B_bar.dtype), B_bar)
            A = jnp.broadcast_to(Lam_bar, Bu.shape)

            def binop(e1, e2):
                a1, b1 = e1
                a2, b2 = e2
                return (a1 * a2, a2 * b1 + b2)
            _, xs = jax.lax.associative_scan(binop, (A, Bu), axis=1)
            Cc = C_re + 1j * C_im
            return 2.0 * jnp.einsum('blp,dp->bld', xs, Cc).real + D_diag * u
        key = jax.random.key(seed)
        ks = jax.random.split(key, 16)
        inp = {'y': jax.random.normal(ks[0], (B, L, D), jnp.float32), 't': jax.random.normal(ks[1], (B, D), jnp.float32), 'Wm': jax.random.normal(ks[2], (D, 6 * D), jnp.float32) * 0.02, 'bm': jax.random.normal(ks[3], (6 * D,), jnp.float32) * 0.02, 'Lam_re': -0.5 * jnp.ones((P,), jnp.float32), 'Lam_im': jnp.pi * jnp.arange(P, dtype=jnp.float32), 'B_re': jax.random.normal(ks[4], (P, D), jnp.float32) / np.sqrt(D), 'B_im': jax.random.normal(ks[5], (P, D), jnp.float32) / np.sqrt(D), 'C_re': jax.random.normal(ks[6], (D, P), jnp.float32) / np.sqrt(P), 'C_im': jax.random.normal(ks[7], (D, P), jnp.float32) / np.sqrt(P), 'D_diag': jax.random.normal(ks[8], (D,), jnp.float32), 'log_step': jax.random.uniform(ks[9], (P,), jnp.float32, np.log(0.001), np.log(0.1)), 'Wc': jax.random.normal(ks[10], (D, 2 * D), jnp.float32) * 0.02, 'bc': jax.random.normal(ks[11], (2 * D,), jnp.float32) * 0.02, 'W1': jax.random.normal(ks[12], (D, 4 * D), jnp.float32) / np.sqrt(D), 'b1': jnp.zeros((4 * D,), jnp.float32), 'W2': jax.random.normal(ks[13], (4 * D, D), jnp.float32) / np.sqrt(4 * D) * 0.1, 'b2': jnp.zeros((D,), jnp.float32)}
        return inp
    _L0_cond_all = _L0_cond_setup()
    _L0_cond_in = {k: v for k, v in _L0_cond_all.items() if k in ('Wm', 'bm', 'Lam_re', 'Lam_im', 'B_re', 'B_im', 'C_re', 'C_im', 'D_diag', 'log_step', 'Wc', 'bc', 'W1', 'b1', 'W2', 'b2')}
    del _L0_cond_all

    def _L1_cond_setup():
        import jax, jax.numpy as jnp
        import numpy as np
        NONGT = 20
        H = 16
        NEG = -9000000000000000.0

        def _gat_attention(self_feat, cond_adj, label_bias, Wq, bq, Wk, bk, Wout, bout):
            B, N, F = self_feat.shape
            ng = min(NONGT, N)
            dh = F // H
            kv = self_feat[:, :ng]
            qh = (self_feat @ Wq.T + bq).reshape(B, N, H, dh)
            kh = (kv @ Wk.T + bk).reshape(B, ng, H, dh)
            aff = jnp.einsum('bnhd,bmhd->bnhm', qh, kh) * (1.0 / np.sqrt(dh))
            mask = cond_adj[:, :, None, :] > 0
            aff = jnp.where(mask, aff, NEG) + label_bias[:, :, None, :]
            w = jax.nn.softmax(aff, axis=-1)
            out_t = jnp.einsum('bnhm,bmf->bnhf', w, kv)
            out = jnp.einsum('bnhf,hgf->bnhg', out_t, Wout) + bout.reshape(H, F // H)
            return out.reshape(B, N, F)

        def _forward(v, q, adj, W_self, b_self, w_bias, b_bias, Wq, bq, Wk, bk, Wout, bout):
            adj_f = adj.astype(jnp.float32)
            exp_v = v
            row_zero = exp_v.sum(-1) == 0
            q_exp = jnp.where(row_zero[..., None], 0.0, q[:, None, :])
            vcq = jnp.concatenate([exp_v, q_exp], axis=-1)
            self_feat = vcq @ W_self.T + b_self
            output = self_feat
            for d in range(2):
                A = adj_f if d == 0 else jnp.swapaxes(adj_f, 1, 2)
                A = A[:, :, :NONGT, :]
                cond = A.sum(-1)
                vb = A @ w_bias + b_bias
                output = output + _gat_attention(self_feat, cond, vb, Wq[d], bq[d], Wk[d], bk[d], Wout[d], bout[d])
            rel = jax.nn.relu(output)
            return exp_v + rel
        key = jax.random.key(seed)
        ks = jax.random.split(key, 8)
        B, N, L, F, Q = (64, 36, 11, 256, 256)
        IN = F + Q
        s = 0.02
        return {'v': jax.random.normal(ks[0], (B, N, F), jnp.float32), 'q': jax.random.normal(ks[1], (B, Q), jnp.float32), 'adj': jax.random.randint(ks[2], (B, N, N, L), 0, 2, jnp.int32), 'W_self': jax.random.normal(ks[3], (F, IN), jnp.float32) * s, 'b_self': jnp.zeros((F,), jnp.float32), 'w_bias': jax.random.normal(ks[4], (L,), jnp.float32) * s, 'b_bias': jnp.zeros((), jnp.float32), 'Wq': jax.random.normal(ks[5], (2, F, F), jnp.float32) * s, 'bq': jnp.zeros((2, F), jnp.float32), 'Wk': jax.random.normal(ks[6], (2, F, F), jnp.float32) * s, 'bk': jnp.zeros((2, F), jnp.float32), 'Wout': jax.random.normal(ks[7], (2, H, F // H, F), jnp.float32) * s, 'bout': jnp.zeros((2, F), jnp.float32)}
    _L1_cond_all = _L1_cond_setup()
    _L1_cond_in = {k: v for k, v in _L1_cond_all.items() if k in ('W_self', 'b_self', 'w_bias', 'b_bias', 'Wq', 'bq', 'Wk', 'bk', 'Wout', 'bout')}
    del _L1_cond_all

    def _L2_cond_setup():
        import jax, jax.numpy as jnp
        import numpy as np
        DIM = 256
        FF_MULT = 2
        EPS = 1e-06

        def _ln(x):
            mu = jnp.mean(x, axis=-1, keepdims=True)
            var = jnp.mean(jnp.square(x - mu), axis=-1, keepdims=True)
            return (x - mu) * jax.lax.rsqrt(var + EPS)
        key = jax.random.key(seed)
        ks = jax.random.split(key, 12)
        b, n, d = (4, 512, DIM)
        h = FF_MULT * d
        s = lambda fan_in: 1.0 / np.sqrt(fan_in)
        return {'x': jax.random.normal(ks[0], (b, n, d), jnp.float32), 't': jax.random.normal(ks[1], (b, d), jnp.float32), 'ada_w': jax.random.normal(ks[2], (d, 6 * d), jnp.float32) * s(d), 'ada_b': jnp.zeros((6 * d,), jnp.float32), 'ssm_w1': jax.random.normal(ks[3], (d, d), jnp.float32) * s(d), 'ssm_b1': jnp.zeros((d,), jnp.float32), 'ssm_w2': jax.random.normal(ks[4], (d, d), jnp.float32) * s(d), 'ssm_b2': jnp.zeros((d,), jnp.float32), 'ff_w1': jax.random.normal(ks[5], (d, h), jnp.float32) * s(d), 'ff_b1': jnp.zeros((h,), jnp.float32), 'ff_w2': jax.random.normal(ks[6], (h, d), jnp.float32) * s(h), 'ff_b2': jnp.zeros((d,), jnp.float32)}
    _L2_cond_all = _L2_cond_setup()
    _L2_cond_in = {k: v for k, v in _L2_cond_all.items() if k in ('ada_w', 'ada_b', 'ssm_w1', 'ssm_b1', 'ssm_w2', 'ssm_b2', 'ff_w1', 'ff_b1', 'ff_w2', 'ff_b2')}
    del _L2_cond_all

    def _L3_cond_setup():
        import jax, jax.numpy as jnp
        import numpy as np
        DIM = 256
        MLP_RATIO = 4
        EPS = 1e-06

        def rmsnorm(x, w):
            return x * jax.lax.rsqrt(jnp.mean(x * x, axis=-1, keepdims=True) + EPS) * w

        def film(x, cond, w, b):
            ss = cond @ w + b
            scale, shift = jnp.split(ss, 2, axis=-1)
            return x * (1.0 + scale[:, None, :]) + shift[:, None, :]
        key = jax.random.key(seed)
        ks = jax.random.split(key, 16)
        B, N, D = (4, 512, DIM)
        H = D * MLP_RATIO
        s = lambda fan_in: 1.0 / np.sqrt(fan_in)
        return {'x': jax.random.normal(ks[0], (B, N, D), jnp.float32), 'cond': jax.random.normal(ks[1], (B, D), jnp.float32), 'norm1_w': jnp.ones((D,), jnp.float32), 'film1_w': jax.random.normal(ks[2], (D, 2 * D), jnp.float32) * s(D), 'film1_b': jnp.zeros((2 * D,), jnp.float32), 'q_w': jax.random.normal(ks[3], (D, D), jnp.float32) * s(D), 'q_b': jnp.zeros((D,), jnp.float32), 'k_w': jax.random.normal(ks[4], (D, D), jnp.float32) * s(D), 'k_b': jnp.zeros((D,), jnp.float32), 'v_w': jax.random.normal(ks[5], (D, D), jnp.float32) * s(D), 'v_b': jnp.zeros((D,), jnp.float32), 'proj_w': jax.random.normal(ks[6], (D, D), jnp.float32) * s(D), 'proj_b': jnp.zeros((D,), jnp.float32), 'norm2_w': jnp.ones((D,), jnp.float32), 'film2_w': jax.random.normal(ks[7], (D, 2 * D), jnp.float32) * s(D), 'film2_b': jnp.zeros((2 * D,), jnp.float32), 'mlp_w1': jax.random.normal(ks[8], (D, H), jnp.float32) * s(D), 'mlp_b1': jnp.zeros((H,), jnp.float32), 'mlp_w2': jax.random.normal(ks[9], (H, D), jnp.float32) * s(H), 'mlp_b2': jnp.zeros((D,), jnp.float32)}
    _L3_cond_all = _L3_cond_setup()
    _L3_cond_in = {k: v for k, v in _L3_cond_all.items() if k in ('norm1_w', 'film1_w', 'film1_b', 'q_w', 'q_b', 'k_w', 'k_b', 'v_w', 'v_b', 'proj_w', 'proj_b', 'norm2_w', 'film2_w', 'film2_b', 'mlp_w1', 'mlp_b1', 'mlp_w2', 'mlp_b2')}
    del _L3_cond_all
    return {'x': x, 'cond_1024': cond_1024, 'mask_BxSxSx11_ik0': mask_BxSxSx11_ik0, 'L0_cond_Wm': _L0_cond_in['Wm'], 'L0_cond_bm': _L0_cond_in['bm'], 'L0_cond_Lam_re': _L0_cond_in['Lam_re'], 'L0_cond_Lam_im': _L0_cond_in['Lam_im'], 'L0_cond_B_re': _L0_cond_in['B_re'], 'L0_cond_B_im': _L0_cond_in['B_im'], 'L0_cond_C_re': _L0_cond_in['C_re'], 'L0_cond_C_im': _L0_cond_in['C_im'], 'L0_cond_D_diag': _L0_cond_in['D_diag'], 'L0_cond_log_step': _L0_cond_in['log_step'], 'L0_cond_Wc': _L0_cond_in['Wc'], 'L0_cond_bc': _L0_cond_in['bc'], 'L0_cond_W1': _L0_cond_in['W1'], 'L0_cond_b1': _L0_cond_in['b1'], 'L0_cond_W2': _L0_cond_in['W2'], 'L0_cond_b2': _L0_cond_in['b2'], 'L1_cond_W_self': _L1_cond_in['W_self'], 'L1_cond_b_self': _L1_cond_in['b_self'], 'L1_cond_w_bias': _L1_cond_in['w_bias'], 'L1_cond_b_bias': _L1_cond_in['b_bias'], 'L1_cond_Wq': _L1_cond_in['Wq'], 'L1_cond_bq': _L1_cond_in['bq'], 'L1_cond_Wk': _L1_cond_in['Wk'], 'L1_cond_bk': _L1_cond_in['bk'], 'L1_cond_Wout': _L1_cond_in['Wout'], 'L1_cond_bout': _L1_cond_in['bout'], 'L2_cond_ada_w': _L2_cond_in['ada_w'], 'L2_cond_ada_b': _L2_cond_in['ada_b'], 'L2_cond_ssm_w1': _L2_cond_in['ssm_w1'], 'L2_cond_ssm_b1': _L2_cond_in['ssm_b1'], 'L2_cond_ssm_w2': _L2_cond_in['ssm_w2'], 'L2_cond_ssm_b2': _L2_cond_in['ssm_b2'], 'L2_cond_ff_w1': _L2_cond_in['ff_w1'], 'L2_cond_ff_b1': _L2_cond_in['ff_b1'], 'L2_cond_ff_w2': _L2_cond_in['ff_w2'], 'L2_cond_ff_b2': _L2_cond_in['ff_b2'], 'L3_cond_norm1_w': _L3_cond_in['norm1_w'], 'L3_cond_film1_w': _L3_cond_in['film1_w'], 'L3_cond_film1_b': _L3_cond_in['film1_b'], 'L3_cond_q_w': _L3_cond_in['q_w'], 'L3_cond_q_b': _L3_cond_in['q_b'], 'L3_cond_k_w': _L3_cond_in['k_w'], 'L3_cond_k_b': _L3_cond_in['k_b'], 'L3_cond_v_w': _L3_cond_in['v_w'], 'L3_cond_v_b': _L3_cond_in['v_b'], 'L3_cond_proj_w': _L3_cond_in['proj_w'], 'L3_cond_proj_b': _L3_cond_in['proj_b'], 'L3_cond_norm2_w': _L3_cond_in['norm2_w'], 'L3_cond_film2_w': _L3_cond_in['film2_w'], 'L3_cond_film2_b': _L3_cond_in['film2_b'], 'L3_cond_mlp_w1': _L3_cond_in['mlp_w1'], 'L3_cond_mlp_b1': _L3_cond_in['mlp_b1'], 'L3_cond_mlp_w2': _L3_cond_in['mlp_w2'], 'L3_cond_mlp_b2': _L3_cond_in['mlp_b2']}

def reference(x, cond_1024, mask_BxSxSx11_ik0, L0_cond_Wm, L0_cond_bm, L0_cond_Lam_re, L0_cond_Lam_im, L0_cond_B_re, L0_cond_B_im, L0_cond_C_re, L0_cond_C_im, L0_cond_D_diag, L0_cond_log_step, L0_cond_Wc, L0_cond_bc, L0_cond_W1, L0_cond_b1, L0_cond_W2, L0_cond_b2, L1_cond_W_self, L1_cond_b_self, L1_cond_w_bias, L1_cond_b_bias, L1_cond_Wq, L1_cond_bq, L1_cond_Wk, L1_cond_bk, L1_cond_Wout, L1_cond_bout, L2_cond_ada_w, L2_cond_ada_b, L2_cond_ssm_w1, L2_cond_ssm_b1, L2_cond_ssm_w2, L2_cond_ssm_b2, L2_cond_ff_w1, L2_cond_ff_b1, L2_cond_ff_w2, L2_cond_ff_b2, L3_cond_norm1_w, L3_cond_film1_w, L3_cond_film1_b, L3_cond_q_w, L3_cond_q_b, L3_cond_k_w, L3_cond_k_b, L3_cond_v_w, L3_cond_v_b, L3_cond_proj_w, L3_cond_proj_b, L3_cond_norm2_w, L3_cond_film2_w, L3_cond_film2_b, L3_cond_mlp_w1, L3_cond_mlp_b1, L3_cond_mlp_w2, L3_cond_mlp_b2):
    import jax
    import jax.numpy as jnp

    def _L0_cond_ref(y, t, Wm, bm, Lam_re, Lam_im, B_re, B_im, C_re, C_im, D_diag, log_step, Wc, bc, W1, b1, W2, b2):
        import jax, jax.numpy as jnp
        import numpy as np
        B, L, D, P = (8, 512, 256, 64)

        def _ln(x):
            m = x.mean(-1, keepdims=True)
            v = x.var(-1, keepdims=True)
            return (x - m) * jax.lax.rsqrt(v + 1e-05)

        def _s5(u, Lam_re, Lam_im, B_re, B_im, C_re, C_im, D_diag, log_step):
            Lam = Lam_re + 1j * Lam_im
            dt = jnp.exp(log_step)
            Lam_bar = jnp.exp(Lam * dt)
            Bc = B_re + 1j * B_im
            B_bar = ((Lam_bar - 1.0) / Lam)[:, None] * Bc
            Bu = jnp.einsum('bld,pd->blp', u.astype(B_bar.dtype), B_bar)
            A = jnp.broadcast_to(Lam_bar, Bu.shape)

            def binop(e1, e2):
                a1, b1 = e1
                a2, b2 = e2
                return (a1 * a2, a2 * b1 + b2)
            _, xs = jax.lax.associative_scan(binop, (A, Bu), axis=1)
            Cc = C_re + 1j * C_im
            return 2.0 * jnp.einsum('blp,dp->bld', xs, Cc).real + D_diag * u
        mod = t @ Wm + bm
        shift_a, scale_a, gate_a, shift_ff, scale_ff, gate_ff = jnp.split(mod, 6, axis=-1)
        y_mod = _ln(y) * (1 + scale_a[:, None]) + shift_a[:, None]
        a_y = _s5(y_mod, Lam_re, Lam_im, B_re, B_im, C_re, C_im, D_diag, log_step)
        y = y + gate_a[:, None] * a_y
        cond = t @ Wc + bc
        scale_c, shift_c = jnp.split(cond, 2, axis=-1)
        y_norm = _ln(y) * (1 + scale_c[:, None]) + shift_c[:, None]
        y_mod = y_norm * (1 + scale_ff[:, None]) + shift_ff[:, None]
        h = jax.nn.gelu(y_mod @ W1 + b1)
        ff_y = h @ W2 + b2
        return y + gate_ff[:, None] * ff_y

    def _L1_cond_ref(v, q, adj, W_self, b_self, w_bias, b_bias, Wq, bq, Wk, bk, Wout, bout):
        import jax, jax.numpy as jnp
        import numpy as np
        NONGT = 20
        H = 16
        NEG = -9000000000000000.0

        def _gat_attention(self_feat, cond_adj, label_bias, Wq, bq, Wk, bk, Wout, bout):
            B, N, F = self_feat.shape
            ng = min(NONGT, N)
            dh = F // H
            kv = self_feat[:, :ng]
            qh = (self_feat @ Wq.T + bq).reshape(B, N, H, dh)
            kh = (kv @ Wk.T + bk).reshape(B, ng, H, dh)
            aff = jnp.einsum('bnhd,bmhd->bnhm', qh, kh) * (1.0 / np.sqrt(dh))
            mask = cond_adj[:, :, None, :] > 0
            aff = jnp.where(mask, aff, NEG) + label_bias[:, :, None, :]
            w = jax.nn.softmax(aff, axis=-1)
            out_t = jnp.einsum('bnhm,bmf->bnhf', w, kv)
            out = jnp.einsum('bnhf,hgf->bnhg', out_t, Wout) + bout.reshape(H, F // H)
            return out.reshape(B, N, F)

        def _forward(v, q, adj, W_self, b_self, w_bias, b_bias, Wq, bq, Wk, bk, Wout, bout):
            adj_f = adj.astype(jnp.float32)
            exp_v = v
            row_zero = exp_v.sum(-1) == 0
            q_exp = jnp.where(row_zero[..., None], 0.0, q[:, None, :])
            vcq = jnp.concatenate([exp_v, q_exp], axis=-1)
            self_feat = vcq @ W_self.T + b_self
            output = self_feat
            for d in range(2):
                A = adj_f if d == 0 else jnp.swapaxes(adj_f, 1, 2)
                A = A[:, :, :NONGT, :]
                cond = A.sum(-1)
                vb = A @ w_bias + b_bias
                output = output + _gat_attention(self_feat, cond, vb, Wq[d], bq[d], Wk[d], bk[d], Wout[d], bout[d])
            rel = jax.nn.relu(output)
            return exp_v + rel
        return _forward(v, q, adj, W_self, b_self, w_bias, b_bias, Wq, bq, Wk, bk, Wout, bout)

    def _L2_cond_ref(x, t, ada_w, ada_b, ssm_w1, ssm_b1, ssm_w2, ssm_b2, ff_w1, ff_b1, ff_w2, ff_b2):
        import jax, jax.numpy as jnp
        import numpy as np
        DIM = 256
        FF_MULT = 2
        EPS = 1e-06

        def _ln(x):
            mu = jnp.mean(x, axis=-1, keepdims=True)
            var = jnp.mean(jnp.square(x - mu), axis=-1, keepdims=True)
            return (x - mu) * jax.lax.rsqrt(var + EPS)
        emb = jnp.dot(jax.nn.silu(t), ada_w) + ada_b
        shift_msa, scale_msa, gate_msa, shift_mlp, scale_mlp, gate_mlp = jnp.split(emb, 6, axis=-1)
        norm = _ln(x) * (1.0 + scale_msa[:, None]) + shift_msa[:, None]
        h = jax.nn.gelu(jnp.dot(norm, ssm_w1) + ssm_b1, approximate=False)
        ssm_out = jnp.dot(h, ssm_w2) + ssm_b2
        x = x + gate_msa[:, None] * ssm_out
        norm2 = _ln(x) * (1.0 + scale_mlp[:, None]) + shift_mlp[:, None]
        hf = jax.nn.gelu(jnp.dot(norm2, ff_w1) + ff_b1, approximate=True)
        ff_out = jnp.dot(hf, ff_w2) + ff_b2
        x = x + gate_mlp[:, None] * ff_out
        return x

    def _L3_cond_ref(x, cond, norm1_w, film1_w, film1_b, q_w, q_b, k_w, k_b, v_w, v_b, proj_w, proj_b, norm2_w, film2_w, film2_b, mlp_w1, mlp_b1, mlp_w2, mlp_b2):
        import jax, jax.numpy as jnp
        import numpy as np
        DIM = 256
        MLP_RATIO = 4
        EPS = 1e-06

        def rmsnorm(x, w):
            return x * jax.lax.rsqrt(jnp.mean(x * x, axis=-1, keepdims=True) + EPS) * w

        def film(x, cond, w, b):
            ss = cond @ w + b
            scale, shift = jnp.split(ss, 2, axis=-1)
            return x * (1.0 + scale[:, None, :]) + shift[:, None, :]
        B, N, D = x.shape
        x_in = x
        h = film(rmsnorm(x, norm1_w), cond, film1_w, film1_b)
        Q = h @ q_w + q_b
        K = h @ k_w + k_b
        V = h @ v_w + v_b
        scores = jnp.einsum('bnd,bmd->bnm', Q, K) * D ** (-0.5)
        attn = jax.nn.softmax(scores, axis=-1)
        out = jnp.einsum('bnm,bmd->bnd', attn, V)
        x = x_in + (out @ proj_w + proj_b)
        x_in = x
        h = film(rmsnorm(x, norm2_w), cond, film2_w, film2_b)
        h = jax.nn.gelu(h @ mlp_w1 + mlp_b1, approximate=False) @ mlp_w2 + mlp_b2
        return x_in + h
    x = _L0_cond_ref(x, cond_1024, L0_cond_Wm, L0_cond_bm, L0_cond_Lam_re, L0_cond_Lam_im, L0_cond_B_re, L0_cond_B_im, L0_cond_C_re, L0_cond_C_im, L0_cond_D_diag, L0_cond_log_step, L0_cond_Wc, L0_cond_bc, L0_cond_W1, L0_cond_b1, L0_cond_W2, L0_cond_b2)
    x = _L1_cond_ref(x, cond_1024, mask_BxSxSx11_ik0, L1_cond_W_self, L1_cond_b_self, L1_cond_w_bias, L1_cond_b_bias, L1_cond_Wq, L1_cond_bq, L1_cond_Wk, L1_cond_bk, L1_cond_Wout, L1_cond_bout)
    x = _L2_cond_ref(x, cond_1024, L2_cond_ada_w, L2_cond_ada_b, L2_cond_ssm_w1, L2_cond_ssm_b1, L2_cond_ssm_w2, L2_cond_ssm_b2, L2_cond_ff_w1, L2_cond_ff_b1, L2_cond_ff_w2, L2_cond_ff_b2)
    x = _L3_cond_ref(x, cond_1024, L3_cond_norm1_w, L3_cond_film1_w, L3_cond_film1_b, L3_cond_q_w, L3_cond_q_b, L3_cond_k_w, L3_cond_k_b, L3_cond_v_w, L3_cond_v_b, L3_cond_proj_w, L3_cond_proj_b, L3_cond_norm2_w, L3_cond_film2_w, L3_cond_film2_b, L3_cond_mlp_w1, L3_cond_mlp_b1, L3_cond_mlp_w2, L3_cond_mlp_b2)
    return x

_drawn_inputs = setup_inputs


def setup_inputs(seed=0):
    import zlib

    import numpy as np

    out = dict(_drawn_inputs(seed))
    spreads = {'L0_cond_Lam_re': (-0.5, 0.6),
     'L0_cond_b1': (0.0, 2.0),
     'L0_cond_b2': (0.0, 0.292),
     'L1_cond_b_self': (0.0, 0.1),
     'L1_cond_bq': (0.0, 0.1),
     'L1_cond_bk': (0.0, 0.1),
     'L1_cond_bout': (0.0, 0.1),
     'L2_cond_ada_b': (0.0, 0.1),
     'L2_cond_ssm_b1': (0.0, 0.1),
     'L2_cond_ssm_b2': (0.0, 0.1),
     'L2_cond_ff_b1': (0.0, 0.1),
     'L2_cond_ff_b2': (0.0, 0.1),
     'L3_cond_norm1_w': (1.0, 0.2),
     'L3_cond_film1_b': (0.0, 0.1),
     'L3_cond_q_b': (0.0, 0.389),
     'L3_cond_k_b': (0.0, 2.0),
     'L3_cond_v_b': (0.0, 0.1),
     'L3_cond_proj_b': (0.0, 0.1),
     'L3_cond_norm2_w': (1.0, 0.2),
     'L3_cond_film2_b': (0.0, 0.1),
     'L3_cond_mlp_b1': (0.0, 0.1),
     'L3_cond_mlp_b2': (0.0, 0.1)}
    factors = {'L0_cond_bm': 3.027, 'L0_cond_Wc': 6.269, 'L0_cond_bc': 31.831, 'L0_cond_W1': 2.948}
    for name, (base, spread) in spreads.items():
        noise = np.random.default_rng([zlib.crc32(name.encode()), seed]).standard_normal(out[name].shape)
        drawn = base * np.exp(spread * noise) if base else spread * noise
        out[name] = jnp.asarray(drawn.astype(out[name].dtype))
    for name, factor in factors.items():
        out[name] = (out[name] * factor).astype(out[name].dtype)
    return out
```

```python
from contextlib import ExitStack

import numpy as np

import concourse.bass as bass
from concourse import mybir

ALU = mybir.AluOpType
ACT = mybir.ActivationFunctionType
AX = mybir.AxisListType
F32 = mybir.dt.float32
BF16 = mybir.dt.bfloat16
I32 = mybir.dt.int32

P = 128
B = 16
NTOK = 256
T = NTOK // P
D = 256
K = D // P
STATES = 64
HEADS, DH, NONGT, LABELS = 16, 16, 20, 11
HPC = 4
CH = HEADS // HPC
HPK = P // DH
NEG = -9000000000000000.0
PI = 3.1415925
HALF_PI = float(np.pi / 2)
ROUND = 1.5 * 2 ** 23
TWO_PI_HI = 6.28125
TWO_PI_MID = 1.9340515e-3
TWO_PI_LO = float(2 * np.pi - 6.28125 - np.float64(np.float32(1.9340515e-3)))

MOD0 = ["shift_a", "scale_a", "gate_a", "shift_ff", "scale_ff", "gate_ff", "scale_c", "shift_c"]
MOD2 = ["shift_msa", "scale_msa", "gate_msa", "shift_mlp", "scale_mlp", "gate_mlp"]
MOD3 = ["film1_scale", "film1_shift", "film2_scale", "film2_shift"]
MOD = {name: K * n for n, name in enumerate(MOD0 + MOD2 + MOD3)}
NMOD = K * len(MOD)
NMOD0, NMOD2, NMOD3 = K * len(MOD0), K * len(MOD2), K * len(MOD3)

COLS = {}
for _name, _n in [("mod", NMOD), ("ff0_b1", 8), ("ssm_b1", 2), ("ff2_b1", 4), ("ff3_b1", 8), ("b_self", 2),
                  ("bq", 4), ("bk", 4), ("q_b", 2), ("k_b", 2), ("norm1_w", 2), ("norm2_w", 2), ("D_diag", 2),
                  ("Lam_re", 1), ("Lam_im", 1), ("log_step", 1), ("v_b", 2)]:
    COLS[_name] = sum(n for _, n in COLS.values()), _n
NCOLS = sum(n for _, n in COLS.values())
ROWS = {}
for _name, _n in [("bout0", D), ("bout1", D), ("proj_b", D), ("mlp_b2", D), ("w_bias", LABELS), ("b_bias", 1)]:
    ROWS[_name] = sum(n for _, n in ROWS.values()), _n
NROWS = sum(n for _, n in ROWS.values())
BIASED = ["ff0", "ssm", "ff2"]
GATES = ["s5", "ff0", "ssm", "ff2"]

MLPS = {
    "ff0": (1024, ACT.Gelu_apprx_tanh, "layer", 1e-5),
    "ssm": (256, ACT.Gelu, "layer", 1e-6),
    "ff2": (512, ACT.Gelu_apprx_tanh, "layer", 1e-6),
    "ff3": (1024, ACT.Gelu, "rms", 1e-6),
}
NORMS = {"s5": ("layer", 1e-5), "att": ("rms", 1e-6), **{n: v[2:] for n, v in MLPS.items()}}
ORDER = ["s5", "ff0", "gat", "ssm", "ff2", "att", "ff3"]
NORMED = [n for n in ORDER if n in NORMS]

FIRST, TURNS = 3, 5
LAST = FIRST + 2 * TURNS


def build_program(nc, A, out):
    with ExitStack() as ctx:
        def sb(name, shape, dt=F32):
            return ctx.enter_context(nc.sbuf_tensor(name, shape, dt))

        def sem(name):
            return ctx.enter_context(nc.semaphore(name))

        PS = [ctx.enter_context(nc.psum_tensor(f"bank{i}", [P, 512], F32)) for i in range(8)]

        X = sb("X", [P, B * T, D])
        cond = sb("cond", [P, K, B])
        cond_silu = sb("cond_silu", [P, K, B])
        sig = sb("sig", [P, K, B])
        cols = sb("cols", [P, NCOLS])
        rows = sb("rows", [P, NROWS])
        mod = sb("mod", [P, NMOD, B])
        MS = sb("MS", [P, len(NORMED), K, B])
        MH = sb("MH", [P, len(NORMED), K, B])
        one_ff = sb("one_ff", [P, K, B])
        ident = sb("ident", [P, P])
        ident_b = sb("ident_b", [P, P], BF16)
        half_neg = sb("half_neg", [P, T])
        arena = sb("arena", [P, K * NMOD * P])
        wmod0 = arena[:, 0:K * NMOD0 * P].rearrange("p (k n) -> p k n", k=K)
        wmod23 = arena[:, K * NMOD0 * P:].rearrange("p (k n) -> p k n", k=K)

        s5_inT = sb("s5_inT", [P, 2, K, P])
        s5_out = sb("s5_out", [P, 2, D])
        s5_diag = sb("s5_diag", [P, K, P])
        cosT = sb("cosT", [P, NTOK])
        sinT = sb("sinT", [P, NTOK])
        decay = sb("decay", [P, NTOK])
        rot = sb("rot", [P, 2, P])
        sc = sb("sc", [P, 40])
        sign = sb("sign", [P, 1])

        W1 = {n: sb(f"{n}_w1", [P, K, MLPS[n][0]]) for n in MLPS}
        W2 = {n: sb(f"{n}_w2", [P, MLPS[n][0] // P, D]) for n in MLPS}
        w_gat = sb("w_gat", [P, K, 7 * D])
        w_qpart = sb("w_qpart", [P, K, D])
        qpart = sb("qpart", [P, K, B])
        w_att = sb("w_att", [P, K, 4 * D])
        w_vp = sb("w_vp", [P, K, D])
        att_row = sb("att_row", [P, D])
        bout = sb("bout", [P, D])

        stats = sb("stats", [P, 2, T, 6])
        mv = sb("mv", [P, 2, 6, T])
        msq = sb("msq", [P, 2, T])
        var_eps = sb("var_eps", [P, 2, T])
        rstd = sb("rstd", [P, 2, T])
        xn = sb("xn", [P, 2, T, D])
        hT = sb("hT", [P, 2, K, NTOK])
        gT = sb("gT", [P, 2, 8, NTOK])
        upd = sb("upd", [P, 2, T, D])
        gates = sb("gates", [P, 2, 2, D])
        exT = sb("exT", [P, 2, T, NTOK])

        s5_bc = upd[:, :, :, :].rearrange("p a t d -> p (a t) d")
        s5_in = exT[:, 0, :, :]
        s5_tmp = exT[:, 1, :, :]
        ff3_w1 = W1["ff3"][0:B, :, :].rearrange("b k n -> b (k n)")
        gate_bias = ff3_w1[:, 0:4 * D].rearrange("b (g d) -> b g d", d=D)
        out_bias = ff3_w1[:, 4 * D:7 * D].rearrange("b (g d) -> b g d", d=D)
        gate_rows = W2["ff3"][0:B, :, :].rearrange("b (g a) d -> b g a d", a=2)

        bu = gT[:, :, 0:2, :]
        wrot = gT[:, :, 2, :]
        zst = gT[:, :, 3, :]
        zc = gT[:, :, 4, :]
        zs = gT[:, :, 5, :]

        room = [0]

        def carve(n):
            room[0] += n
            assert room[0] <= K * NMOD * P
            return arena[:, room[0] - n:room[0]]

        adj = [carve(4 * NONGT * LABELS).bitcast(I32).rearrange("p (g l) -> p g l", l=LABELS) for _ in range(2)]
        adj_w = carve(4 * NONGT * LABELS).rearrange("p (g l) -> p g l", l=LABELS)
        cnt = carve(4 * NONGT)
        pen = carve(4 * NONGT)
        lab = carve(4 * NONGT)
        cbias = [carve(4 * NONGT).rearrange("p (d t m) -> p d t m", d=2, t=T) for _ in range(2)]
        sfA = carve(K * NTOK).rearrange("p (k n) -> p k n", k=K)
        sfT = [exT[:, i, :, :] for i in range(2)]
        kvrep = carve(K * HPC * NONGT).rearrange("p (k h m) -> p k h m", k=K, h=HPC)
        KB = [carve(4 * HPK * NONGT).rearrange("p (g h m) -> p g h m", g=4, h=HPK) for _ in range(2)]
        VB = [carve(2 * D)[0:HPC * NONGT, :].rearrange("p (d n) -> p d n", d=2) for _ in range(2)]
        sco = [carve(2 * HEADS * NONGT).rearrange("p (g m) -> p g m", m=NONGT) for _ in range(T)]
        prb = [carve(2 * HEADS * NONGT).rearrange("p (g m) -> p g m", m=NONGT) for _ in range(T)]
        smax = [carve(2 * HEADS) for _ in range(T)]
        ssum = [carve(2 * HEADS) for _ in range(T)]
        srec = [carve(2 * HEADS) for _ in range(T)]
        rsum = carve(2 * T).rearrange("p (a t) -> p a t", a=2)
        QT = [gT[:, i, 0:4, :].rearrange("p (d k) n -> p d k n", d=2) for i in range(2)]
        wT = gT[:, :, 4:8, :].rearrange("p a (c2 c) n -> p a c2 (c n)", c2=2)
        nz = sb("nz", [P, 2, T], BF16)
        head_mask = sb("head_mask", [P, HPK, NONGT])
        v_mask = sb("v_mask", [HPC * NONGT, HPC, DH])

        qT = gT[:, :, 0:2, :]
        kT = gT[:, :, 2:4, :]
        vp = gT[:, :, 4:6, :]
        ex = gT[:, :, 6:8, :]
        amax = sb("amax", [P, 2, T])
        nmax = sb("nmax", [P, 2, T])
        asum = sb("asum", [P, 2, T])
        arec = sb("arec", [P, 2, T])

        gate_dram = nc.dram_tensor("gate_dram", (B, len(GATES) * 2 * D), F32, kind="Internal").ap()

        def col(name, n=0):
            return cols[:, COLS[name][0] + n:COLS[name][0] + n + 1]

        def row(name):
            return rows[:, ROWS[name][0]:ROWS[name][0] + ROWS[name][1]]

        L = {n: sem(f"loaded_{n}") for n in ("small", "x0", "x", "wmod0", "s5", "wmod23", "w_gat", "w_att")}
        LW = {n: sem(f"loaded_{n}") for n in MLPS}
        consts_done = sem("consts_done")
        const_step = sem("const_step")
        setup_step = sem("setup_step")
        act_setup = sem("act_setup")
        silu_ready = sem("silu_ready")
        mod0_psum = sem("mod0_psum")
        mod0_ready = sem("mod0_ready")
        s5_in_ready = sem("s5_in_ready")
        s5_inT_psum = sem("s5_inT_psum")
        s5_ready = sem("s5_ready")
        mod23_psum = sem("mod23_psum")
        gates0_ready = sem("gates0_ready")
        gates2_ready = sem("gates2_ready")
        gates_stored = sem("gates_stored")
        gates2_stored = sem("gates2_stored")
        stored = sem("stored")

        S = {}
        for n in ORDER:
            names = ["xT_psum", "hT_ready", "out_psum", "out_read"]
            if n != "att":
                names += ["x_ready"]
            if n in NORMS and NORMS[n][0] == "rms":
                names += ["msq_done"]
            if n in MLPS:
                names += ["hid_psum", "hid_ready"]
            if n in BIASED:
                names += ["upd_ready"]
            S[n] = {k: sem(f"{n}_{k}") for k in names}
        gate_loaded = [sem(f"gate_loaded_{i}") for i in range(2)]
        adj_loaded = [sem(f"adj_loaded_{i}") for i in range(2)]
        stats_done, aggr_done, var_ready, rstd_ready, xn_ready = (
            sem(k) for k in ("stats_done", "aggr_done", "var_ready", "rstd_ready", "xn_ready"))
        for n in ("s5", "ff3"):
            S[n]["upd_ready"] = S[n]["out_read"]
        S["att"]["x_ready"] = S["att"]["out_read"]
        s5 = {k: sem(f"s5_{k}") for k in
                                ("bu_psum", "bu_ready", "rot_ready", "scan_ready", "zs_ready", "zc_ready")}
        ga = {k: sem(f"gat_{k}") for k in
                                ("adj_used", "adj_w", "lab", "cnt", "pen", "cb", "xs_ready", "nz_ready", "nz_psum",
                                 "sf_psum", "sfA_ready", "sfT_ready", "kvrep_ready", "q_psum", "q_ready", "k_psum",
                                 "KB_ready", "v_psum", "VB_ready", "s_psum", "s_biased", "smax_done", "s_shifted",
                                 "exp_done", "ssum_done", "srec_done", "w_ready", "wT_psum", "wT_ready", "bias_done")}
        at = {k: sem(f"att_{k}") for k in
                                ("q_psum", "q_ready", "k_psum", "k_ready", "v_psum", "v_ready", "s_psum", "amax_done",
                                 "nmax_done", "exp_done", "arec_done", "exT_psum", "exT_ready", "row_added")}
        ws_psum = sem("ws_psum")
        ws_ready = sem("ws_ready")
        block = ctx.enter_context(nc.Block())

        def prev(n):
            return S[ORDER[ORDER.index(n) - 1]]

        def wait_x(eng, n, b):
            if n == "s5":
                if isinstance(b, int) and b < 2:
                    eng.wait_ge(L["x0"], 16)
                else:
                    eng.wait_ge(L["x"], 16 * (B // 2 - 1))
            else:
                eng.wait_ge(prev(n)["x_ready"], b + 1)

        def steps(eng, one):
            for b in range(FIRST):
                one(b, b % 2)
            with eng.Fori(0, TURNS) as i:
                for j in range(2):
                    one(i * 2 + (FIRST + j), (FIRST + j) % 2)
            for b in range(LAST, B):
                one(b, b % 2)

        def hid_bank(banks, par, j):
            return j if banks == 4 else banks * par + j

        def loads(b, par):
            return (b - par) * 8 + 16

        def nth(n, b):
            return b + B * NORMED.index(n)

        def after(b, lag):
            return not isinstance(b, int) or b >= lag

        def before_end(b, ahead):
            return not isinstance(b, int) or b + ahead < B

        @block.sync
        def _(sp):
            def load(dst, src, s):
                sp.dma_start(dst, src).then_inc(s, 16)

            load(cols[:, :], A["cols"], L["small"])
            load(cond[:, :, :], A["cond"], L["small"])
            load(rows[:, :], A["rows"].partition_broadcast(P), L["small"])
            load(ff3_w1[:, 0:4 * D], A["gate_bias"].partition_broadcast(B), L["small"])
            load(ff3_w1[:, 4 * D:7 * D], A["out_bias"].partition_broadcast(B), L["small"])
            load(s5_bc[:, :, :], A["s5_bc"], L["s5"])
            xv = A["x"].rearrange("b (t p) d -> p (b t) d", p=P)
            load(X[:, 0:4, :], xv[:, 0:4, :], L["x0"])
            load(wmod0, A["wmod0"], L["wmod0"])
            for c in range(1, B // 2):
                load(X[:, 4 * c:4 * c + 4, :], xv[:, 4 * c:4 * c + 4, :], L["x"])
            load(wmod23, A["wmod23"], L["wmod23"])
            load(w_gat[:, :, :], A["w_gat"], L["w_gat"])
            load(w_qpart[:, :, :], A["w_qpart"], L["w_gat"])
            load(w_att[:, :, :], A["w_att"], L["w_att"])
            load(W1["ff0"][:, :, :], A["ff0_w1"], LW["ff0"])
            load(W2["ff0"][:, :, :], A["ff0_w2"], LW["ff0"])
            for n in ("ssm", "ff2"):
                load(W1[n][:, :, :], A[f"{n}_w1"], LW[n])
                load(W2[n][:, :, :], A[f"{n}_w2"], LW[n])

            def load_gate(n, g):
                def one(b, par):
                    if after(b, 2):
                        sp.wait_ge(S[n]["x_ready"], b - 1)
                    src = gate_dram[bass.ds(b, 1), 2 * D * g:2 * D * (g + 1)]
                    sp.dma_start(gates[:, par, :, :].rearrange("p a d -> p (a d)"),
                                 src.broadcast_to([P, 2 * D])).then_inc(gate_loaded[par], 16)
                steps(sp, one)

            sp.wait_ge(gates0_ready, 1)
            sp.dma_start(gate_dram[:, 0:4 * D], gate_rows[:, 0:2, :, :].rearrange("b g a d -> b (g a d)"))\
              .then_inc(gates_stored, 16)
            sp.wait_ge(gates_stored, 16)
            load_gate("s5", 0)
            sp.wait_ge(gates2_ready, 1)
            sp.dma_start(gate_dram[:, 4 * D:8 * D], gate_rows[:, 2:4, :, :].rearrange("b g a d -> b (g a d)"))\
              .then_inc(gates2_stored, 16)
            def load_adj(b, par):
                if after(b, 2):
                    sp.wait_ge(ga["adj_used"], b - 1)
                src = A["adj"][b] if isinstance(b, int) else A["adj"][bass.ds(b, 1)].rearrange("o p n -> (o p) n")
                sp.dma_start(adj[par].rearrange("p g l -> p (g l)"), src).then_inc(adj_loaded[par], 16)

            sp.wait_ge(mod23_psum, 2)
            load_adj(0, 0)
            load_adj(1, 1)
            sp.wait_ge(S["s5"]["x_ready"], B)
            load_gate("ff0", 1)

            steps(sp, lambda b, par: load_adj(b, par) if after(b, 2) else None)
            sp.wait_ge(gates2_stored, 16)
            load(W1["ff3"][:, :, :], A["ff3_w1"], LW["ff3"])
            load(W2["ff3"][:, :, :], A["ff3_w2"], LW["ff3"])
            sp.wait_ge(S["ff0"]["x_ready"], B)
            load_gate("ssm", 2)
            sp.wait_ge(S["ssm"]["x_ready"], B)
            load_gate("ff2", 3)

            ov = out.rearrange("b (t p) d -> p (b t) d", p=P)

            def store(b, par):
                sp.wait_ge(S["ff3"]["x_ready"], b + 1)
                if isinstance(b, int):
                    sp.dma_start(ov[:, 2 * b:2 * b + 2, :], X[:, 2 * b:2 * b + 2, :]).then_inc(stored, 16)
                else:
                    sp.dma_start(ov[:, bass.ds(b * 2, 2), :], X[:, bass.ds(b * 2, 2), :]).then_inc(stored, 16)

            steps(sp, store)
            sp.wait_ge(stored, 16 * B)

        @block.gpsimd
        def _(pool):
            pool.memset(ident[:, :], 0.0).then_inc(const_step, 1)
            pool.memset(ident_b[:, :], 0.0).then_inc(const_step, 1)
            pool.memset(half_neg[:, :], -0.5).then_inc(const_step, 1)
            pool.memset(head_mask[:, :, :], DH ** -0.5).then_inc(const_step, 1)
            pool.memset(v_mask[:, :, :], 1.0).then_inc(const_step, 1)
            pool.wait_ge(const_step, 5)
            for m in (ident, ident_b):
                pool.affine_select(out=m[:, :], in_=m[:, :], compare_op=ALU.not_equal, fill=1.0, base=0,
                                   pattern=[[-1, P]], channel_multiplier=1).then_inc(const_step, 1)
            pool.affine_select(out=head_mask[:, :, :], in_=head_mask[:, :, :], compare_op=ALU.is_ge, fill=0.0, base=0,
                               pattern=[[-DH, HPK], [0, NONGT]], channel_multiplier=1).then_inc(const_step, 1)
            pool.affine_select(out=v_mask[:, :, :], in_=v_mask[:, :, :], compare_op=ALU.is_ge, fill=0.0, base=0,
                               pattern=[[-NONGT, HPC], [0, DH]], channel_multiplier=1).then_inc(const_step, 1)
            pool.wait_ge(const_step, 9)
            pool.affine_select(out=head_mask[:, :, :], in_=head_mask[:, :, :], compare_op=ALU.is_ge, fill=0.0,
                               base=DH - 1, pattern=[[DH, HPK], [0, NONGT]], channel_multiplier=-1)\
                .then_inc(consts_done, 1)
            pool.affine_select(out=v_mask[:, :, :], in_=v_mask[:, :, :], compare_op=ALU.is_ge, fill=0.0,
                               base=NONGT - 1, pattern=[[NONGT, HPC], [0, DH]], channel_multiplier=-1)\
                .then_inc(consts_done, 1)

            def inv_std(n, b, par):
                s = S[n]
                pool.wait_ge(var_ready, nth(n, b) + 1)
                pool.tensor_tensor(rstd[:, par, :], var_eps[:, par, :], half_neg[:, :], ALU.pow)\
                    .then_inc(rstd_ready, 1)

            def add_bias(n, b, par):
                pool.wait_ge(S[n]["out_read"], b + 1)
                pool.tensor_tensor(upd[:, par, :, :], upd[:, par, :, :],
                                   gates[:, par, 1:2, :].broadcast_to([P, T, D]), ALU.add).then_inc(S[n]["upd_ready"], 1)

            def s5_step(b, par):
                pool.wait_ge(s5["bu_ready"], 2 * (b + 1))
                pool.tensor_tensor(wrot[:, par, :], bu[:, par, 0, :], bu[:, par, 1, :], ALU.add)\
                    .then_inc(s5["rot_ready"], 1)
                pool.wait_ge(s5["scan_ready"], b + 1)
                if after(b, 2):
                    pool.wait_ge(S["s5"]["out_psum"], b - 1)
                pool.tensor_tensor(zc[:, par, :], zst[:, par, :], cosT[:, :], ALU.mult).then_inc(s5["zc_ready"], 1)

            def begin(n):
                if n in NORMS:
                    inv_std(n, 0, 0)
                    inv_std(n, 1, 1)

            def phase(n, follow):
                def one(b, par):
                    if n in NORMS and before_end(b, 2):
                        inv_std(n, b + 2, par)
                    if n == "s5":
                        s5_step(b, par)
                    if n in BIASED and after(b, 1):
                        add_bias(n, b - 1, 1 - par)
                    if n == "gat":
                        gat_step(b, par)
                steps(pool, one)
                if follow:
                    begin(follow)
                if n in BIASED:
                    add_bias(n, B - 1, (B - 1) % 2)

            def gat_shift(b, t):
                pool.wait_ge(ga["smax_done"], T * b + (t + 1))
                pool.tensor_tensor(sco[t], sco[t], smax[t].unsqueeze(2).broadcast_to([P, 2 * HEADS, NONGT]),
                                   ALU.subtract).then_inc(ga["s_shifted"], 1)

            def gat_weights(b, t):
                pool.wait_ge(ga["srec_done"], T * b + (t + 1))
                pool.tensor_tensor(prb[t], prb[t], srec[t].unsqueeze(2).broadcast_to([P, 2 * HEADS, NONGT]),
                                   ALU.mult).then_inc(ga["w_ready"], 1)

            def gat_step(b, par):
                gat_shift(b, 0)
                gat_shift(b, 1)
                gat_weights(b, 0)
                gat_weights(b, 1)

            begin("s5")
            for n, follow in zip(ORDER, ORDER[1:] + [None]):
                phase(n, follow)

        @block.scalar
        def _(act):
            act.wait_ge(L["small"], 16 * 5)
            act.activation(sc[:, 0:1], col("log_step"), ACT.Exp).then_inc(act_setup, 1)
            act.wait_ge(setup_step, 1)
            act.activation(sc[:, 2:3], sc[:, 1:2], ACT.Exp).then_inc(act_setup, 1)
            act.activation(sig[:, :, :], cond[:, :, :], ACT.Exp, scale=-1.0).then_inc(silu_ready, 1)
            act.wait_ge(setup_step, 10)
            act.activation(sc[:, 9:10], sc[:, 7:8], ACT.Sin).then_inc(act_setup, 1)
            act.activation(sc[:, 10:11], sc[:, 8:9], ACT.Sin).then_inc(act_setup, 1)

            def modulate(n, b, par):
                s, j = S[n], NORMED.index(n)
                act.wait_ge(s["xT_psum"], b + 1)
                if after(b, 2):
                    act.wait_ge(s5["bu_psum"], b - 1)
                for k in range(K):
                    act.activation(hT[:, par, k, :], PS[par][:, k * NTOK:(k + 1) * NTOK], ACT.Identity,
                                   bias=MH[:, j, k, bass.ds(b, 1)], scale=MS[:, j, k, bass.ds(b, 1)])\
                        .then_inc(s["hT_ready"], 1)

            def hidden(n, b, par):
                s, (H, fn, _, _) = S[n], MLPS[n]
                banks = H // P // 2
                if after(b, 2):
                    act.wait_ge(s["out_psum"], b - 1)
                for j in range(banks):
                    act.wait_ge(s["hid_psum"], b * banks + (j + 1))
                    bank = PS[2 + hid_bank(banks, par, j)]
                    for i in range(2):
                        m = 2 * j + i
                        act.activation(gT[:, par, m, :], bank[:, i * NTOK:(i + 1) * NTOK], fn,
                                       bias=col(f"{n}_b1", m)).then_inc(s["hid_ready"], 1)

            def gat_copy(b, par):
                wait_x(act, "gat", b)
                if not after(b, 2):
                    act.wait_ge(prev("gat")["xT_psum"], B)
                if after(b, 2):
                    act.wait_ge(S["gat"]["xT_psum"], b - 1)
                    act.wait_ge(ga["nz_ready"], b - 1)
                for t in range(T):
                    act.activation(xn[:, par, t, :], X[:, bass.ds(b * 2 + t, 1), :].rearrange("p o d -> p (o d)"),
                                   ACT.Copy, accum_out=rsum[:, par, t:t + 1]).then_inc(ga["xs_ready"], 1)

            def gat_xT(b, par):
                act.wait_ge(S["gat"]["xT_psum"], b + 1)
                if after(b, 2):
                    act.wait_ge(ga["sf_psum"], b - 1)
                act.activation(hT[:, par, :, :].rearrange("p k n -> p (k n)"), PS[0][:, :], ACT.Copy)\
                    .then_inc(S["gat"]["hT_ready"], 1)

            def gat_self(b, par):
                act.wait_ge(ga["sf_psum"], b + 1)
                if after(b, 1):
                    act.wait_ge(ga["sfT_ready"], K * b)
                for k in range(K):
                    act.activation(sfA[:, k, :], PS[2][:, k * NTOK:(k + 1) * NTOK], ACT.Identity,
                                   bias=col("b_self", k)).then_inc(ga["sfA_ready"], 1)

            def gat_q(b, par):
                if after(b, 2):
                    act.wait_ge(ga["s_psum"], T * (b - 1))
                for d in range(2):
                    act.wait_ge(ga["q_psum"], 2 * b + (d + 1))
                    for k in range(K):
                        act.activation(QT[par][:, d, k, :], PS[3 - d][:, k * NTOK:(k + 1) * NTOK], ACT.Identity,
                                       bias=col("bq", 2 * d + k)).then_inc(ga["q_ready"], 1)

            def gat_exp(b, par, t):
                act.wait_ge(ga["s_shifted"], T * b + (t + 1))
                if after(b, 1):
                    act.wait_ge(ga["wT_psum"], 4 * b)
                act.activation(prb[t], sco[t], ACT.Exp).then_inc(ga["exp_done"], 1)

            def gat_wT(b, par, t):
                if after(b, 1) and t == 0:
                    act.wait_ge(S["gat"]["out_psum"], b)
                for d in range(2):
                    act.wait_ge(ga["wT_psum"], 4 * b + (2 * t + d + 1))
                    act.activation(wT[0:HPC * NONGT, t, d, :], PS[7 - 7 * d][0:HPC * NONGT, :], ACT.Copy)\
                        .then_inc(ga["wT_ready"], 1)

            def att_qk(b, par):
                for m, (ready, psum, dst, bank, bias) in enumerate(
                        ((at["q_ready"], at["q_psum"], qT, PS[2], "q_b"), (at["k_ready"], at["k_psum"], kT, PS[3], "k_b"))):
                    act.wait_ge(psum, b + 1)
                    if after(b, 2) and m == 0:
                        act.wait_ge(at["s_psum"], b - 1)
                    for k in range(K):
                        act.activation(dst[:, par, k, :], bank[:, k * NTOK:(k + 1) * NTOK], ACT.Identity,
                                       bias=col(bias, k)).then_inc(ready, 1)

            def att_exp(b, par):
                act.wait_ge(at["nmax_done"], b + 1)
                if after(b, 2):
                    act.wait_ge(at["exT_psum"], b - 1)
                    act.wait_ge(at["arec_done"], b - 1)
                for t in range(T):
                    act.activation(ex[:, par, t, :], PS[4][:, t * NTOK:(t + 1) * NTOK], ACT.Exp,
                                   bias=nmax[:, par, t:t + 1], scale=D ** -0.5, accum_out=asum[:, par, t:t + 1])\
                        .then_inc(at["exp_done"], 1)

            def begin(n):
                if n == "s5":
                    act.wait_ge(mod0_ready, 1)
                    modulate(n, 0, 0)
                if n == "gat":
                    act.wait_ge(mod23_psum, 2)
                    gat_copy(0, 0)
                    gat_copy(1, 1)
                    gat_xT(0, 0)

            def phase(n, follow):
                if n == "gat":
                    gat_xT(1, 1)
                    gat_copy(2, 0)
                    gat_self(0, 0)
                    gat_q(0, 0)
                if n == "att":
                    att_qk(0, 0)

                def one(b, par):
                    if n == "s5" and before_end(b, 1):
                        modulate(n, b + 1, 1 - par)
                    if n in MLPS:
                        hidden(n, b, par)
                    if n == "gat":
                        if before_end(b, 1):
                            gat_self(b + 1, 1 - par)
                        if before_end(b, 2):
                            gat_xT(b + 2, par)
                        gat_exp(b, par, 0)
                        gat_exp(b, par, 1)
                        if before_end(b, 1):
                            gat_q(b + 1, 1 - par)
                        if before_end(b, 3):
                            gat_copy(b + 3, 1 - par)
                        gat_wT(b, par, 0)
                        gat_wT(b, par, 1)
                    if n == "att":
                        att_exp(b, par)
                        if before_end(b, 1):
                            att_qk(b + 1, 1 - par)
                steps(act, one)
                if follow:
                    begin(follow)

            begin("s5")
            for n, follow in zip(ORDER, ORDER[1:] + [None]):
                phase(n, follow)

        @block.tensor
        def _(pe):
            def group(dst, pairs, inc=None):
                for i, (l, r) in enumerate(pairs):
                    mm = pe.matmul(dst, l, r, start=(i == 0), stop=(i == len(pairs) - 1))
                if inc is not None:
                    mm.then_inc(inc, 1)

            pe.wait_ge(s5_in_ready, 2)
            pe.wait_ge(consts_done, 2)
            for i in range(2):
                for k in range(K):
                    tr = pe.transpose(PS[4][:, (2 * i + k) * P:(2 * i + k + 1) * P], s5_in[:, i, k * P:(k + 1) * P],
                                      ident[:, :])
            tr.then_inc(s5_inT_psum, 1)

            pe.wait_ge(L["small"], 16 * 5)
            pe.wait_ge(L["wmod0"], 16)
            for j in range(NMOD0):
                group(PS[2][:, j * B:(j + 1) * B],
                      [(wmod0[:, k, j * P:(j + 1) * P], cond[:, k, :]) for k in range(K)])
            for g, name in enumerate(("gate_a", "gate_ff")):
                a = MOD[name] * P
                group(PS[3][0:B, g * D:(g + 1) * D], [(cond[:, k, :], wmod0[:, k, a:a + D]) for k in range(K)],
                      mod0_psum if g else None)
            def transposes(n, b, par):
                s = S[n]
                if n == "gat":
                    pe.wait_ge(ga["xs_ready"], T * (b + 1))
                    bank = PS[0]
                    if after(b, 1):
                        pe.wait_ge(s["hT_ready"], b)
                    if after(b, 3):
                        pe.wait_ge(ga["wT_ready"], 4 * (b - 2))
                else:
                    pe.wait_ge(xn_ready, T * (nth(n, b) + 1))
                    bank = PS[par]
                    if n == "att" and after(b, 2):
                        pe.wait_ge(at["exT_ready"], b - 1)
                    if prev(n) is S["gat"] and not after(b, 1):
                        pe.wait_ge(ga["wT_ready"], 4 * B)
                for k in range(K):
                    for t in range(T):
                        tr = pe.transpose(bank[:, k * NTOK + t * P:k * NTOK + (t + 1) * P],
                                          xn[:, par, t, k * P:(k + 1) * P], ident[:, :])
                tr.then_inc(s["xT_psum"], 1)

            def gat_zero_rows(b, par):
                pe.wait_ge(ga["nz_ready"], b + 1)
                if after(b, 1):
                    pe.wait_ge(ga["KB_ready"], 4 * b)
                for t in range(T):
                    mm = pe.matmul(PS[1][:, t * P:(t + 1) * P], nz[:, par, t:t + 1].broadcast_to([P, P]),
                                   ident_b[:, :], start=True, stop=True)
                mm.then_inc(ga["nz_psum"], 1)

            def out_bank(n, b, par):
                if after(b, 2):
                    pe.wait_ge(S[n]["out_read"], b - 1)
                elif n != "s5":
                    pe.wait_ge(prev(n)["out_read"], B)
                return PS[6 + par]

            def s5_in_mm(b, par):
                s = S["s5"]
                pe.wait_ge(s["hT_ready"], K * (b + 1))
                if after(b, 2):
                    pe.wait_ge(s5["bu_ready"], 2 * (b - 1))
                bank = out_bank("s5", b, par)
                for t in range(T):
                    for k in range(K):
                        pe.matmul(bank[:, t * D + k * P:t * D + (k + 1) * P], hT[:, par, k, t * P:(t + 1) * P],
                                  s5_diag[:, k, :], start=(t == 0 and k == 0), stop=False, skip_group_check=True)
                for i in range(2):
                    group(PS[2 + par][:, i * NTOK:(i + 1) * NTOK],
                          [(s5_inT[:, i, k, :], hT[:, par, k, :]) for k in range(K)], s5["bu_psum"] if i else None)

            def s5_out_mm(b, par):
                bank = PS[6 + par]
                pe.wait_ge(s5["zc_ready"], b + 1)
                pe.wait_ge(s5["zs_ready"], b + 1)
                for t in range(T):
                    tok = slice(t * P, (t + 1) * P)
                    pe.matmul(bank[:, t * D:(t + 1) * D], zc[:, par, tok], s5_out[:, 0, :], start=False, stop=False,
                              skip_group_check=True)
                    mm = pe.matmul(bank[:, t * D:(t + 1) * D], zs[:, par, tok], s5_out[:, 1, :], start=False,
                                   stop=True, skip_group_check=True)
                mm.then_inc(S["s5"]["out_psum"], 1)

            def up(n, b, par):
                s, H = S[n], MLPS[n][0]
                banks = H // P // 2
                pe.wait_ge(s["hT_ready"], K * (b + 1))
                for j in range(banks):
                    if banks == 4 and after(b, 1):
                        pe.wait_ge(s["hid_ready"], (b - 1) * 2 * banks + 2 * (j + 1))
                    if banks < 4 and after(b, 2) and j == 0:
                        pe.wait_ge(s["hid_ready"], (b - 1) * 2 * banks)
                    for i in range(2):
                        m = 2 * j + i
                        group(PS[2 + hid_bank(banks, par, j)][:, i * NTOK:(i + 1) * NTOK],
                              [(W1[n][:, k, m * P:(m + 1) * P], hT[:, par, k, :]) for k in range(K)],
                              s["hid_psum"] if i else None)

            def down(n, b, par):
                s, H = S[n], MLPS[n][0]
                M = H // P
                bank = out_bank(n, b, par)
                pe.wait_ge(s["hid_ready"], M * (b + 1))
                for t in range(T):
                    group(bank[:, t * D:(t + 1) * D],
                          [(gT[:, par, m, t * P:(t + 1) * P], W2[n][:, m, :]) for m in range(M)],
                          s["out_psum"] if t == T - 1 else None)

            WG = {name: slice(i * D, (i + 1) * D) for i, name in enumerate(("self", "q0", "q1", "k0", "k1"))}

            def gat_self(b, par):
                pe.wait_ge(S["gat"]["hT_ready"], b + 1)
                if after(b, 1):
                    pe.wait_ge(ga["q_ready"], 4 * b)
                for m in range(K):
                    group(PS[2][:, m * NTOK:(m + 1) * NTOK],
                          [(w_gat[:, k, m * P:(m + 1) * P], hT[:, par, k, :]) for k in range(K)],
                          ga["sf_psum"] if m == K - 1 else None)

            def gat_q(b, par, d):
                pe.wait_ge(ga["sfT_ready"], K * (b + 1))
                if d == 0 and after(b, 1):
                    pe.wait_ge(ga["VB_ready"], b)
                for m in range(K):
                    a = (1 + d) * D + m * P
                    group(PS[3 - d][:, m * NTOK:(m + 1) * NTOK],
                          [(w_gat[:, k, a:a + P], sfT[par][:, k, :]) for k in range(K)],
                          ga["q_psum"] if m == K - 1 else None)

            def gat_k(b, par):
                for d in range(2):
                    for m in range(K):
                        g = 2 * d + m
                        a = (3 + d) * D + m * P
                        group(PS[1][:, 256 + g * NONGT:256 + (g + 1) * NONGT],
                              [(w_gat[:, k, a:a + P], sfT[par][:, k, 0:NONGT]) for k in range(K)],
                              ga["k_psum"] if g == 3 else None)

            def gat_v(b, par):
                pe.wait_ge(ga["kvrep_ready"], b + 1)
                pe.wait_ge(ga["q_ready"], 4 * b + 2)
                group(PS[3][0:HPC * NONGT, :],
                      [(kvrep[:, k, :, :].rearrange("p h m -> p (h m)"), w_gat[:, k, 5 * D:7 * D]) for k in range(K)],
                      ga["v_psum"])

            def gat_scores(b, par, t):
                if t == 0:
                    pe.wait_ge(ga["KB_ready"], 4 * (b + 1))
                    pe.wait_ge(ga["q_ready"], 4 * (b + 1))
                    if after(b, 1):
                        pe.wait_ge(ga["s_biased"], T * b)
                else:
                    pe.wait_ge(ga["s_biased"], T * b + t)
                for d in range(2):
                    for k in range(K):
                        mm = pe.matmul(PS[4 + d][:, k * HPK * NONGT:(k + 1) * HPK * NONGT],
                                       QT[par][:, d, k, t * P:(t + 1) * P],
                                       KB[par][:, 2 * d + k, :, :].rearrange("p h m -> p (h m)"),
                                       start=True, stop=True)
                mm.then_inc(ga["s_psum"], 1)

            def gat_wT(b, par, t):
                pe.wait_ge(ga["w_ready"], T * b + (t + 1))
                for d in range(2):
                    bank = PS[7 - 7 * d]
                    if t:
                        pe.wait_ge(ga["wT_ready"], 4 * b + (2 * t + d - 1))
                    elif not d:
                        if after(b, 1):
                            pe.wait_ge(ga["wT_ready"], 4 * b)
                        else:
                            pe.wait_ge(prev("gat")["out_read"], B)
                    elif before_end(b, 2):
                        pe.wait_ge(S["gat"]["hT_ready"], b + 3)
                    for c in range(CH):
                        h0 = (d * HEADS + c * HPC)
                        tr = pe.transpose(bank[0:HPC * NONGT, c * P:(c + 1) * P],
                                          prb[t][:, h0:h0 + HPC, :].rearrange("p h m -> p (h m)"), ident[:, :])
                    tr.then_inc(ga["wT_psum"], 1)

            def gat_out(b, par):
                if after(b, 1):
                    pe.wait_ge(S["gat"]["out_read"], b)
                else:
                    pe.wait_ge(prev("gat")["out_read"], B)
                pe.wait_ge(ga["VB_ready"], b + 1)
                for t in range(T):
                    pe.wait_ge(ga["wT_ready"], 4 * b + (2 * t + 2))
                    for k in range(K):
                        pe.matmul(PS[6][:, t * D + k * P:t * D + (k + 1) * P], sfT[par][:, k, t * P:(t + 1) * P],
                                  ident[:, :], start=(k == 0), stop=False, skip_group_check=True)
                    for d in range(2):
                        for c in range(CH):
                            mm = pe.matmul(PS[6][:, t * D + c * HPC * DH:t * D + (c + 1) * HPC * DH],
                                           wT[0:HPC * NONGT, t, d, c * P:(c + 1) * P],
                                           VB[par][:, d, c * HPC * DH:(c + 1) * HPC * DH],
                                           start=False, stop=(d == 1), skip_group_check=True)
                mm.then_inc(S["gat"]["out_psum"], 1)

            def att_qk(b, par):
                pe.wait_ge(S["att"]["hT_ready"], K * (b + 1))
                for i, (psum, ready, bank) in enumerate(((at["q_psum"], at["q_ready"], PS[2]), (at["k_psum"], at["k_ready"], PS[3]))):
                    if after(b, 1):
                        pe.wait_ge(ready, K * b)
                    for m in range(K):
                        a = i * D + m * P
                        group(bank[:, m * NTOK:(m + 1) * NTOK],
                              [(w_att[:, k, a:a + P], hT[:, par, k, :]) for k in range(K)],
                              psum if m == K - 1 else None)

            def att_v(b, par):
                if after(b, 1):
                    pe.wait_ge(at["v_ready"], b)
                else:
                    pe.wait_ge(ws_ready, 2)
                for t in range(T):
                    group(PS[5][:, t * D:(t + 1) * D],
                          [(hT[:, par, k, t * P:(t + 1) * P], w_vp[:, k, :]) for k in range(K)],
                          at["v_psum"] if t == T - 1 else None)

            def att_scores(b, par):
                pe.wait_ge(at["q_ready"], K * (b + 1))
                pe.wait_ge(at["k_ready"], K * (b + 1))
                if after(b, 1):
                    pe.wait_ge(at["exp_done"], T * b)
                for t in range(T):
                    group(PS[4][:, t * NTOK:(t + 1) * NTOK],
                          [(qT[:, par, k, t * P:(t + 1) * P], kT[:, par, k, :]) for k in range(K)],
                          at["s_psum"] if t == T - 1 else None)

            def att_exT(b, par):
                pe.wait_ge(at["exp_done"], T * (b + 1))
                for m in range(T):
                    for t in range(T):
                        tr = pe.transpose(PS[par][:, m * NTOK + t * P:m * NTOK + (t + 1) * P],
                                          ex[:, par, t, m * P:(m + 1) * P], ident[:, :])
                tr.then_inc(at["exT_psum"], 1)

            def att_out(b, par):
                bank = out_bank("att", b, par)
                pe.wait_ge(at["v_ready"], b + 1)
                pe.wait_ge(at["exT_ready"], b + 1)
                for t in range(T):
                    group(bank[:, t * D:(t + 1) * D],
                          [(exT[:, par, m, t * P:(t + 1) * P], vp[:, par, m, :]) for m in range(T)],
                          S["att"]["out_psum"] if t == T - 1 else None)

            def setup23():
                pe.wait_ge(L["wmod23"], 16)
                pe.wait_ge(silu_ready, 3)
                pe.wait_ge(s5_ready, 1)
                for j in range(NMOD2 + NMOD3):
                    c = cond_silu if j < NMOD2 else cond
                    group(PS[4][:, j * B:(j + 1) * B], [(wmod23[:, k, j * P:(j + 1) * P], c[:, k, :]) for k in range(K)])
                pe.wait_ge(L["w_gat"], 32)
                for m in range(K):
                    a = NMOD2 + NMOD3 + m
                    group(PS[4][:, a * B:(a + 1) * B],
                          [(w_qpart[:, k, m * P:(m + 1) * P], cond[:, k, :]) for k in range(K)],
                          mod23_psum if m == K - 1 else None)
                for g, name in enumerate(("gate_msa", "gate_mlp")):
                    a = (MOD[name] - NMOD0) * P
                    group(PS[5][0:B, g * D:(g + 1) * D],
                          [(cond_silu[:, k, :], wmod23[:, k, a:a + D]) for k in range(K)], mod23_psum if g else None)

            def setup_vp():
                pe.wait_ge(L["w_att"], 16)
                pe.wait_ge(gates2_ready, 1)
                for m in range(K):
                    group(PS[4][:, m * D:(m + 1) * D],
                          [(w_att[:, k, 2 * D + m * P:2 * D + (m + 1) * P], w_att[:, k, 3 * D:4 * D])
                           for k in range(K)])
                group(PS[5][:, 0:D], [(col("v_b", k).broadcast_to([P, P]), w_att[:, k, 3 * D:4 * D]) for k in range(K)],
                      ws_psum)

            def begin(n):
                transposes(n, 0, 0)

            def phase(n, follow):
                if n == "s5":
                    pe.wait_ge(s5_ready, 1)
                if n in MLPS:
                    pe.wait_ge(LW[n], 32)
                if n == "ff0":
                    pe.wait_ge(ws_ready, 2)
                if n == "gat":
                    transposes(n, 1, 1)
                    gat_zero_rows(0, 0)
                    gat_self(0, 0)
                    gat_q(0, 0, 0)
                    gat_q(0, 0, 1)
                    gat_k(0, 0)
                    gat_v(0, 0)
                if n == "att":
                    att_qk(0, 0)
                    att_v(0, 0)

                def one(b, par):
                    if n == "s5" or n in MLPS:
                        if n == "s5":
                            s5_in_mm(b, par)
                        else:
                            up(n, b, par)
                        if before_end(b, 1):
                            transposes(n, b + 1, 1 - par)
                        if n == "s5" and isinstance(b, int) and b == LAST:
                            setup23()
                        if n == "s5" and isinstance(b, int) and b == LAST + 1:
                            setup_vp()
                        if after(b, 1):
                            (s5_out_mm if n == "s5" else lambda *a: down(n, *a))(b - 1, 1 - par)
                    more = before_end(b, 1)
                    if n == "gat":
                        if more:
                            gat_zero_rows(b + 1, 1 - par)
                            gat_self(b + 1, 1 - par)
                        if after(b, 1):
                            gat_out(b - 1, 1 - par)
                        gat_scores(b, par, 0)
                        if before_end(b, 2):
                            transposes(n, b + 2, par)
                        gat_scores(b, par, 1)
                        if more:
                            gat_q(b + 1, 1 - par, 0)
                            gat_q(b + 1, 1 - par, 1)
                            gat_k(b + 1, 1 - par)
                        gat_wT(b, par, 0)
                        if more:
                            gat_v(b + 1, 1 - par)
                        gat_wT(b, par, 1)
                    if n == "att":
                        if more:
                            transposes(n, b + 1, 1 - par)
                        att_scores(b, par)
                        if more:
                            att_qk(b + 1, 1 - par)
                        att_exT(b, par)
                        if more:
                            att_v(b + 1, 1 - par)
                            att_out(b, par)
                steps(pe, one)
                if follow:
                    begin(follow)
                last = (B - 1) % 2
                if n == "s5":
                    s5_out_mm(B - 1, last)
                elif n in MLPS:
                    down(n, B - 1, last)
                elif n == "gat":
                    gat_out(B - 1, last)
                else:
                    att_out(B - 1, last)

            begin("s5")
            for n, follow in zip(ORDER, ORDER[1:] + [None]):
                phase(n, follow)

        @block.vector
        def _(dve):
            chain = [0]

            def link(ins):
                chain[0] += 1
                ins.then_inc(setup_step, 1)
                dve.wait_ge(setup_step, chain[0])

            def ts(out_, in_, s1, s2=None, op0=ALU.mult, op1=None):
                if op1 is None:
                    return dve.tensor_scalar(out_, in_, s1, None, op0)
                return dve.tensor_scalar(out_, in_, s1, s2, op0, op1)

            def stt(out_, in0, scalar, in1, op0, op1):
                return dve.scalar_tensor_tensor(out=out_, in0=in0, scalar=scalar, in1=in1, op0=op0, op1=op1)

            def c(i):
                return sc[:, i:i + 1]

            def s5_scalars():
                dve.wait_ge(L["small"], 16 * 5)
                dve.wait_ge(act_setup, 1)
                link(dve.tensor_tensor(c(1), col("Lam_re"), c(0), ALU.mult))
                link(dve.tensor_tensor(c(3), col("Lam_im"), c(0), ALU.mult))
                link(ts(c(12), c(3), float(1 / (2 * np.pi)), ROUND, ALU.mult, ALU.add))
                link(ts(c(4), c(12), -ROUND, None, ALU.add))
                link(stt(c(5), c(4), -TWO_PI_HI, c(3), ALU.mult, ALU.add))
                link(stt(c(6), c(4), -TWO_PI_MID, c(5), ALU.mult, ALU.add))
                link(stt(c(11), c(4), -TWO_PI_LO, c(6), ALU.mult, ALU.add))
                link(ts(c(7), c(11), PI, -PI, ALU.min, ALU.max))
                link(stt(c(12), c(7), -1.0, c(7), ALU.mult, ALU.max))
                link(ts(c(8), c(12), -1.0, HALF_PI, ALU.mult, ALU.add))

            def s5_setup():
                dve.wait_ge(act_setup, 4)
                link(dve.tensor_tensor(c(13), c(2), c(10), ALU.mult))
                link(ts(c(13), c(13), -1.0, None, ALU.add))
                link(dve.tensor_tensor(c(14), c(2), c(9), ALU.mult))
                re, im = col("Lam_re"), col("Lam_im")
                link(dve.tensor_tensor(c(15), re, re, ALU.mult))
                link(stt(c(16), im, im, c(15), ALU.mult, ALU.add))
                link(dve.reciprocal(c(17), c(16)))
                link(dve.tensor_tensor(c(18), c(13), re, ALU.mult))
                link(stt(c(19), c(14), im, c(18), ALU.mult, ALU.add))
                link(dve.tensor_tensor(c(20), c(19), c(17), ALU.mult))
                link(dve.tensor_tensor(c(21), c(13), im, ALU.mult))
                link(stt(c(22), c(14), re, c(21), ALU.mult, ALU.subtract))
                link(dve.tensor_tensor(c(23), c(22), c(17), ALU.mult))
                link(ts(c(24), c(23), sign[:, 0:1], -1.0, ALU.mult, ALU.mult))
                link(ts(c(25), c(20), sign[:, 0:1]))
                link(ts(c(26), sign[:, 0:1], 2.0))
                dve.wait_ge(L["s5"], 16)
                link(ts(s5_tmp[:, 0, :], s5_bc[:, 0, :], c(20)))
                link(ts(s5_tmp[:, 1, :], s5_bc[:, 0, :], c(23)))
                stt(s5_in[:, 0, :], s5_bc[:, 1, :], c(24), s5_tmp[:, 0, :], ALU.mult, ALU.add).then_inc(s5_in_ready, 1)
                stt(s5_in[:, 1, :], s5_bc[:, 1, :], c(25), s5_tmp[:, 1, :], ALU.mult, ALU.add).then_inc(s5_in_ready, 1)
                link(ts(s5_out[:, 0, :], s5_bc[:, 2, :], c(26)))
                link(ts(s5_out[:, 1, :], s5_bc[:, 3, :], -2.0))
                dve.wait_ge(consts_done, 2)
                for k in range(K):
                    link(ts(s5_diag[:, k, :], ident[:, :], col("D_diag", k)))
                link(dve.memset(decay[:, :], 1.0))
                link(ts(decay[:, :], decay[:, :], c(2)))
                link(dve.memset(cosT[:, 0:1], 1.0))
                link(dve.memset(sinT[:, 0:1], 0.0))
                ck, sk = c(10), c(9)
                n = 1
                while n < NTOK:
                    link(ts(rot[:, 0, 0:n], sinT[:, 0:n], sk))
                    link(ts(rot[:, 1, 0:n], cosT[:, 0:n], sk))
                    link(stt(cosT[:, n:2 * n], cosT[:, 0:n], ck, rot[:, 0, 0:n], ALU.mult, ALU.subtract))
                    link(stt(sinT[:, n:2 * n], sinT[:, 0:n], ck, rot[:, 1, 0:n], ALU.mult, ALU.add))
                    if 2 * n < NTOK:
                        i = 27 + 3 * (n.bit_length() % 2)
                        link(dve.tensor_tensor(c(i), sk, sk, ALU.mult))
                        link(stt(c(i + 1), ck, ck, c(i), ALU.mult, ALU.subtract))
                        link(stt(c(i + 2), sk, 2.0, ck, ALU.mult, ALU.mult))
                        ck, sk = c(i + 1), c(i + 2)
                    n *= 2
                dve.wait_ge(s5_inT_psum, 1)
                dve.tensor_copy(s5_inT[:, :, :, :].rearrange("p i k n -> p (i k n)"), PS[4][:, :])\
                   .then_inc(s5_ready, 1)

            def mods0():
                dve.wait_ge(mod0_psum, 1)
                a, m = COLS["mod"][0], mod
                link(dve.tensor_tensor(m[:, 0:NMOD0, :], PS[2][:, 0:NMOD0 * B].rearrange("p (j b) -> p j b", b=B),
                                       cols[:, a:a + NMOD0].unsqueeze(2).broadcast_to([P, NMOD0, B]), ALU.add))
                link(dve.tensor_tensor(gate_rows[:, 0:2, 0, :], PS[3][0:B, :].rearrange("b (g d) -> b g d", g=2),
                                       gate_bias[:, 0:2, :], ALU.add))
                link(dve.memset(gate_rows[:, 0, 1, :], 0.0))
                dve.tensor_tensor(gate_rows[:, 1, 1, :], gate_rows[:, 1, 0, :], out_bias[:, 0, :], ALU.mult)\
                   .then_inc(gates0_ready, 1)
                v = lambda name: mod[:, MOD[name]:MOD[name] + K, :]
                link(ts(one_ff[:, :, :], v("scale_ff"), 1.0, None, ALU.add))
                link(stt(MS[:, 1, :, :], v("scale_c"), 1.0, one_ff[:, :, :], ALU.add, ALU.mult))
                link(dve.tensor_tensor(MH[:, 1, :, :], v("shift_c"), one_ff[:, :, :], ALU.mult))
                link(dve.tensor_tensor(MH[:, 1, :, :], MH[:, 1, :, :], v("shift_ff"), ALU.add))
                link(dve.tensor_copy(MH[:, 0, :, :], v("shift_a")))
                ts(MS[:, 0, :, :], v("scale_a"), 1.0, None, ALU.add).then_inc(mod0_ready, 1)

            def silu():
                dve.wait_ge(silu_ready, 1)
                ts(sig[:, :, :], sig[:, :, :], 1.0, None, ALU.add).then_inc(silu_ready, 1)
                dve.wait_ge(silu_ready, 2)
                link(dve.reciprocal(sig[:, :, :], sig[:, :, :]))
                dve.tensor_tensor(cond_silu[:, :, :], cond[:, :, :], sig[:, :, :], ALU.mult).then_inc(silu_ready, 1)

            def mods23():
                dve.wait_ge(mod23_psum, 2)
                a, n23 = COLS["mod"][0] + NMOD0, NMOD2 + NMOD3
                link(dve.tensor_tensor(mod[:, NMOD0:, :], PS[4][:, 0:n23 * B].rearrange("p (j b) -> p j b", b=B),
                                       cols[:, a:a + n23].unsqueeze(2).broadcast_to([P, n23, B]), ALU.add))
                link(dve.tensor_copy(qpart[:, :, :],
                                     PS[4][:, n23 * B:(n23 + K) * B].rearrange("p (j b) -> p j b", b=B)))
                link(dve.tensor_tensor(gate_rows[:, 2:4, 0, :], PS[5][0:B, :].rearrange("b (g d) -> b g d", g=2),
                                       gate_bias[:, 2:4, :], ALU.add))
                dve.tensor_tensor(gate_rows[:, 2:4, 1, :], gate_rows[:, 2:4, 0, :], out_bias[:, 1:3, :], ALU.mult)\
                   .then_inc(gates2_ready, 1)
                v = lambda name: mod[:, MOD[name]:MOD[name] + K, :]
                for name, sc_, sh in (("ssm", "scale_msa", "shift_msa"), ("ff2", "scale_mlp", "shift_mlp")):
                    j = NORMED.index(name)
                    link(ts(MS[:, j, :, :], v(sc_), 1.0, None, ALU.add))
                    link(dve.tensor_copy(MH[:, j, :, :], v(sh)))
                for name, w, sc_, sh in (("att", "norm1_w", "film1_scale", "film1_shift"),
                                         ("ff3", "norm2_w", "film2_scale", "film2_shift")):
                    j, a = NORMED.index(name), COLS[w][0]
                    link(stt(MS[:, j, :, :], v(sc_), 1.0, cols[:, a:a + K].unsqueeze(2).broadcast_to([P, K, B]),
                             ALU.add, ALU.mult))
                    link(dve.tensor_copy(MH[:, j, :, :], v(sh)))
                link(dve.tensor_tensor(bout[:, :], row("bout0"), row("bout1"), ALU.add))

            def vp_weights():
                dve.wait_ge(ws_psum, 1)
                dve.tensor_copy(w_vp[:, :, :], PS[4][:, :].rearrange("p (k n) -> p k n", k=K)).then_inc(ws_ready, 1)
                dve.tensor_tensor(att_row[:, :], PS[5][:, 0:D], row("proj_b"), ALU.add).then_inc(ws_ready, 1)

            def statistics(n, b, par):
                s, (kind, eps) = S[n], NORMS[n]
                wait_x(dve, n, b)
                for t in range(T):
                    dve.bn_stats(stats[:, par, t, :], X[:, bass.ds(b * 2 + t, 1), :].rearrange("p o d -> p (o d)"))\
                       .then_inc(stats_done, 1)
                dve.wait_ge(stats_done, T * (nth(n, b) + 1))
                mean_e, m2_e, mean_o, m2_o = (stats[:, par, :, i] for i in (1, 2, 4, 5))
                mean, m2, dif, dif2, mean2, sq = (mv[:, par, i, :] for i in range(6))
                dve.tensor_tensor(dif, mean_e, mean_o, ALU.subtract).then_inc(aggr_done, 1)
                stt(m2, m2_e, D * eps, m2_o, ALU.add, ALU.add).then_inc(aggr_done, 1)
                dve.tensor_tensor(mean2, mean_e, mean_o, ALU.add).then_inc(aggr_done, 1)
                dve.wait_ge(aggr_done, 5 * nth(n, b) + 3)
                stt(dif2, dif, 0.25, dif, ALU.mult, ALU.mult).then_inc(aggr_done, 1)
                if kind == "rms":
                    stt(sq, mean2, 0.25, mean2, ALU.mult, ALU.mult).then_inc(aggr_done, 1)
                    dve.wait_ge(aggr_done, 5 * nth(n, b) + 5)
                    dve.tensor_tensor(msq[:, par, :], dif2, sq, ALU.add).then_inc(s["msq_done"], 1)
                    dve.wait_ge(s["msq_done"], b + 1)
                    stt(var_eps[:, par, :], m2, 1 / D, msq[:, par, :], ALU.mult, ALU.add).then_inc(var_ready, 1)
                else:
                    ts(mean, mean2, 0.5).then_inc(aggr_done, 1)
                    dve.wait_ge(aggr_done, 5 * nth(n, b) + 5)
                    stt(var_eps[:, par, :], m2, 1 / D, dif2, ALU.mult, ALU.add).then_inc(var_ready, 1)

            def normalise(n, b, par):
                s, kind = S[n], NORMS[n][0]
                dve.wait_ge(rstd_ready, nth(n, b) + 1)
                if after(b, 2):
                    dve.wait_ge(s["xT_psum"], b - 1)
                for t in range(T):
                    xb = X[:, bass.ds(b * 2 + t, 1), :].rearrange("p o d -> p (o d)")
                    r = rstd[:, par, t:t + 1]
                    if kind == "rms":
                        ins = ts(xn[:, par, t, :], xb, r)
                    else:
                        ins = ts(xn[:, par, t, :], xb, mv[:, par, 0, t:t + 1], r, ALU.subtract, ALU.mult)
                    ins.then_inc(xn_ready, 1)

            def modulate(n, b, par):
                s, j = S[n], NORMED.index(n)
                dve.wait_ge(s["xT_psum"], b + 1)
                if after(b, 2):
                    if n in MLPS:
                        dve.wait_ge(s["hid_psum"], (b - 1) * (MLPS[n][0] // P // 2))
                    else:
                        dve.wait_ge(at["v_psum"], b - 1)
                for k in range(K):
                    ts(hT[:, par, k, :], PS[par][:, k * NTOK:(k + 1) * NTOK], MS[:, j, k, bass.ds(b, 1)],
                       MH[:, j, k, bass.ds(b, 1)], ALU.mult, ALU.add).then_inc(s["hT_ready"], 1)

            def gate(n, b, par):
                s = S[n]
                dve.wait_ge(s["out_psum"], b + 1)
                if n in GATES:
                    dve.wait_ge(gate_loaded[par], loads(b, par) + 8 * B * GATES.index(n))
                o = PS[6 + par][:, :].rearrange("p (t d) -> p t d", t=T)
                if n == "ff3":
                    dve.tensor_tensor(upd[:, par, :, :], o, row("mlp_b2").unsqueeze(1).broadcast_to([P, T, D]),
                                      ALU.add).then_inc(s["out_read"], 1)
                else:
                    dve.tensor_tensor(upd[:, par, :, :], o, gates[:, par, 0:1, :].broadcast_to([P, T, D]),
                                      ALU.mult).then_inc(s["out_read"], 1)

            def add_upd(n, b, par):
                xb = X[:, bass.ds(b * 2, 2), :]
                dve.wait_ge(S[n]["upd_ready"], b + 1)
                dve.tensor_tensor(xb, xb, upd[:, par, :, :], ALU.add).then_inc(S[n]["x_ready"], 1)

            def s5_rotate(b, par):
                dve.wait_ge(s5["bu_psum"], b + 1)
                if after(b, 2):
                    dve.wait_ge(s5["rot_ready"], b - 1)
                for i, table in enumerate((cosT, sinT)):
                    dve.tensor_tensor(bu[:, par, i, :], PS[2 + par][:, i * NTOK:(i + 1) * NTOK], table[:, :],
                                      ALU.mult).then_inc(s5["bu_ready"], 1)

            def s5_scan(b, par):
                dve.wait_ge(s5["rot_ready"], b + 1)
                if after(b, 2):
                    dve.wait_ge(s5["zc_ready"], b - 1)
                    dve.wait_ge(S["s5"]["out_psum"], b - 1)
                dve.tensor_tensor_scan(zst[:, par, :], decay[:, :], wrot[:, par, :], 0.0, ALU.mult, ALU.add)\
                   .then_inc(s5["scan_ready"], 1)
                dve.wait_ge(s5["scan_ready"], b + 1)
                dve.tensor_tensor(zs[:, par, :], zst[:, par, :], sinT[:, :], ALU.mult).then_inc(s5["zs_ready"], 1)

            def gat_nz(b, par):
                dve.wait_ge(ga["xs_ready"], T * (b + 1))
                if after(b, 2):
                    dve.wait_ge(ga["nz_psum"], b - 1)
                ts(nz[:, par, :], rsum[:, par, :], 0.0, None, ALU.not_equal).then_inc(ga["nz_ready"], 1)

            def gat_labels(b, par):
                dve.wait_ge(adj_loaded[par], loads(b, par))
                wb = row("w_bias").unsqueeze(1).broadcast_to([P, 4 * NONGT, LABELS])
                dve.tensor_tensor(adj_w, adj[par], wb, ALU.mult).then_inc(ga["adj_w"], 1)
                dve.tensor_reduce(cnt, adj[par], AX.X, ALU.add).then_inc(ga["adj_used"], 1)
                dve.wait_ge(ga["adj_w"], b + 1)
                dve.tensor_reduce(lab, adj_w, AX.X, ALU.add).then_inc(ga["lab"], 1)
                dve.wait_ge(ga["adj_used"], b + 1)
                ts(pen, cnt, 0.0, NEG, ALU.is_le, ALU.mult).then_inc(ga["pen"], 1)
                dve.wait_ge(ga["lab"], b + 1)
                dve.wait_ge(ga["pen"], b + 1)
                stt(cbias[par].rearrange("p d t m -> p (d t m)"), lab, row("b_bias"), pen, ALU.add, ALU.add)\
                    .then_inc(ga["cb"], 1)

            def gat_sfT(b, par):
                dve.wait_ge(ga["sfA_ready"], K * (b + 1))
                dve.wait_ge(ga["nz_psum"], b + 1)
                if after(b, 2):
                    dve.wait_ge(S["gat"]["out_psum"], b - 1)
                for k in range(K):
                    stt(sfT[par][:, k, :], PS[1][:, 0:NTOK], qpart[:, k, bass.ds(b, 1)], sfA[:, k, :],
                        ALU.mult, ALU.add).then_inc(ga["sfT_ready"], 1)
                dve.wait_ge(ga["sfT_ready"], K * (b + 1))
                if after(b, 1):
                    dve.wait_ge(ga["v_psum"], b)
                dve.tensor_copy(kvrep, sfT[par][:, :, 0:NONGT].unsqueeze(2).broadcast_to([P, K, HPC, NONGT]))\
                   .then_inc(ga["kvrep_ready"], 1)

            def gat_KB(b, par):
                dve.wait_ge(ga["k_psum"], b + 1)
                if after(b, 2):
                    dve.wait_ge(ga["s_psum"], T * (b - 1))
                for g in range(4):
                    stt(KB[par][:, g, :, :],
                        PS[1][:, 256 + g * NONGT:256 + (g + 1) * NONGT].unsqueeze(1).broadcast_to([P, HPK, NONGT]),
                        col("bk", g), head_mask[:, :, :], ALU.add, ALU.mult).then_inc(ga["KB_ready"], 1)

            def gat_VB(b, par):
                dve.wait_ge(ga["v_psum"], b + 1)
                if after(b, 2):
                    dve.wait_ge(S["gat"]["out_psum"], b - 1)
                M = HPC * NONGT
                dve.tensor_tensor(VB[par].rearrange("p d (c n) -> p (d c) n", c=CH),
                                  PS[3][0:M, :].rearrange("p (g n) -> p g n", n=HPC * DH),
                                  v_mask[:, :, :].rearrange("p h e -> p (h e)").unsqueeze(1)
                                  .broadcast_to([M, 2 * CH, HPC * DH]), ALU.mult).then_inc(ga["VB_ready"], 1)

            def gat_bias(b, par, t):
                dve.wait_ge(ga["s_psum"], T * b + (t + 1))
                dve.wait_ge(ga["cb"], b + 1)
                if after(b, 1):
                    dve.wait_ge(ga["exp_done"], T * (b - 1) + (t + 1))
                for d in range(2):
                    ins = dve.tensor_tensor(
                        sco[t][:, d * HEADS:(d + 1) * HEADS, :],
                        PS[4 + d][:, 0:HEADS * NONGT].rearrange("p (h m) -> p h m", m=NONGT),
                        cbias[par][:, d, t, :].unsqueeze(1).broadcast_to([P, HEADS, NONGT]), ALU.add)
                ins.then_inc(ga["s_biased"], 1)
                dve.wait_ge(ga["s_biased"], T * b + (t + 1))
                dve.tensor_reduce(smax[t], sco[t], AX.X, ALU.max).then_inc(ga["smax_done"], 1)

            def gat_sum(b, par, t):
                dve.wait_ge(ga["exp_done"], T * b + (t + 1))
                dve.tensor_reduce(ssum[t], prb[t], AX.X, ALU.add).then_inc(ga["ssum_done"], 1)
                dve.wait_ge(ga["ssum_done"], T * b + (t + 1))
                dve.reciprocal(srec[t], ssum[t]).then_inc(ga["srec_done"], 1)

            def gat_residual(b, par):
                dve.wait_ge(S["gat"]["out_psum"], b + 1)
                o = PS[6][:, :].rearrange("p (t d) -> p t d", t=T)
                dve.tensor_tensor(upd[:, par, :, :], o, bout[:, :].unsqueeze(1).broadcast_to([P, T, D]), ALU.add)\
                   .then_inc(S["gat"]["out_read"], 1)
                dve.wait_ge(S["gat"]["out_read"], b + 1)
                xb = X[:, bass.ds(b * 2, 2), :]
                stt(xb, upd[:, par, :, :], 0.0, xb, ALU.max, ALU.add).then_inc(S["gat"]["x_ready"], 1)

            def att_max(b, par):
                dve.wait_ge(at["s_psum"], b + 1)
                dve.tensor_reduce(amax[:, par, :], PS[4][:, :].rearrange("p (t m) -> p t m", t=T), AX.X, ALU.max)\
                   .then_inc(at["amax_done"], 1)
                dve.wait_ge(at["amax_done"], b + 1)
                if after(b, 2):
                    dve.wait_ge(at["exp_done"], T * (b - 1))
                ts(nmax[:, par, :], amax[:, par, :], -(D ** -0.5)).then_inc(at["nmax_done"], 1)

            def att_v(b, par):
                dve.wait_ge(at["v_psum"], b + 1)
                if after(b, 2):
                    dve.wait_ge(S["att"]["out_psum"], b - 1)
                dve.tensor_copy(vp[:, par, :, :].rearrange("p t d -> p (t d)"), PS[5][:, :]).then_inc(at["v_ready"], 1)

            def att_exT(b, par):
                dve.wait_ge(at["exT_psum"], b + 1)
                if after(b, 2):
                    dve.wait_ge(S["att"]["out_psum"], b - 1)
                dve.tensor_copy(exT[:, par, :, :].rearrange("p m n -> p (m n)"), PS[par][:, :])\
                   .then_inc(at["exT_ready"], 1)
                dve.wait_ge(at["exp_done"], T * (b + 1))
                dve.reciprocal(arec[:, par, :], asum[:, par, :]).then_inc(at["arec_done"], 1)

            def att_residual(b, par):
                xb = X[:, bass.ds(b * 2, 2), :]
                dve.tensor_tensor(xb, xb, att_row[:, :].unsqueeze(1).broadcast_to([P, T, D]), ALU.add)\
                   .then_inc(at["row_added"], 1)
                dve.wait_ge(S["att"]["out_psum"], b + 1)
                dve.wait_ge(at["arec_done"], b + 1)
                dve.wait_ge(at["row_added"], b + 1)
                for t in range(T):
                    xt = X[:, bass.ds(b * 2 + t, 1), :].rearrange("p o d -> p (o d)")
                    ins = stt(xt, PS[6 + par][:, t * D:(t + 1) * D], arec[:, par, t:t + 1], xt, ALU.mult, ALU.add)
                ins.then_inc(S["att"]["out_read"], 1)

            def begin(n):
                if n in NORMS:
                    for b in range(2):
                        statistics(n, b, b)
                        normalise(n, b, b)
                    if n != "s5":
                        modulate(n, 0, 0)
                if n == "gat":
                    gat_nz(0, 0)
                    gat_nz(1, 1)

            def phase(n, follow):
                if n == "gat":
                    gat_labels(0, 0)
                    gat_sfT(0, 0)
                    gat_KB(0, 0)
                    gat_VB(0, 0)
                    gat_nz(2, 0)
                if n == "att":
                    att_v(0, 0)

                def one(b, par):
                    more = before_end(b, 1)
                    if n in NORMS and before_end(b, 2):
                        statistics(n, b + 2, par)
                    if n in ("s5", *MLPS) and after(b, 2):
                        add_upd(n, b - 2, par)
                    if n == "s5":
                        s5_rotate(b, par)
                    if n in MLPS and more:
                        modulate(n, b + 1, 1 - par)
                    if n == "att":
                        if more:
                            modulate(n, b + 1, 1 - par)
                        att_max(b, par)
                        att_exT(b, par)
                        if more:
                            att_v(b + 1, 1 - par)
                    if n in NORMS and before_end(b, 2):
                        normalise(n, b + 2, par)
                    if n == "s5":
                        s5_scan(b, par)
                        if isinstance(b, int) and b == LAST:
                            mods23()
                        if isinstance(b, int) and b == LAST + 1:
                            vp_weights()
                    if n in ("s5", *MLPS) and after(b, 1):
                        gate(n, b - 1, 1 - par)
                    if n == "gat":
                        gat_bias(b, par, 0)
                        if more:
                            gat_sfT(b + 1, 1 - par)
                        gat_bias(b, par, 1)
                        if after(b, 1):
                            gat_residual(b - 1, 1 - par)
                        gat_sum(b, par, 0)
                        if more:
                            gat_KB(b + 1, 1 - par)
                        gat_sum(b, par, 1)
                        if more:
                            gat_labels(b + 1, 1 - par)
                            gat_VB(b + 1, 1 - par)
                        if before_end(b, 3):
                            gat_nz(b + 3, 1 - par)
                    if n == "att" and more:
                        att_residual(b, par)
                steps(dve, one)
                if follow:
                    begin(follow)
                last = (B - 1) % 2
                if n in ("s5", *MLPS):
                    add_upd(n, B - 2, 1 - last)
                    gate(n, B - 1, last)
                    add_upd(n, B - 1, last)
                elif n == "gat":
                    gat_residual(B - 1, last)
                else:
                    att_residual(B - 1, last)

            s5_scalars()
            link(dve.memset(sign[0:STATES, :], 1.0))
            link(dve.memset(sign[STATES:P, :], -1.0))
            s5_setup()
            mods0()
            begin("s5")
            silu()
            for n, follow in zip(ORDER, ORDER[1:] + [None]):
                phase(n, follow)


_OUT = ((B, NTOK, D), "float32")


def lay_out(inputs):
    g = {k: np.asarray(v) for k, v in inputs.items()}

    def tiles(w):
        return np.ascontiguousarray(w.reshape(-1, P, w.shape[1]).transpose(1, 0, 2))

    def column(v):
        return v.reshape(-1, P).T

    x = g["x"]
    cond = g["cond_1024"]
    a = {"x": x, "cond": np.ascontiguousarray(cond.T.reshape(K, P, B).transpose(1, 0, 2))}
    a["wmod0"] = tiles(np.concatenate([g["L0_cond_Wm"], g["L0_cond_Wc"]], 1))
    a["wmod23"] = tiles(np.concatenate([g["L2_cond_ada_w"], g["L3_cond_film1_w"], g["L3_cond_film2_w"]], 1))
    mod_bias = np.concatenate([g["L0_cond_bm"], g["L0_cond_bc"], g["L2_cond_ada_b"], g["L3_cond_film1_b"],
                               g["L3_cond_film2_b"]])
    two = lambda v: np.concatenate([v, v])
    parts = {
        "mod": column(mod_bias), "ff0_b1": column(g["L0_cond_b1"]), "ssm_b1": column(g["L2_cond_ssm_b1"]),
        "ff2_b1": column(g["L2_cond_ff_b1"]), "ff3_b1": column(g["L3_cond_mlp_b1"]),
        "b_self": column(g["L1_cond_b_self"]), "bq": column(g["L1_cond_bq"].reshape(-1)),
        "bk": column(g["L1_cond_bk"].reshape(-1)), "q_b": column(g["L3_cond_q_b"]), "k_b": column(g["L3_cond_k_b"]),
        "norm1_w": column(g["L3_cond_norm1_w"]), "norm2_w": column(g["L3_cond_norm2_w"]),
        "D_diag": column(g["L0_cond_D_diag"]), "Lam_re": column(two(g["L0_cond_Lam_re"])),
        "Lam_im": column(two(g["L0_cond_Lam_im"])), "log_step": column(two(g["L0_cond_log_step"])),
        "v_b": column(g["L3_cond_v_b"]),
    }
    a["cols"] = np.ascontiguousarray(np.concatenate([parts[n] for n in COLS], 1))
    bout = g["L1_cond_bout"].reshape(2, D)
    a["rows"] = np.concatenate([bout[0], bout[1], g["L3_cond_proj_b"], g["L3_cond_mlp_b2"], g["L1_cond_w_bias"],
                                g["L1_cond_b_bias"].reshape(1)])
    bias = {n: mod_bias[MOD[n] * P:MOD[n] * P + D] for n in ("gate_a", "gate_ff", "gate_msa", "gate_mlp")}
    a["gate_bias"] = np.concatenate(list(bias.values()))
    a["out_bias"] = np.concatenate([g["L0_cond_b2"], g["L2_cond_ssm_b2"], g["L2_cond_ff_b2"]])
    br, bi, cr, ci = g["L0_cond_B_re"], g["L0_cond_B_im"], g["L0_cond_C_re"].T, g["L0_cond_C_im"].T
    a["s5_bc"] = np.ascontiguousarray(np.stack([np.concatenate(v) for v in ((br, bi), (bi, br), (cr, ci), (ci, cr))], 1))
    for n, w1, w2 in (("ff0", "L0_cond_W1", "L0_cond_W2"), ("ssm", "L2_cond_ssm_w1", "L2_cond_ssm_w2"),
                      ("ff2", "L2_cond_ff_w1", "L2_cond_ff_w2"), ("ff3", "L3_cond_mlp_w1", "L3_cond_mlp_w2")):
        a[f"{n}_w1"], a[f"{n}_w2"] = tiles(g[w1]), tiles(g[w2])
    w_self = g["L1_cond_W_self"].T
    wo = g["L1_cond_Wout"].reshape(2, D, D)
    a["w_gat"] = tiles(np.concatenate([w_self[:D], *(w.T for w in g["L1_cond_Wq"]), *(w.T for w in g["L1_cond_Wk"]),
                                       *(w.T for w in wo)], 1))
    a["w_qpart"] = tiles(w_self[D:])
    a["w_att"] = tiles(np.concatenate([g["L3_cond_q_w"], g["L3_cond_k_w"], g["L3_cond_v_w"].T, g["L3_cond_proj_w"]], 1))
    m = g["mask_BxSxSx11_ik0"]
    d0 = m[:, :, :NONGT].reshape(B, T, P, NONGT, LABELS)
    d1 = m[:, :NONGT].transpose(0, 2, 1, 3).reshape(B, T, P, NONGT, LABELS)
    a["adj"] = np.ascontiguousarray(np.stack([d0, d1], 1).transpose(0, 3, 1, 2, 4, 5)).reshape(B, P, -1)
    return a


def kernel(**inputs):
    import concourse.bacc as _bacc
    from concourse.bass_utils import run_bass_kernel_spmd as _run

    nc = _bacc.Bacc("TRN2", target_bir_lowering=False, num_devices=1)
    laid = lay_out(inputs)
    arrays, aps = {}, {}
    for name, a in laid.items():
        arrays[f"in_{name}"] = a
        aps[name] = nc.dram_tensor(f"in_{name}", a.shape, mybir.dt.from_np(a.dtype), kind="ExternalInput").ap()
    out = nc.dram_tensor("out_0", _OUT[0], F32, kind="ExternalOutput").ap()
    build_program(nc, aps, out)
    r = _run(nc, [arrays], core_ids=[0])
    return r.results[0]["out_0"]
```

```python
from contextlib import ExitStack

import numpy as np

import concourse.bass as bass
from concourse import mybir

ALU = mybir.AluOpType
ACT = mybir.ActivationFunctionType
AX = mybir.AxisListType
F32 = mybir.dt.float32
F32R = mybir.dt.float32r
BF16 = mybir.dt.bfloat16
I32 = mybir.dt.int32

P = 128
B = 16
NTOK = 256
T = NTOK // P
D = 256
K = D // P
STATES = 64
HEADS, DH, NONGT, LABELS = 16, 16, 20, 11
HPC = 4
CH = HEADS // HPC
HPK = P // DH
NEG = -9000000000000000.0
PI = 3.1415925
HALF_PI = float(np.pi / 2)
ROUND = 1.5 * 2 ** 23
TWO_PI_HI = 6.28125
TWO_PI_MID = 1.9340515e-3
TWO_PI_LO = float(2 * np.pi - 6.28125 - np.float64(np.float32(1.9340515e-3)))

MOD0 = ["shift_a", "scale_a", "gate_a", "shift_ff", "scale_ff", "gate_ff", "scale_c", "shift_c"]
MOD2 = ["shift_msa", "scale_msa", "gate_msa", "shift_mlp", "scale_mlp", "gate_mlp"]
MOD3 = ["film1_scale", "film1_shift", "film2_scale", "film2_shift"]
MOD = {name: K * n for n, name in enumerate(MOD0 + MOD2 + MOD3)}
NMOD = K * len(MOD)
NMOD0, NMOD2, NMOD3 = K * len(MOD0), K * len(MOD2), K * len(MOD3)

COLS = {}
for _name, _n in [("mod", NMOD), ("ff0_b1", 8), ("ssm_b1", 2), ("ff2_b1", 4), ("ff3_b1", 8), ("b_self", 2),
                  ("bq", 4), ("bk", 4), ("q_b", 2), ("k_b", 2), ("norm1_w", 2), ("norm2_w", 2), ("D_diag", 2),
                  ("Lam_re", 1), ("Lam_im", 1), ("log_step", 1), ("v_b", 2)]:
    COLS[_name] = sum(n for _, n in COLS.values()), _n
NCOLS = sum(n for _, n in COLS.values())
ROWS = {}
for _name, _n in [("bout0", D), ("bout1", D), ("proj_b", D), ("mlp_b2", D), ("w_bias", LABELS), ("b_bias", 1)]:
    ROWS[_name] = sum(n for _, n in ROWS.values()), _n
NROWS = sum(n for _, n in ROWS.values())
BIASED = ["ff0", "ssm", "ff2"]
GATES = ["s5", "ff0", "ssm", "ff2"]

MLPS = {
    "ff0": (1024, ACT.Gelu_apprx_tanh, "layer", 1e-5),
    "ssm": (256, ACT.Gelu, "layer", 1e-6),
    "ff2": (512, ACT.Gelu_apprx_tanh, "layer", 1e-6),
    "ff3": (1024, ACT.Gelu, "rms", 1e-6),
}
BANKS = {n: v[0] // P // 2 for n, v in MLPS.items()}
PIECE = 1024
WEIGHT_AT = {"ff0": 0, "ssm": 0, "ff2": MLPS["ssm"][0] * 2 * K, "ff3": 0}
PIECES = {"ff0": 4, "ssm": 7, "ff2": 7, "ff3": 11}
PIECE_AT = [0, 1, 2, 3, 0, 1, 2, 1, 2, 0, 3]
ATT_QK_AT, ATT_V_AT = 0, 3 * PIECE
NORMS = {"s5": ("layer", 1e-5), "att": ("rms", 1e-6), **{n: v[2:] for n, v in MLPS.items()}}
ORDER = ["s5", "ff0", "gat", "ssm", "ff2", "att", "ff3"]
NORMED = [n for n in ORDER if n in NORMS]

FIRST, TURNS = 3, 4
LAST = FIRST + 2 * TURNS
AHEAD = {n: 2 if n == "s5" else 3 for n in NORMS}
SPLIT = [n for n in ORDER if n in MLPS or n == "att"]


def build_program(nc, A, out):
    with ExitStack() as ctx:
        def sb(name, shape, dt=F32):
            return ctx.enter_context(nc.sbuf_tensor(name, shape, dt))

        def sem(name):
            return ctx.enter_context(nc.semaphore(name))

        PS = [ctx.enter_context(nc.psum_tensor(f"bank{i}", [P, 512], F32)) for i in range(8)]

        X = sb("X", [P, B * T, D])
        cond = sb("cond", [P, K, B])
        cond_silu = sb("cond_silu", [P, K, B])
        sig = sb("sig", [P, K, B])
        cols = sb("cols", [P, NCOLS])
        rows = sb("rows", [P, NROWS])
        mod = sb("mod", [P, NMOD, B])
        MS = sb("MS", [P, len(NORMED), K, B])
        MH = sb("MH", [P, len(NORMED), K, B])
        one_ff = sb("one_ff", [P, K, B])
        ident = sb("ident", [P, P])
        ident_b = sb("ident_b", [P, P], BF16)
        half_neg = sb("half_neg", [P, T])
        s5_inT = sb("s5_inT", [P, 2, K, P])
        s5_out = sb("s5_out", [P, 2, D])
        s5_diag = sb("s5_diag", [P, K, P])
        cosT = sb("cosT", [P, NTOK])
        sinT = sb("sinT", [P, NTOK])
        decay = sb("decay", [P, NTOK])
        rot = sb("rot", [P, 2, P])
        sc = sb("sc", [P, 40])
        sign = sb("sign", [P, 1])

        w_raw = sb("w_raw", [P, 2, PIECE])
        w_gat = sb("w_gat", [P, K, 7 * D])
        w_qpart = sb("w_qpart", [P, K, D])
        qpart = sb("qpart", [P, K, B])
        w_att = sb("w_att", [P, K, 4 * D])
        w_vp = sb("w_vp", [P, K, D])
        att_row = sb("att_row", [P, D])
        bout = sb("bout", [P, D])

        stats = sb("stats", [P, 2, T, 6])
        mv = sb("mv", [P, 2, 6, T])
        msq = sb("msq", [P, 2, T])
        var_eps = sb("var_eps", [P, 2, T])
        rstd = sb("rstd", [P, 2, T])
        xn = sb("xn", [P, 2, T, D])
        hT = sb("hT", [P, 2, K, NTOK])
        gT = sb("gT", [P, 2, 8, NTOK])
        upd = sb("upd", [P, 2, T, D])
        gates = sb("gates", [P, 2, 2, D])
        exT = sb("exT", [P, 2, T, NTOK])

        s5_bc = upd[:, :, :, :].rearrange("p a t d -> p (a t) d")
        s5_in = exT[:, 0, :, :]
        s5_tmp = exT[:, 1, :, :]

        NW = 2 * K * MLPS["ff0"][0]
        G_COLS, H_COLS = 2 * 8 * NTOK, 2 * K * NTOK
        rooms = (nc.sbuf_usable_end - 8 * (NW + G_COLS + H_COLS)) // 64 * 64
        top = [rooms]

        def place(name, shape, dt, at):
            return nc.alloc_sbuf_tensor_at(name, shape, dt, offset=at)

        def new_room(n):
            top[0] += 4 * n
            return top[0] - 4 * n

        weight_room, split_room, input_room = new_room(2 * NW), new_room(2 * G_COLS), new_room(2 * H_COLS)
        wmod0 = place("wmod0", [P, K, NMOD0 * P], F32, weight_room)
        w_hi = place("w_hi", [P, NW], F32R, weight_room)
        w_lo = place("w_lo", [P, NW], F32R, weight_room + 4 * NW)
        g_hi = place("g_hi", [P, 2, 8, NTOK], F32R, split_room)
        g_lo = place("g_lo", [P, 2, 8, NTOK], F32R, split_room + 4 * G_COLS)
        wmod23 = place("wmod23", [P, K, (NMOD2 + NMOD3) * P], F32, split_room)
        bias_at = split_room + 4 * K * (NMOD2 + NMOD3) * P
        gate_bias = place("gate_bias", [B, 4, D], F32, bias_at)
        out_bias = place("out_bias", [B, 3, D], F32, bias_at + 4 * 4 * D)
        assert bias_at + 4 * 7 * D <= input_room
        arena = place("arena", [P, 2 * G_COLS], F32, split_room)
        h_hi = place("h_hi", [P, 2, K, NTOK], F32R, input_room)
        h_lo = place("h_lo", [P, 2, K, NTOK], F32R, input_room + 4 * H_COLS)
        gate_rows = place("gate_rows", [B, 4, 2, D], F32, input_room)

        def w1(part, n, k, m):
            a = WEIGHT_AT[n] + k * MLPS[n][0] + m * P
            return part[:, a:a + P]

        def w2(part, n, m):
            a = WEIGHT_AT[n] + K * MLPS[n][0] + m * D
            return part[:, a:a + D]

        bu = gT[:, :, 0:2, :]
        wrot = gT[:, :, 2, :]
        zst = gT[:, :, 3, :]
        zc = gT[:, :, 4, :]
        zs = gT[:, :, 5, :]

        room = [0]

        def carve(n):
            room[0] += n
            assert room[0] <= 2 * G_COLS
            return arena[:, room[0] - n:room[0]]

        adj = [sb(f"adj{i}", [P, 4 * NONGT, LABELS], I32)[:, :, :] for i in range(2)]
        rsum = sb("rsum", [P, 2, T])
        adj_w = carve(4 * NONGT * LABELS).rearrange("p (g l) -> p g l", l=LABELS)
        cnt = carve(4 * NONGT)
        pen = carve(4 * NONGT)
        lab = carve(4 * NONGT)
        cbias = [carve(4 * NONGT).rearrange("p (d t m) -> p d t m", d=2, t=T) for _ in range(2)]
        sfA = carve(K * NTOK).rearrange("p (k n) -> p k n", k=K)
        sfT = [exT[:, i, :, :] for i in range(2)]
        kvrep = carve(K * HPC * NONGT).rearrange("p (k h m) -> p k h m", k=K, h=HPC)
        KB = [carve(4 * HPK * NONGT).rearrange("p (g h m) -> p g h m", g=4, h=HPK) for _ in range(2)]
        VB = [carve(2 * D)[0:HPC * NONGT, :].rearrange("p (d n) -> p d n", d=2) for _ in range(2)]
        sco = [carve(2 * HEADS * NONGT).rearrange("p (g m) -> p g m", m=NONGT) for _ in range(T)]
        prb = [carve(2 * HEADS * NONGT).rearrange("p (g m) -> p g m", m=NONGT) for _ in range(T)]
        smax = [carve(2 * HEADS) for _ in range(T)]
        ssum = [carve(2 * HEADS) for _ in range(T)]
        srec = [carve(2 * HEADS) for _ in range(T)]
        QT = [gT[:, i, 0:4, :].rearrange("p (d k) n -> p d k n", d=2) for i in range(2)]
        wT = gT[:, :, 4:8, :].rearrange("p a (c2 c) n -> p a c2 (c n)", c2=2)
        nz = sb("nz", [P, 2, T], BF16)
        head_mask = sb("head_mask", [P, HPK, NONGT])
        v_mask = sb("v_mask", [HPC * NONGT, HPC, DH])

        qT = gT[:, :, 0:2, :]
        kT = gT[:, :, 2:4, :]
        vp = gT[:, :, 4:6, :]
        ex = gT[:, :, 6:8, :]
        Q, KK, V, E = (slice(2 * i, 2 * i + 2) for i in range(4))
        amax = sb("amax", [P, 2, T])
        nmax = sb("nmax", [P, 2, T])
        asum = sb("asum", [P, 2, T])
        arec = sb("arec", [P, 2, T])

        assert nc.sbuf_base <= rooms

        gate_dram = nc.dram_tensor("gate_dram", (B, len(GATES) * 2 * D), F32, kind="Internal").ap()

        def col(name, n=0):
            return cols[:, COLS[name][0] + n:COLS[name][0] + n + 1]

        def row(name):
            return rows[:, ROWS[name][0]:ROWS[name][0] + ROWS[name][1]]

        L = {n: sem(f"loaded_{n}") for n in ("small", "x0", "x", "wmod0", "s5", "wmod23", "w_gat", "w_att")}
        piece_loaded = [sem(f"piece_loaded_{i}") for i in range(2)]
        w_hi_ready, w_lo_ready = sem("w_hi_ready"), sem("w_lo_ready")
        h_hi_ready, h_lo_ready, g_hi_ready, g_lo_ready = (
            sem(k) for k in ("h_hi_ready", "h_lo_ready", "g_hi_ready", "g_lo_ready"))
        consts_done = sem("consts_done")
        const_step = sem("const_step")
        setup_step = sem("setup_step")
        act_setup = sem("act_setup")
        silu_ready = sem("silu_ready")
        mod0_psum = sem("mod0_psum")
        mod0_ready = sem("mod0_ready")
        s5_in_ready = sem("s5_in_ready")
        s5_inT_psum = sem("s5_inT_psum")
        s5_ready = sem("s5_ready")
        mod23_psum = sem("mod23_psum")
        gates0_ready = sem("gates0_ready")
        gates2_ready = sem("gates2_ready")
        gates_stored = sem("gates_stored")
        gates2_stored = sem("gates2_stored")
        stored = sem("stored")

        S = {}
        for n in ORDER:
            names = ["xT_psum", "hT_ready", "out_psum", "out_read"]
            if n != "att":
                names += ["x_ready"]
            if n in NORMS and NORMS[n][0] == "rms":
                names += ["msq_done"]
            if n in MLPS:
                names += ["hid_psum", "hid_ready"]
            if n in BIASED:
                names += ["upd_ready"]
            S[n] = {k: sem(f"{n}_{k}") for k in names}
        gate_loaded = [sem(f"gate_loaded_{i}") for i in range(2)]
        adj_loaded = [sem(f"adj_loaded_{i}") for i in range(2)]
        stats_done, aggr_done, var_ready, rstd_ready, xn_ready = (
            sem(k) for k in ("stats_done", "aggr_done", "var_ready", "rstd_ready", "xn_ready"))
        for n in ("s5", "ff3"):
            S[n]["upd_ready"] = S[n]["out_read"]
        S["att"]["x_ready"] = S["att"]["out_read"]
        s5 = {k: sem(f"s5_{k}") for k in
                                ("bu_psum", "bu_ready", "rot_ready", "scan_ready", "zs_ready", "zc_ready")}
        ga = {k: sem(f"gat_{k}") for k in
                                ("adj_used", "adj_w", "lab", "pen", "cb", "xs_ready", "nz_ready", "nz_psum",
                                 "sf_psum", "sf_used", "sfA_ready", "sfT_ready", "kvrep_ready", "q_psum", "q_ready", "k_psum",
                                 "KB_ready", "v_psum", "VB_ready", "s_psum", "s_biased", "smax_done", "s_shifted",
                                 "exp_done", "ssum_done", "srec_done", "w_ready", "wT_psum", "wT_ready")}
        at = {k: sem(f"att_{k}") for k in
                                ("w_hi", "w_lo", "q_psum", "q_hi", "k_psum", "k_hi", "qk_lo", "v_psum", "v_ready",
                                 "v_hi", "v_lo", "s_psum", "amax_done", "nmax_done", "exp_done", "arec_done",
                                 "exT_psum", "exT_ready", "exT_hi", "exT_lo", "row_added")}
        ws_psum = sem("ws_psum")
        ws_ready = sem("ws_ready")
        block = ctx.enter_context(nc.Block())

        def prev(n):
            return S[ORDER[ORDER.index(n) - 1]]

        def wait_x(eng, n, b):
            if n == "s5":
                if isinstance(b, int) and b < 2:
                    eng.wait_ge(L["x0"], 16)
                else:
                    eng.wait_ge(L["x"], 16 * (B // 2 - 1))
            else:
                eng.wait_ge(prev(n)["x_ready"], b + 1)

        def steps(eng, one):
            for b in range(FIRST):
                one(b, b % 2)
            with eng.Fori(0, TURNS) as i:
                for j in range(2):
                    one(i * 2 + (FIRST + j), (FIRST + j) % 2)
            for b in range(LAST, B):
                one(b, b % 2)

        def hid_bank(banks, par, j):
            return j if banks == 4 else banks * par + j

        def loads(b, par):
            return (b - par) * 8 + 16

        def nth(n, b):
            return b + B * NORMED.index(n)

        def mth(n, b):
            return b + B * SPLIT.index(n)

        def hidden_count(n, b, j=0):
            earlier = list(MLPS)[:list(MLPS).index(n)]
            return b * BANKS[n] + (j + B * sum(BANKS[e] for e in earlier))

        def after(b, lag):
            return not isinstance(b, int) or b >= lag

        def before_end(b, ahead):
            return not isinstance(b, int) or b + ahead < B

        def piece_at(i):
            return PIECE * PIECE_AT[i]

        def pieces_at(n, b):
            at = {"s5": {1: [0], 2: [1], LAST: [2], LAST + 1: [3]}, "gat": {0: [4], 1: [5], 2: [6]},
                  "att": {1: [7], 2: [8], B - 1: [9, 10]}}
            return at[n][b] if isinstance(b, int) and n in at and b in at[n] else []

        def att_weights():
            return (ATT_QK_AT, w_att[:, :, 0:2 * D]), (ATT_V_AT, w_vp[:, :, :])

        def hidden_lo(eng, n, b, par):
            for j in range(BANKS[n]):
                eng.wait_ge(g_hi_ready, 2 * hidden_count(n, b, j + 1))
                eng.tensor_tensor(g_lo[:, par, 2 * j:2 * j + 2, :], gT[:, par, 2 * j:2 * j + 2, :],
                                  g_hi[:, par, 2 * j:2 * j + 2, :], ALU.subtract).then_inc(g_lo_ready, 1)

        @block.sync
        def _(sp):
            def load(dst, src, s):
                sp.dma_start(dst, src).then_inc(s, 16)

            load(cols[:, :], A["cols"], L["small"])
            load(cond[:, :, :], A["cond"], L["small"])
            load(rows[:, :], A["rows"].partition_broadcast(P), L["small"])
            load(gate_bias[:, :, :].rearrange("b g d -> b (g d)"), A["gate_bias"].partition_broadcast(B), L["small"])
            load(out_bias[:, :, :].rearrange("b g d -> b (g d)"), A["out_bias"].partition_broadcast(B), L["small"])
            load(s5_bc[:, :, :], A["s5_bc"], L["s5"])
            xv = A["x"].rearrange("b (t p) d -> p (b t) d", p=P)
            load(X[:, 0:4, :], xv[:, 0:4, :], L["x0"])
            load(wmod0[:, :, :], A["wmod0"], L["wmod0"])
            for c in range(1, B // 2):
                load(X[:, 4 * c:4 * c + 4, :], xv[:, 4 * c:4 * c + 4, :], L["x"])

            def load_piece(i):
                if i >= 2:
                    sp.wait_ge(w_lo_ready, i - 1)
                load(w_raw[:, i % 2, :], A["w_mlp"][:, i * PIECE:(i + 1) * PIECE], piece_loaded[i % 2])

            load_piece(0)
            load_piece(1)
            load(wmod23[:, :, :], A["wmod23"], L["wmod23"])
            load(w_gat[:, :, :], A["w_gat"], L["w_gat"])
            load(w_qpart[:, :, :], A["w_qpart"], L["w_gat"])
            load(w_att[:, :, :], A["w_att"], L["w_att"])

            def load_gate(n, g):
                def one(b, par):
                    if after(b, 2):
                        sp.wait_ge(S[n]["x_ready"], b - 1)
                    src = gate_dram[bass.ds(b, 1), 2 * D * g:2 * D * (g + 1)]
                    sp.dma_start(gates[:, par, :, :].rearrange("p a d -> p (a d)"),
                                 src.broadcast_to([P, 2 * D])).then_inc(gate_loaded[par], 16)
                    if n == "s5" and isinstance(b, int) and b == FIRST - 1:
                        load_piece(2)
                        load_piece(3)
                steps(sp, one)

            sp.wait_ge(gates0_ready, 1)
            sp.dma_start(gate_dram[:, 0:4 * D], gate_rows[:, 0:2, :, :].rearrange("b g a d -> b (g a d)"))\
              .then_inc(gates_stored, 16)
            sp.wait_ge(gates_stored, 16)
            load_gate("s5", 0)
            sp.wait_ge(gates2_ready, 1)
            sp.dma_start(gate_dram[:, 4 * D:8 * D], gate_rows[:, 2:4, :, :].rearrange("b g a d -> b (g a d)"))\
              .then_inc(gates2_stored, 16)
            def load_adj(b, par):
                if after(b, 2):
                    sp.wait_ge(ga["adj_used"], b - 1)
                src = A["adj"][b] if isinstance(b, int) else A["adj"][bass.ds(b, 1)].rearrange("o p n -> (o p) n")
                sp.dma_start(adj[par].rearrange("p g l -> p (g l)"), src).then_inc(adj_loaded[par], 16)

            load_adj(0, 0)
            load_adj(1, 1)
            sp.wait_ge(S["s5"]["x_ready"], B)
            load_piece(4)
            load_piece(5)
            load_gate("ff0", 1)

            def gat_loads(b, par):
                if after(b, 2):
                    load_adj(b, par)
                if isinstance(b, int) and b == FIRST - 1:
                    load_piece(6)

            steps(sp, gat_loads)
            load_piece(7)
            load_piece(8)
            sp.wait_ge(S["ff0"]["x_ready"], B)
            load_gate("ssm", 2)
            sp.wait_ge(S["ssm"]["x_ready"], B)
            load_gate("ff2", 3)
            load_piece(9)
            load_piece(10)

            ov = out.rearrange("b (t p) d -> p (b t) d", p=P)

            def store(b, par):
                sp.wait_ge(S["ff3"]["x_ready"], b + 1)
                if isinstance(b, int):
                    sp.dma_start(ov[:, 2 * b:2 * b + 2, :], X[:, 2 * b:2 * b + 2, :]).then_inc(stored, 16)
                else:
                    sp.dma_start(ov[:, bass.ds(b * 2, 2), :], X[:, bass.ds(b * 2, 2), :]).then_inc(stored, 16)

            steps(sp, store)
            sp.wait_ge(stored, 16 * B)

        @block.gpsimd
        def _(pool):
            pool.memset(ident[:, :], 0.0).then_inc(const_step, 1)
            pool.memset(ident_b[:, :], 0.0).then_inc(const_step, 1)
            pool.memset(half_neg[:, :], -0.5).then_inc(const_step, 1)
            pool.memset(head_mask[:, :, :], DH ** -0.5).then_inc(const_step, 1)
            pool.memset(v_mask[:, :, :], 1.0).then_inc(const_step, 1)
            pool.wait_ge(const_step, 5)
            for m in (ident, ident_b):
                pool.affine_select(out=m[:, :], in_=m[:, :], compare_op=ALU.not_equal, fill=1.0, base=0,
                                   pattern=[[-1, P]], channel_multiplier=1).then_inc(const_step, 1)
            pool.affine_select(out=head_mask[:, :, :], in_=head_mask[:, :, :], compare_op=ALU.is_ge, fill=0.0, base=0,
                               pattern=[[-DH, HPK], [0, NONGT]], channel_multiplier=1).then_inc(const_step, 1)
            pool.affine_select(out=v_mask[:, :, :], in_=v_mask[:, :, :], compare_op=ALU.is_ge, fill=0.0, base=0,
                               pattern=[[-NONGT, HPC], [0, DH]], channel_multiplier=1).then_inc(const_step, 1)
            pool.wait_ge(const_step, 9)
            pool.affine_select(out=head_mask[:, :, :], in_=head_mask[:, :, :], compare_op=ALU.is_ge, fill=0.0,
                               base=DH - 1, pattern=[[DH, HPK], [0, NONGT]], channel_multiplier=-1)\
                .then_inc(consts_done, 1)
            pool.affine_select(out=v_mask[:, :, :], in_=v_mask[:, :, :], compare_op=ALU.is_ge, fill=0.0,
                               base=NONGT - 1, pattern=[[NONGT, HPC], [0, DH]], channel_multiplier=-1)\
                .then_inc(consts_done, 1)

            def inv_std(n, b, par):
                s = S[n]
                pool.wait_ge(var_ready, nth(n, b) + 1)
                pool.tensor_tensor(rstd[:, par, :], var_eps[:, par, :], half_neg[:, :], ALU.pow)\
                    .then_inc(rstd_ready, 1)

            def add_bias(n, b, par):
                pool.wait_ge(S[n]["out_read"], b + 1)
                pool.tensor_tensor(upd[:, par, :, :], upd[:, par, :, :],
                                   gates[:, par, 1:2, :].broadcast_to([P, T, D]), ALU.add).then_inc(S[n]["upd_ready"], 1)

            def s5_step(b, par):
                pool.wait_ge(s5["bu_ready"], 2 * (b + 1))
                pool.tensor_tensor(wrot[:, par, :], bu[:, par, 0, :], bu[:, par, 1, :], ALU.add)\
                    .then_inc(s5["rot_ready"], 1)
                pool.wait_ge(s5["scan_ready"], b + 1)
                if after(b, 2):
                    pool.wait_ge(S["s5"]["out_psum"], b - 1)
                pool.tensor_tensor(zc[:, par, :], zst[:, par, :], cosT[:, :], ALU.mult).then_inc(s5["zc_ready"], 1)

            def piece_lo(i):
                a = piece_at(i)
                pool.wait_ge(w_hi_ready, i + 1)
                pool.tensor_tensor(w_lo[:, a:a + PIECE], w_raw[:, i % 2, :], w_hi[:, a:a + PIECE], ALU.subtract)\
                    .then_inc(w_lo_ready, 1)

            def input_lo(n, b, par):
                pool.wait_ge(h_hi_ready, mth(n, b) + 1)
                pool.tensor_tensor(h_lo[:, par, :, :], hT[:, par, :, :], h_hi[:, par, :, :], ALU.subtract)\
                    .then_inc(h_lo_ready, 1)

            def att_weights_lo():
                pool.wait_ge(at["w_hi"], 2)
                for a, raw in att_weights():
                    n = raw.shape[1] * raw.shape[2]
                    view = lambda w: w[:, a:a + n].rearrange("p (k n) -> p k n", k=K)
                    pool.tensor_tensor(view(w_lo), raw, view(w_hi), ALU.subtract).then_inc(at["w_lo"], 1)

            def att_lo(b, par, what, raw, hi, lo):
                pool.wait_ge(hi, b + 1)
                pool.tensor_tensor(g_lo[:, par, what, :], raw[:, par, :, :], g_hi[:, par, what, :], ALU.subtract)\
                    .then_inc(lo, 1)

            def att_qk_lo(b, par):
                att_lo(b, par, Q, qT, at["q_hi"], at["qk_lo"])
                att_lo(b, par, KK, kT, at["k_hi"], at["qk_lo"])

            def begin(n):
                if n in NORMS:
                    inv_std(n, 0, 0)
                    inv_std(n, 1, 1)
                if n in SPLIT:
                    inv_std(n, 2, 0)
                    inv_std(n, 3, 1)
                    input_lo(n, 0, 0)
                    input_lo(n, 1, 1)

            def phase(n, follow):
                if n == "att":
                    att_qk_lo(0, 0)

                def one(b, par):
                    if n == "s5" and before_end(b, 2):
                        inv_std(n, b + 2, par)
                    if n == "s5":
                        s5_step(b, par)
                    if n == "ff2" and isinstance(b, int) and b == 2:
                        att_weights_lo()
                    if n == "att":
                        att_lo(b, par, V, vp, at["v_hi"], at["v_lo"])
                        if after(b, 1):
                            att_lo(b - 1, 1 - par, E, exT, at["exT_hi"], at["exT_lo"])
                        if before_end(b, 1):
                            att_qk_lo(b + 1, 1 - par)
                    if n in SPLIT:
                        if n in ("ff0", "ssm", "ff3"):
                            hidden_lo(pool, n, b, par)
                        if before_end(b, 2):
                            input_lo(n, b + 2, par)
                    for i in pieces_at(n, b):
                        piece_lo(i)
                    if n in BIASED and after(b, 1):
                        add_bias(n, b - 1, 1 - par)
                    if n in SPLIT and before_end(b, 4):
                        inv_std(n, b + 4, par)
                    if n == "gat":
                        gat_step(b, par)
                steps(pool, one)
                if n == "att":
                    att_lo(B - 1, (B - 1) % 2, E, exT, at["exT_hi"], at["exT_lo"])
                if follow:
                    begin(follow)
                if n in BIASED:
                    add_bias(n, B - 1, (B - 1) % 2)

            def gat_shift(b, t):
                pool.wait_ge(ga["smax_done"], T * b + (t + 1))
                pool.tensor_tensor(sco[t], sco[t], smax[t].unsqueeze(2).broadcast_to([P, 2 * HEADS, NONGT]),
                                   ALU.subtract).then_inc(ga["s_shifted"], 1)

            def gat_weights(b, t):
                pool.wait_ge(ga["srec_done"], T * b + (t + 1))
                pool.tensor_tensor(prb[t], prb[t], srec[t].unsqueeze(2).broadcast_to([P, 2 * HEADS, NONGT]),
                                   ALU.mult).then_inc(ga["w_ready"], 1)

            def gat_step(b, par):
                gat_shift(b, 0)
                gat_shift(b, 1)
                gat_weights(b, 0)
                gat_weights(b, 1)

            begin("s5")
            for n, follow in zip(ORDER, ORDER[1:] + [None]):
                phase(n, follow)

        @block.scalar
        def _(act):
            act.wait_ge(L["small"], 16 * 5)
            act.activation(sc[:, 0:1], col("log_step"), ACT.Exp).then_inc(act_setup, 1)
            act.wait_ge(setup_step, 1)
            act.activation(sc[:, 2:3], sc[:, 1:2], ACT.Exp).then_inc(act_setup, 1)
            act.activation(sig[:, :, :], cond[:, :, :], ACT.Exp, scale=-1.0).then_inc(silu_ready, 1)
            act.wait_ge(setup_step, 10)
            act.activation(sc[:, 9:10], sc[:, 7:8], ACT.Sin).then_inc(act_setup, 1)
            act.activation(sc[:, 10:11], sc[:, 8:9], ACT.Sin).then_inc(act_setup, 1)

            def modulate(n, b, par):
                s, j = S[n], NORMED.index(n)
                act.wait_ge(s["xT_psum"], b + 1)
                if after(b, 2):
                    act.wait_ge(s5["bu_psum"], b - 1)
                for k in range(K):
                    act.activation(hT[:, par, k, :], PS[par][:, k * NTOK:(k + 1) * NTOK], ACT.Identity,
                                   bias=MH[:, j, k, bass.ds(b, 1)], scale=MS[:, j, k, bass.ds(b, 1)])\
                        .then_inc(s["hT_ready"], 1)

            def input_hi(n, b, par):
                act.wait_ge(S[n]["hT_ready"], K * (b + 1))
                if n == "ff0" and not after(b, 2):
                    act.wait_ge(gates2_stored, 16)
                if after(b, 2):
                    if n in MLPS:
                        act.wait_ge(S[n]["hid_psum"], (b - 1) * BANKS[n])
                    else:
                        act.wait_ge(at["v_psum"], b - 1)
                act.activation(h_hi[:, par, :, :], hT[:, par, :, :], ACT.Copy).then_inc(h_hi_ready, 1)

            def piece_hi(i):
                a = piece_at(i)
                act.wait_ge(piece_loaded[i % 2], 16 * (i // 2 + 1))
                for n, follow in (("ff0", "ssm"), ("ff2", "ff3")):
                    if PIECES[n] <= i < PIECES[follow]:
                        act.wait_ge(S[n]["out_psum"], B)
                if i >= 9:
                    act.wait_ge(at["v_psum"], B)
                act.activation(w_hi[:, a:a + PIECE], w_raw[:, i % 2, :], ACT.Copy).then_inc(w_hi_ready, 1)

            def hidden(n, b, par):
                s, (H, fn, _, _) = S[n], MLPS[n]
                banks = BANKS[n]
                if after(b, 2):
                    act.wait_ge(s["out_psum"], b - 1)
                for j in range(banks):
                    act.wait_ge(s["hid_psum"], b * banks + (j + 1))
                    bank = PS[2 + hid_bank(banks, par, j)]
                    for i in range(2):
                        m = 2 * j + i
                        act.activation(gT[:, par, m, :], bank[:, i * NTOK:(i + 1) * NTOK], fn,
                                       bias=col(f"{n}_b1", m)).then_inc(s["hid_ready"], 1)
                        act.activation(g_hi[:, par, m, :], bank[:, i * NTOK:(i + 1) * NTOK], fn,
                                       bias=col(f"{n}_b1", m)).then_inc(g_hi_ready, 1)

            def gat_copy(b, par):
                wait_x(act, "gat", b)
                if not after(b, 2):
                    act.wait_ge(prev("gat")["xT_psum"], B)
                if after(b, 2):
                    act.wait_ge(S["gat"]["xT_psum"], b - 1)
                    act.wait_ge(ga["nz_ready"], b - 1)
                for t in range(T):
                    act.activation(xn[:, par, t, :], X[:, bass.ds(b * 2 + t, 1), :].rearrange("p o d -> p (o d)"),
                                   ACT.Copy, accum_out=rsum[:, par, t:t + 1]).then_inc(ga["xs_ready"], 1)

            def gat_xT(b, par):
                act.wait_ge(S["gat"]["xT_psum"], b + 1)
                if after(b, 2):
                    act.wait_ge(ga["sf_psum"], b - 1)
                act.activation(hT[:, par, :, :].rearrange("p k n -> p (k n)"), PS[0][:, :], ACT.Copy)\
                    .then_inc(S["gat"]["hT_ready"], 1)

            def gat_self(b, par):
                act.wait_ge(ga["sf_psum"], b + 1)
                if after(b, 1):
                    act.wait_ge(ga["sfT_ready"], K * b)
                for k in range(K):
                    act.activation(sfA[:, k, :], PS[2][:, k * NTOK:(k + 1) * NTOK], ACT.Identity,
                                   bias=col("b_self", k)).then_inc(ga["sfA_ready"], 1)

            def gat_q(b, par):
                if after(b, 2):
                    act.wait_ge(ga["s_psum"], T * (b - 1))
                for d in range(2):
                    act.wait_ge(ga["q_psum"], 2 * b + (d + 1))
                    for k in range(K):
                        act.activation(QT[par][:, d, k, :], PS[3 - d][:, k * NTOK:(k + 1) * NTOK], ACT.Identity,
                                       bias=col("bq", 2 * d + k)).then_inc(ga["q_ready"], 1)

            def gat_exp(b, par, t):
                act.wait_ge(ga["s_shifted"], T * b + (t + 1))
                if after(b, 1):
                    act.wait_ge(ga["wT_psum"], 4 * b - 2 * (T - 1 - t))
                act.activation(prb[t], sco[t], ACT.Exp).then_inc(ga["exp_done"], 1)

            def gat_wT(b, par, t):
                if after(b, 1) and t == 0:
                    act.wait_ge(S["gat"]["out_psum"], b)
                for d in range(2):
                    act.wait_ge(ga["wT_psum"], 4 * b + (2 * t + d + 1))
                    act.activation(wT[0:HPC * NONGT, t, d, :], PS[7 - 7 * d][0:HPC * NONGT, :], ACT.Copy)\
                        .then_inc(ga["wT_ready"], 1)

            def att_weights_hi():
                act.wait_ge(S["ssm"]["out_psum"], B)
                act.wait_ge(ws_ready, 2)
                for a, raw in att_weights():
                    n = raw.shape[1] * raw.shape[2]
                    act.activation(w_hi[:, a:a + n].rearrange("p (k n) -> p k n", k=K), raw, ACT.Copy)\
                       .then_inc(at["w_hi"], 1)

            def att_qk(b, par):
                for what, hi, psum, dst, bank, bias in ((Q, at["q_hi"], at["q_psum"], qT, PS[2], "q_b"),
                                                        (KK, at["k_hi"], at["k_psum"], kT, PS[3], "k_b")):
                    act.wait_ge(psum, b + 1)
                    if after(b, 2) and what is Q:
                        act.wait_ge(at["s_psum"], b - 1)
                    for to in (dst[:, par, :, :], g_hi[:, par, what, :]):
                        for k in range(K):
                            ins = act.activation(to[:, k, :], bank[:, k * NTOK:(k + 1) * NTOK], ACT.Identity,
                                                 bias=col(bias, k))
                    ins.then_inc(hi, 1)

            def att_v_hi(b, par):
                act.wait_ge(at["v_ready"], b + 1)
                if after(b, 2):
                    act.wait_ge(S["att"]["out_psum"], b - 1)
                act.activation(g_hi[:, par, V, :], vp[:, par, :, :], ACT.Copy).then_inc(at["v_hi"], 1)

            def att_exT_hi(b, par):
                act.wait_ge(at["exT_ready"], b + 1)
                if after(b, 2):
                    act.wait_ge(S["att"]["out_psum"], b - 1)
                act.activation(g_hi[:, par, E, :], exT[:, par, :, :], ACT.Copy).then_inc(at["exT_hi"], 1)

            def att_exp(b, par):
                act.wait_ge(at["nmax_done"], b + 1)
                if after(b, 2):
                    act.wait_ge(at["exT_psum"], b - 1)
                    act.wait_ge(at["arec_done"], b - 1)
                for t in range(T):
                    act.activation(ex[:, par, t, :], PS[4][:, t * NTOK:(t + 1) * NTOK], ACT.Exp,
                                   bias=nmax[:, par, t:t + 1], scale=D ** -0.5, accum_out=asum[:, par, t:t + 1])\
                        .then_inc(at["exp_done"], 1)

            def begin(n):
                if n == "s5":
                    act.wait_ge(mod0_ready, 1)
                    modulate(n, 0, 0)
                if n in SPLIT:
                    input_hi(n, 0, 0)
                    input_hi(n, 1, 1)
                if n == "gat":
                    gat_copy(0, 0)
                    gat_copy(1, 1)
                    gat_xT(0, 0)

            def phase(n, follow):
                if n == "gat":
                    gat_xT(1, 1)
                    gat_copy(2, 0)
                    gat_self(0, 0)
                    gat_q(0, 0)
                if n == "att":
                    att_qk(0, 0)

                def one(b, par):
                    if n == "s5" and before_end(b, 1):
                        modulate(n, b + 1, 1 - par)
                    for i in pieces_at(n, b) if n != "att" else []:
                        piece_hi(i)
                    if n in MLPS:
                        hidden(n, b, par)
                        if n == "ff2" and isinstance(b, int) and b == 2:
                            att_weights_hi()
                    if n == "gat":
                        if after(b, 1):
                            gat_wT(b - 1, 1 - par, 0)
                        if before_end(b, 1):
                            gat_self(b + 1, 1 - par)
                        if after(b, 1):
                            gat_wT(b - 1, 1 - par, 1)
                        gat_exp(b, par, 0)
                        if before_end(b, 2):
                            gat_xT(b + 2, par)
                        gat_exp(b, par, 1)
                        if before_end(b, 1):
                            gat_q(b + 1, 1 - par)
                        if before_end(b, 3):
                            gat_copy(b + 3, 1 - par)
                    if n == "att":
                        att_v_hi(b, par)
                        if after(b, 1):
                            att_exT_hi(b - 1, 1 - par)
                        att_exp(b, par)
                        if before_end(b, 1):
                            att_qk(b + 1, 1 - par)
                    if n in SPLIT and before_end(b, 2):
                        input_hi(n, b + 2, par)
                    if n == "att":
                        for i in pieces_at(n, b):
                            piece_hi(i)
                steps(act, one)
                if n == "att":
                    att_exT_hi(B - 1, (B - 1) % 2)
                if n == "gat":
                    gat_wT(B - 1, (B - 1) % 2, 0)
                    gat_wT(B - 1, (B - 1) % 2, 1)
                if follow:
                    begin(follow)

            begin("s5")
            for n, follow in zip(ORDER, ORDER[1:] + [None]):
                phase(n, follow)

        @block.tensor
        def _(pe):
            def group(dst, pairs, inc=None):
                for i, (l, r) in enumerate(pairs):
                    mm = pe.matmul(dst, l, r, start=(i == 0), stop=(i == len(pairs) - 1))
                if inc is not None:
                    mm.then_inc(inc, 1)

            pe.wait_ge(s5_in_ready, 2)
            pe.wait_ge(consts_done, 2)
            for i in range(2):
                for k in range(K):
                    tr = pe.transpose(PS[4][:, (2 * i + k) * P:(2 * i + k + 1) * P], s5_in[:, i, k * P:(k + 1) * P],
                                      ident[:, :])
            tr.then_inc(s5_inT_psum, 1)

            pe.wait_ge(L["small"], 16 * 5)
            pe.wait_ge(L["wmod0"], 16)
            for j in range(NMOD0):
                group(PS[2][:, j * B:(j + 1) * B],
                      [(wmod0[:, k, j * P:(j + 1) * P], cond[:, k, :]) for k in range(K)])
            for g, name in enumerate(("gate_a", "gate_ff")):
                a = MOD[name] * P
                group(PS[3][0:B, g * D:(g + 1) * D], [(cond[:, k, :], wmod0[:, k, a:a + D]) for k in range(K)],
                      mod0_psum if g else None)
            def transposes(n, b, par):
                s = S[n]
                if n == "gat":
                    pe.wait_ge(ga["xs_ready"], T * (b + 1))
                    bank = PS[0]
                    if after(b, 1):
                        pe.wait_ge(s["hT_ready"], b)
                    if after(b, 3):
                        pe.wait_ge(ga["wT_ready"], 4 * (b - 2))
                else:
                    pe.wait_ge(xn_ready, T * (nth(n, b) + 1))
                    bank = PS[par]
                    if prev(n) is S["gat"] and not after(b, 1):
                        pe.wait_ge(ga["wT_ready"], 4 * B)
                for k in range(K):
                    for t in range(T):
                        tr = pe.transpose(bank[:, k * NTOK + t * P:k * NTOK + (t + 1) * P],
                                          xn[:, par, t, k * P:(k + 1) * P], ident[:, :])
                tr.then_inc(s["xT_psum"], 1)

            def gat_zero_rows(b, par):
                pe.wait_ge(ga["nz_ready"], b + 1)
                if after(b, 1):
                    pe.wait_ge(ga["KB_ready"], 4 * b)
                for t in range(T):
                    mm = pe.matmul(PS[1][:, t * P:(t + 1) * P], nz[:, par, t:t + 1].broadcast_to([P, P]),
                                   ident_b[:, :], start=True, stop=True)
                mm.then_inc(ga["nz_psum"], 1)

            def out_bank(n, b, par):
                if after(b, 2):
                    pe.wait_ge(S[n]["out_read"], b - 1)
                elif n != "s5":
                    pe.wait_ge(prev(n)["out_read"], B)
                return PS[6 + par]

            def s5_in_mm(b, par):
                s = S["s5"]
                pe.wait_ge(s["hT_ready"], K * (b + 1))
                if after(b, 2):
                    pe.wait_ge(s5["bu_ready"], 2 * (b - 1))
                bank = out_bank("s5", b, par)
                for t in range(T):
                    for k in range(K):
                        pe.matmul(bank[:, t * D + k * P:t * D + (k + 1) * P], hT[:, par, k, t * P:(t + 1) * P],
                                  s5_diag[:, k, :], start=(t == 0 and k == 0), stop=False, skip_group_check=True)
                for i in range(2):
                    group(PS[2 + par][:, i * NTOK:(i + 1) * NTOK],
                          [(s5_inT[:, i, k, :], hT[:, par, k, :]) for k in range(K)], s5["bu_psum"] if i else None)

            def s5_out_mm(b, par):
                bank = PS[6 + par]
                pe.wait_ge(s5["zc_ready"], b + 1)
                pe.wait_ge(s5["zs_ready"], b + 1)
                for t in range(T):
                    tok = slice(t * P, (t + 1) * P)
                    pe.matmul(bank[:, t * D:(t + 1) * D], zc[:, par, tok], s5_out[:, 0, :], start=False, stop=False,
                              skip_group_check=True)
                    mm = pe.matmul(bank[:, t * D:(t + 1) * D], zs[:, par, tok], s5_out[:, 1, :], start=False,
                                   stop=True, skip_group_check=True)
                mm.then_inc(S["s5"]["out_psum"], 1)

            def up(n, b, par):
                s, banks = S[n], BANKS[n]
                pe.wait_ge(h_lo_ready, mth(n, b) + 1)
                for j in range(banks):
                    if banks == 4 and after(b, 1):
                        pe.wait_ge(g_hi_ready, 2 * hidden_count(n, b - 1, j + 1))
                    if banks < 4 and after(b, 2) and j == 0:
                        pe.wait_ge(g_hi_ready, 2 * hidden_count(n, b - 1))
                    for i in range(2):
                        m = 2 * j + i
                        group(PS[2 + hid_bank(banks, par, j)][:, i * NTOK:(i + 1) * NTOK],
                              [(w1(w, n, k, m), h[:, par, k, :]) for k in range(K)
                               for w, h in ((w_lo, h_hi), (w_hi, h_hi), (w_hi, h_lo))],
                              s["hid_psum"] if i else None)

            def down(n, b, par):
                s, H = S[n], MLPS[n][0]
                M = H // P
                bank = out_bank(n, b, par)
                pe.wait_ge(g_lo_ready, hidden_count(n, b + 1))
                for t in range(T):
                    group(bank[:, t * D:(t + 1) * D],
                          [(g[:, par, m, t * P:(t + 1) * P], w2(w, n, m)) for m in range(M)
                           for g, w in ((g_lo, w_hi), (g_hi, w_hi), (g_hi, w_lo))],
                          s["out_psum"] if t == T - 1 else None)

            WG = {name: slice(i * D, (i + 1) * D) for i, name in enumerate(("self", "q0", "q1", "k0", "k1"))}

            def gat_self(b, par):
                pe.wait_ge(S["gat"]["hT_ready"], b + 1)
                if after(b, 1):
                    pe.wait_ge(ga["q_ready"], 4 * b)
                for m in range(K):
                    group(PS[2][:, m * NTOK:(m + 1) * NTOK],
                          [(w_gat[:, k, m * P:(m + 1) * P], hT[:, par, k, :]) for k in range(K)],
                          ga["sf_psum"] if m == K - 1 else None)

            def gat_q(b, par, d):
                pe.wait_ge(ga["sfT_ready"], K * (b + 1))
                if d == 0 and after(b, 1):
                    pe.wait_ge(ga["VB_ready"], b)
                for m in range(K):
                    a = (1 + d) * D + m * P
                    group(PS[3 - d][:, m * NTOK:(m + 1) * NTOK],
                          [(w_gat[:, k, a:a + P], sfT[par][:, k, :]) for k in range(K)],
                          ga["q_psum"] if m == K - 1 else None)

            def gat_k(b, par):
                for d in range(2):
                    for m in range(K):
                        g = 2 * d + m
                        a = (3 + d) * D + m * P
                        group(PS[1][:, 256 + g * NONGT:256 + (g + 1) * NONGT],
                              [(w_gat[:, k, a:a + P], sfT[par][:, k, 0:NONGT]) for k in range(K)],
                              ga["k_psum"] if g == 3 else None)

            def gat_v(b, par):
                pe.wait_ge(ga["kvrep_ready"], b + 1)
                pe.wait_ge(ga["q_ready"], 4 * b + 2)
                group(PS[3][0:HPC * NONGT, :],
                      [(kvrep[:, k, :, :].rearrange("p h m -> p (h m)"), w_gat[:, k, 5 * D:7 * D]) for k in range(K)],
                      ga["v_psum"])

            def gat_scores(b, par, t):
                if t == 0:
                    pe.wait_ge(ga["KB_ready"], 4 * (b + 1))
                    pe.wait_ge(ga["q_ready"], 4 * (b + 1))
                    if after(b, 1):
                        pe.wait_ge(ga["s_biased"], T * b)
                else:
                    pe.wait_ge(ga["s_biased"], T * b + t)
                for d in range(2):
                    for k in range(K):
                        mm = pe.matmul(PS[4 + d][:, k * HPK * NONGT:(k + 1) * HPK * NONGT],
                                       QT[par][:, d, k, t * P:(t + 1) * P],
                                       KB[par][:, 2 * d + k, :, :].rearrange("p h m -> p (h m)"),
                                       start=True, stop=True)
                mm.then_inc(ga["s_psum"], 1)

            def gat_wT(b, par, t):
                pe.wait_ge(ga["w_ready"], T * b + (t + 1))
                for d in range(2):
                    bank = PS[7 - 7 * d]
                    if t:
                        pe.wait_ge(ga["wT_ready"], 4 * b + (2 * t + d - 1))
                    elif not d:
                        if after(b, 1):
                            pe.wait_ge(ga["wT_ready"], 4 * b)
                        else:
                            pe.wait_ge(prev("gat")["out_read"], B)
                    elif before_end(b, 2):
                        pe.wait_ge(S["gat"]["hT_ready"], b + 3)
                    for c in range(CH):
                        h0 = (d * HEADS + c * HPC)
                        tr = pe.transpose(bank[0:HPC * NONGT, c * P:(c + 1) * P],
                                          prb[t][:, h0:h0 + HPC, :].rearrange("p h m -> p (h m)"), ident[:, :])
                    tr.then_inc(ga["wT_psum"], 1)

            def gat_open(b, par):
                if after(b, 1):
                    pe.wait_ge(S["gat"]["out_read"], b)
                else:
                    pe.wait_ge(prev("gat")["out_read"], B)
                for t in range(T):
                    for k in range(K):
                        mm = pe.matmul(PS[6][:, t * D + k * P:t * D + (k + 1) * P], sfT[par][:, k, t * P:(t + 1) * P],
                                       ident[:, :], start=(t == 0 and k == 0), stop=False, skip_group_check=True)
                mm.then_inc(ga["sf_used"], 1)

            def gat_out(b, par):
                for t in range(T):
                    pe.wait_ge(ga["wT_ready"], 4 * b + (2 * t + 2))
                    for d in range(2):
                        for c in range(CH):
                            mm = pe.matmul(PS[6][:, t * D + c * HPC * DH:t * D + (c + 1) * HPC * DH],
                                           wT[0:HPC * NONGT, t, d, c * P:(c + 1) * P],
                                           VB[par][:, d, c * HPC * DH:(c + 1) * HPC * DH],
                                           start=False, stop=(d == 1), skip_group_check=True)
                mm.then_inc(S["gat"]["out_psum"], 1)

            def three(pairs):
                return [p(*part) for p in pairs for part in ((1, 0), (0, 0), (0, 1))]

            HL, WL, GL = (h_hi, h_lo), (w_hi, w_lo), (g_hi, g_lo)

            def att_qk(b, par):
                pe.wait_ge(h_lo_ready, mth("att", b) + 1)
                for i, (psum, hi, bank) in enumerate(((at["q_psum"], at["q_hi"], PS[2]), (at["k_psum"], at["k_hi"], PS[3]))):
                    if after(b, 1):
                        pe.wait_ge(hi, b)
                    for m in range(K):
                        a = ATT_QK_AT + i * D + m * P
                        group(bank[:, m * NTOK:(m + 1) * NTOK],
                              three([lambda x, y, k=k, a=a: (WL[x][:, a + k * 2 * D:a + k * 2 * D + P],
                                                             HL[y][:, par, k, :]) for k in range(K)]),
                              psum if m == K - 1 else None)

            def att_v(b, par):
                if after(b, 1):
                    pe.wait_ge(at["v_ready"], b)
                for t in range(T):
                    group(PS[5][:, t * D:(t + 1) * D],
                          three([lambda x, y, k=k, t=t: (HL[x][:, par, k, t * P:(t + 1) * P],
                                                         WL[y][:, ATT_V_AT + k * D:ATT_V_AT + (k + 1) * D])
                                 for k in range(K)]),
                          at["v_psum"] if t == T - 1 else None)

            def att_scores(b, par):
                pe.wait_ge(at["qk_lo"], 2 * (b + 1))
                if after(b, 1):
                    pe.wait_ge(at["exp_done"], T * b)
                for t in range(T):
                    group(PS[4][:, t * NTOK:(t + 1) * NTOK],
                          three([lambda x, y, k=k, t=t: (GL[x][:, par, Q.start + k, t * P:(t + 1) * P],
                                                         GL[y][:, par, KK.start + k, :]) for k in range(K)]),
                          at["s_psum"] if t == T - 1 else None)

            def att_exT(b, par):
                pe.wait_ge(at["exp_done"], T * (b + 1))
                if after(b, 1):
                    pe.wait_ge(at["exT_ready"], b)
                else:
                    pe.wait_ge(prev("att")["out_read"], B)
                for m in range(T):
                    for t in range(T):
                        tr = pe.transpose(PS[7][:, m * NTOK + t * P:m * NTOK + (t + 1) * P],
                                          ex[:, par, t, m * P:(m + 1) * P], ident[:, :])
                tr.then_inc(at["exT_psum"], 1)

            def att_out(b, par):
                pe.wait_ge(at["v_lo"], b + 1)
                pe.wait_ge(at["exT_lo"], b + 1)
                if after(b, 1):
                    pe.wait_ge(S["att"]["out_read"], b)
                for t in range(T):
                    group(PS[6][:, t * D:(t + 1) * D],
                          three([lambda x, y, m=m, t=t: (GL[x][:, par, E.start + m, t * P:(t + 1) * P],
                                                         GL[y][:, par, V.start + m, :]) for m in range(T)]),
                          S["att"]["out_psum"] if t == T - 1 else None)

            def setup23():
                pe.wait_ge(L["wmod23"], 16)
                pe.wait_ge(silu_ready, 3)
                pe.wait_ge(s5_ready, 1)
                for j in range(NMOD2 + NMOD3):
                    c = cond_silu if j < NMOD2 else cond
                    group(PS[4][:, j * B:(j + 1) * B], [(wmod23[:, k, j * P:(j + 1) * P], c[:, k, :]) for k in range(K)])
                pe.wait_ge(L["w_gat"], 32)
                for m in range(K):
                    a = NMOD2 + NMOD3 + m
                    group(PS[4][:, a * B:(a + 1) * B],
                          [(w_qpart[:, k, m * P:(m + 1) * P], cond[:, k, :]) for k in range(K)],
                          mod23_psum if m == K - 1 else None)
                for g, name in enumerate(("gate_msa", "gate_mlp")):
                    a = (MOD[name] - NMOD0) * P
                    group(PS[5][0:B, g * D:(g + 1) * D],
                          [(cond_silu[:, k, :], wmod23[:, k, a:a + D]) for k in range(K)], mod23_psum if g else None)

            def setup_vp():
                pe.wait_ge(L["w_att"], 16)
                pe.wait_ge(gates2_ready, 1)
                for m in range(K):
                    group(PS[4][:, m * D:(m + 1) * D],
                          [(w_att[:, k, 2 * D + m * P:2 * D + (m + 1) * P], w_att[:, k, 3 * D:4 * D])
                           for k in range(K)])
                group(PS[5][:, 0:D], [(col("v_b", k).broadcast_to([P, P]), w_att[:, k, 3 * D:4 * D]) for k in range(K)],
                      ws_psum)

            def begin(n):
                transposes(n, 0, 0)
                if n in SPLIT:
                    transposes(n, 1, 1)

            def phase(n, follow):
                if n == "s5":
                    pe.wait_ge(s5_ready, 1)
                if n in MLPS:
                    pe.wait_ge(w_lo_ready, PIECES[n])
                if n == "ff0":
                    pe.wait_ge(ws_ready, 2)
                if n == "gat":
                    transposes(n, 1, 1)
                    gat_zero_rows(0, 0)
                    gat_self(0, 0)
                    gat_q(0, 0, 0)
                    gat_q(0, 0, 1)
                    gat_k(0, 0)
                    gat_v(0, 0)
                if n == "att":
                    pe.wait_ge(at["w_lo"], 2)
                    att_qk(0, 0)
                    att_v(0, 0)

                def one(b, par):
                    if n == "s5" or n in MLPS:
                        if n == "s5":
                            s5_in_mm(b, par)
                            if before_end(b, 1):
                                transposes(n, b + 1, 1 - par)
                        else:
                            up(n, b, par)
                            if before_end(b, 2):
                                transposes(n, b + 2, par)
                        if n == "s5" and isinstance(b, int) and b == LAST:
                            setup23()
                        if n == "s5" and isinstance(b, int) and b == LAST + 1:
                            setup_vp()
                        if after(b, 1):
                            (s5_out_mm if n == "s5" else lambda *a: down(n, *a))(b - 1, 1 - par)
                    more = before_end(b, 1)
                    if n == "gat":
                        gat_scores(b, par, 0)
                        if after(b, 1):
                            gat_wT(b - 1, 1 - par, 0)
                        if more:
                            gat_zero_rows(b + 1, 1 - par)
                            gat_self(b + 1, 1 - par)
                        if after(b, 1):
                            gat_wT(b - 1, 1 - par, 1)
                        gat_scores(b, par, 1)
                        if after(b, 1):
                            gat_out(b - 1, 1 - par)
                        if before_end(b, 2):
                            transposes(n, b + 2, par)
                        if more:
                            gat_q(b + 1, 1 - par, 0)
                            gat_q(b + 1, 1 - par, 1)
                            gat_k(b + 1, 1 - par)
                        gat_open(b, par)
                        if more:
                            gat_v(b + 1, 1 - par)
                    if n == "att":
                        att_scores(b, par)
                        if before_end(b, 2):
                            transposes(n, b + 2, par)
                        if more:
                            att_qk(b + 1, 1 - par)
                        att_exT(b, par)
                        if more:
                            att_v(b + 1, 1 - par)
                        if after(b, 1):
                            att_out(b - 1, 1 - par)
                steps(pe, one)
                if n == "gat":
                    gat_wT(B - 1, (B - 1) % 2, 0)
                    gat_wT(B - 1, (B - 1) % 2, 1)
                if follow:
                    begin(follow)
                last = (B - 1) % 2
                if n == "s5":
                    s5_out_mm(B - 1, last)
                elif n in MLPS:
                    down(n, B - 1, last)
                elif n == "gat":
                    gat_out(B - 1, last)
                else:
                    att_out(B - 1, last)

            begin("s5")
            for n, follow in zip(ORDER, ORDER[1:] + [None]):
                phase(n, follow)

        @block.vector
        def _(dve):
            chain = [0]

            def link(ins):
                chain[0] += 1
                ins.then_inc(setup_step, 1)
                dve.wait_ge(setup_step, chain[0])

            def ts(out_, in_, s1, s2=None, op0=ALU.mult, op1=None):
                if op1 is None:
                    return dve.tensor_scalar(out_, in_, s1, None, op0)
                return dve.tensor_scalar(out_, in_, s1, s2, op0, op1)

            def stt(out_, in0, scalar, in1, op0, op1):
                return dve.scalar_tensor_tensor(out=out_, in0=in0, scalar=scalar, in1=in1, op0=op0, op1=op1)

            def c(i):
                return sc[:, i:i + 1]

            def s5_scalars():
                dve.wait_ge(L["small"], 16 * 5)
                dve.wait_ge(act_setup, 1)
                link(dve.tensor_tensor(c(1), col("Lam_re"), c(0), ALU.mult))
                link(dve.tensor_tensor(c(3), col("Lam_im"), c(0), ALU.mult))
                link(ts(c(12), c(3), float(1 / (2 * np.pi)), ROUND, ALU.mult, ALU.add))
                link(ts(c(4), c(12), -ROUND, None, ALU.add))
                link(stt(c(5), c(4), -TWO_PI_HI, c(3), ALU.mult, ALU.add))
                link(stt(c(6), c(4), -TWO_PI_MID, c(5), ALU.mult, ALU.add))
                link(stt(c(11), c(4), -TWO_PI_LO, c(6), ALU.mult, ALU.add))
                link(ts(c(7), c(11), PI, -PI, ALU.min, ALU.max))
                link(stt(c(12), c(7), -1.0, c(7), ALU.mult, ALU.max))
                link(ts(c(8), c(12), -1.0, HALF_PI, ALU.mult, ALU.add))

            def s5_setup():
                dve.wait_ge(act_setup, 4)
                link(dve.tensor_tensor(c(13), c(2), c(10), ALU.mult))
                link(ts(c(13), c(13), -1.0, None, ALU.add))
                link(dve.tensor_tensor(c(14), c(2), c(9), ALU.mult))
                re, im = col("Lam_re"), col("Lam_im")
                link(dve.tensor_tensor(c(15), re, re, ALU.mult))
                link(stt(c(16), im, im, c(15), ALU.mult, ALU.add))
                link(dve.reciprocal(c(17), c(16)))
                link(dve.tensor_tensor(c(18), c(13), re, ALU.mult))
                link(stt(c(19), c(14), im, c(18), ALU.mult, ALU.add))
                link(dve.tensor_tensor(c(20), c(19), c(17), ALU.mult))
                link(dve.tensor_tensor(c(21), c(13), im, ALU.mult))
                link(stt(c(22), c(14), re, c(21), ALU.mult, ALU.subtract))
                link(dve.tensor_tensor(c(23), c(22), c(17), ALU.mult))
                link(ts(c(24), c(23), sign[:, 0:1], -1.0, ALU.mult, ALU.mult))
                link(ts(c(25), c(20), sign[:, 0:1]))
                link(ts(c(26), sign[:, 0:1], 2.0))
                dve.wait_ge(L["s5"], 16)
                link(ts(s5_tmp[:, 0, :], s5_bc[:, 0, :], c(20)))
                link(ts(s5_tmp[:, 1, :], s5_bc[:, 0, :], c(23)))
                stt(s5_in[:, 0, :], s5_bc[:, 1, :], c(24), s5_tmp[:, 0, :], ALU.mult, ALU.add).then_inc(s5_in_ready, 1)
                stt(s5_in[:, 1, :], s5_bc[:, 1, :], c(25), s5_tmp[:, 1, :], ALU.mult, ALU.add).then_inc(s5_in_ready, 1)
                link(ts(s5_out[:, 0, :], s5_bc[:, 2, :], c(26)))
                link(ts(s5_out[:, 1, :], s5_bc[:, 3, :], -2.0))
                dve.wait_ge(consts_done, 2)
                for k in range(K):
                    link(ts(s5_diag[:, k, :], ident[:, :], col("D_diag", k)))
                link(dve.memset(decay[:, :], 1.0))
                link(ts(decay[:, :], decay[:, :], c(2)))
                link(dve.memset(cosT[:, 0:1], 1.0))
                link(dve.memset(sinT[:, 0:1], 0.0))
                ck, sk = c(10), c(9)
                n = 1
                while n < NTOK:
                    link(ts(rot[:, 0, 0:n], sinT[:, 0:n], sk))
                    link(ts(rot[:, 1, 0:n], cosT[:, 0:n], sk))
                    link(stt(cosT[:, n:2 * n], cosT[:, 0:n], ck, rot[:, 0, 0:n], ALU.mult, ALU.subtract))
                    link(stt(sinT[:, n:2 * n], sinT[:, 0:n], ck, rot[:, 1, 0:n], ALU.mult, ALU.add))
                    if 2 * n < NTOK:
                        i = 27 + 3 * (n.bit_length() % 2)
                        link(dve.tensor_tensor(c(i), sk, sk, ALU.mult))
                        link(stt(c(i + 1), ck, ck, c(i), ALU.mult, ALU.subtract))
                        link(stt(c(i + 2), sk, 2.0, ck, ALU.mult, ALU.mult))
                        ck, sk = c(i + 1), c(i + 2)
                    n *= 2
                dve.wait_ge(s5_inT_psum, 1)
                dve.tensor_copy(s5_inT[:, :, :, :].rearrange("p i k n -> p (i k n)"), PS[4][:, :])\
                   .then_inc(s5_ready, 1)

            def mods0():
                dve.wait_ge(mod0_psum, 1)
                a, m = COLS["mod"][0], mod
                link(dve.tensor_tensor(m[:, 0:NMOD0, :], PS[2][:, 0:NMOD0 * B].rearrange("p (j b) -> p j b", b=B),
                                       cols[:, a:a + NMOD0].unsqueeze(2).broadcast_to([P, NMOD0, B]), ALU.add))
                link(dve.tensor_tensor(gate_rows[:, 0:2, 0, :], PS[3][0:B, :].rearrange("b (g d) -> b g d", g=2),
                                       gate_bias[:, 0:2, :], ALU.add))
                link(dve.memset(gate_rows[:, 0, 1, :], 0.0))
                dve.tensor_tensor(gate_rows[:, 1, 1, :], gate_rows[:, 1, 0, :], out_bias[:, 0, :], ALU.mult)\
                   .then_inc(gates0_ready, 1)
                v = lambda name: mod[:, MOD[name]:MOD[name] + K, :]
                link(ts(one_ff[:, :, :], v("scale_ff"), 1.0, None, ALU.add))
                link(stt(MS[:, 1, :, :], v("scale_c"), 1.0, one_ff[:, :, :], ALU.add, ALU.mult))
                link(dve.tensor_tensor(MH[:, 1, :, :], v("shift_c"), one_ff[:, :, :], ALU.mult))
                link(dve.tensor_tensor(MH[:, 1, :, :], MH[:, 1, :, :], v("shift_ff"), ALU.add))
                link(dve.tensor_copy(MH[:, 0, :, :], v("shift_a")))
                ts(MS[:, 0, :, :], v("scale_a"), 1.0, None, ALU.add).then_inc(mod0_ready, 1)

            def silu():
                dve.wait_ge(silu_ready, 1)
                ts(sig[:, :, :], sig[:, :, :], 1.0, None, ALU.add).then_inc(silu_ready, 1)
                dve.wait_ge(silu_ready, 2)
                link(dve.reciprocal(sig[:, :, :], sig[:, :, :]))
                dve.tensor_tensor(cond_silu[:, :, :], cond[:, :, :], sig[:, :, :], ALU.mult).then_inc(silu_ready, 1)

            def mods23():
                dve.wait_ge(mod23_psum, 2)
                a, n23 = COLS["mod"][0] + NMOD0, NMOD2 + NMOD3
                link(dve.tensor_tensor(mod[:, NMOD0:, :], PS[4][:, 0:n23 * B].rearrange("p (j b) -> p j b", b=B),
                                       cols[:, a:a + n23].unsqueeze(2).broadcast_to([P, n23, B]), ALU.add))
                link(dve.tensor_copy(qpart[:, :, :],
                                     PS[4][:, n23 * B:(n23 + K) * B].rearrange("p (j b) -> p j b", b=B)))
                link(dve.tensor_tensor(gate_rows[:, 2:4, 0, :], PS[5][0:B, :].rearrange("b (g d) -> b g d", g=2),
                                       gate_bias[:, 2:4, :], ALU.add))
                dve.tensor_tensor(gate_rows[:, 2:4, 1, :], gate_rows[:, 2:4, 0, :], out_bias[:, 1:3, :], ALU.mult)\
                   .then_inc(gates2_ready, 1)
                v = lambda name: mod[:, MOD[name]:MOD[name] + K, :]
                for name, sc_, sh in (("ssm", "scale_msa", "shift_msa"), ("ff2", "scale_mlp", "shift_mlp")):
                    j = NORMED.index(name)
                    link(ts(MS[:, j, :, :], v(sc_), 1.0, None, ALU.add))
                    link(dve.tensor_copy(MH[:, j, :, :], v(sh)))
                for name, w, sc_, sh in (("att", "norm1_w", "film1_scale", "film1_shift"),
                                         ("ff3", "norm2_w", "film2_scale", "film2_shift")):
                    j, a = NORMED.index(name), COLS[w][0]
                    link(stt(MS[:, j, :, :], v(sc_), 1.0, cols[:, a:a + K].unsqueeze(2).broadcast_to([P, K, B]),
                             ALU.add, ALU.mult))
                    link(dve.tensor_copy(MH[:, j, :, :], v(sh)))
                link(dve.tensor_tensor(bout[:, :], row("bout0"), row("bout1"), ALU.add))

            def vp_weights():
                dve.wait_ge(ws_psum, 1)
                dve.tensor_copy(w_vp[:, :, :], PS[4][:, :].rearrange("p (k n) -> p k n", k=K)).then_inc(ws_ready, 1)
                dve.tensor_tensor(att_row[:, :], PS[5][:, 0:D], row("proj_b"), ALU.add).then_inc(ws_ready, 1)

            def statistics(n, b, par):
                s, (kind, eps) = S[n], NORMS[n]
                wait_x(dve, n, b)
                for t in range(T):
                    dve.bn_stats(stats[:, par, t, :], X[:, bass.ds(b * 2 + t, 1), :].rearrange("p o d -> p (o d)"))\
                       .then_inc(stats_done, 1)
                dve.wait_ge(stats_done, T * (nth(n, b) + 1))
                mean_e, m2_e, mean_o, m2_o = (stats[:, par, :, i] for i in (1, 2, 4, 5))
                mean, m2, dif, dif2, mean2, sq = (mv[:, par, i, :] for i in range(6))
                dve.tensor_tensor(dif, mean_e, mean_o, ALU.subtract).then_inc(aggr_done, 1)
                stt(m2, m2_e, D * eps, m2_o, ALU.add, ALU.add).then_inc(aggr_done, 1)
                dve.tensor_tensor(mean2, mean_e, mean_o, ALU.add).then_inc(aggr_done, 1)
                dve.wait_ge(aggr_done, 5 * nth(n, b) + 3)
                stt(dif2, dif, 0.25, dif, ALU.mult, ALU.mult).then_inc(aggr_done, 1)
                if kind == "rms":
                    stt(sq, mean2, 0.25, mean2, ALU.mult, ALU.mult).then_inc(aggr_done, 1)
                    dve.wait_ge(aggr_done, 5 * nth(n, b) + 5)
                    dve.tensor_tensor(msq[:, par, :], dif2, sq, ALU.add).then_inc(s["msq_done"], 1)
                    dve.wait_ge(s["msq_done"], b + 1)
                    stt(var_eps[:, par, :], m2, 1 / D, msq[:, par, :], ALU.mult, ALU.add).then_inc(var_ready, 1)
                else:
                    ts(mean, mean2, 0.5).then_inc(aggr_done, 1)
                    dve.wait_ge(aggr_done, 5 * nth(n, b) + 5)
                    stt(var_eps[:, par, :], m2, 1 / D, dif2, ALU.mult, ALU.add).then_inc(var_ready, 1)

            def normalise(n, b, par):
                s, kind = S[n], NORMS[n][0]
                dve.wait_ge(rstd_ready, nth(n, b) + 1)
                if after(b, 2):
                    dve.wait_ge(s["xT_psum"], b - 1)
                for t in range(T):
                    xb = X[:, bass.ds(b * 2 + t, 1), :].rearrange("p o d -> p (o d)")
                    r = rstd[:, par, t:t + 1]
                    if kind == "rms":
                        ins = ts(xn[:, par, t, :], xb, r)
                    else:
                        ins = ts(xn[:, par, t, :], xb, mv[:, par, 0, t:t + 1], r, ALU.subtract, ALU.mult)
                    ins.then_inc(xn_ready, 1)

            def modulate(n, b, par):
                s, j = S[n], NORMED.index(n)
                dve.wait_ge(s["xT_psum"], b + 1)
                if after(b, 2):
                    if n in MLPS:
                        dve.wait_ge(s["hid_psum"], (b - 1) * BANKS[n])
                    else:
                        dve.wait_ge(at["v_psum"], b - 1)
                for k in range(K):
                    ts(hT[:, par, k, :], PS[par][:, k * NTOK:(k + 1) * NTOK], MS[:, j, k, bass.ds(b, 1)],
                       MH[:, j, k, bass.ds(b, 1)], ALU.mult, ALU.add).then_inc(s["hT_ready"], 1)

            def gate(n, b, par):
                s = S[n]
                dve.wait_ge(s["out_psum"], b + 1)
                if n in GATES:
                    dve.wait_ge(gate_loaded[par], loads(b, par) + 8 * B * GATES.index(n))
                o = PS[6 + par][:, :].rearrange("p (t d) -> p t d", t=T)
                if n == "ff3":
                    dve.tensor_tensor(upd[:, par, :, :], o, row("mlp_b2").unsqueeze(1).broadcast_to([P, T, D]),
                                      ALU.add).then_inc(s["out_read"], 1)
                else:
                    dve.tensor_tensor(upd[:, par, :, :], o, gates[:, par, 0:1, :].broadcast_to([P, T, D]),
                                      ALU.mult).then_inc(s["out_read"], 1)

            def add_upd(n, b, par):
                xb = X[:, bass.ds(b * 2, 2), :]
                dve.wait_ge(S[n]["upd_ready"], b + 1)
                dve.tensor_tensor(xb, xb, upd[:, par, :, :], ALU.add).then_inc(S[n]["x_ready"], 1)

            def s5_rotate(b, par):
                dve.wait_ge(s5["bu_psum"], b + 1)
                if after(b, 2):
                    dve.wait_ge(s5["rot_ready"], b - 1)
                for i, table in enumerate((cosT, sinT)):
                    dve.tensor_tensor(bu[:, par, i, :], PS[2 + par][:, i * NTOK:(i + 1) * NTOK], table[:, :],
                                      ALU.mult).then_inc(s5["bu_ready"], 1)

            def s5_scan(b, par):
                dve.wait_ge(s5["rot_ready"], b + 1)
                if after(b, 2):
                    dve.wait_ge(s5["zc_ready"], b - 1)
                    dve.wait_ge(S["s5"]["out_psum"], b - 1)
                dve.tensor_tensor_scan(zst[:, par, :], decay[:, :], wrot[:, par, :], 0.0, ALU.mult, ALU.add)\
                   .then_inc(s5["scan_ready"], 1)
                dve.wait_ge(s5["scan_ready"], b + 1)
                dve.tensor_tensor(zs[:, par, :], zst[:, par, :], sinT[:, :], ALU.mult).then_inc(s5["zs_ready"], 1)

            def gat_nz(b, par):
                dve.wait_ge(ga["xs_ready"], T * (b + 1))
                if after(b, 2):
                    dve.wait_ge(ga["nz_psum"], b - 1)
                ts(nz[:, par, :], rsum[:, par, :], 0.0, None, ALU.not_equal).then_inc(ga["nz_ready"], 1)

            def gat_labels(b, par):
                dve.wait_ge(adj_loaded[par], loads(b, par))
                wb = row("w_bias").unsqueeze(1).broadcast_to([P, 4 * NONGT, LABELS])
                dve.tensor_tensor(adj_w, adj[par], wb, ALU.mult).then_inc(ga["adj_w"], 1)
                dve.tensor_reduce(cnt, adj[par], AX.X, ALU.add).then_inc(ga["adj_used"], 1)
                dve.wait_ge(ga["adj_w"], b + 1)
                dve.tensor_reduce(lab, adj_w, AX.X, ALU.add).then_inc(ga["lab"], 1)
                dve.wait_ge(ga["adj_used"], b + 1)
                ts(pen, cnt, 0.0, NEG, ALU.is_le, ALU.mult).then_inc(ga["pen"], 1)
                dve.wait_ge(ga["lab"], b + 1)
                dve.wait_ge(ga["pen"], b + 1)
                stt(cbias[par].rearrange("p d t m -> p (d t m)"), lab, row("b_bias"), pen, ALU.add, ALU.add)\
                    .then_inc(ga["cb"], 1)

            def gat_sfT(b, par):
                dve.wait_ge(ga["sfA_ready"], K * (b + 1))
                dve.wait_ge(ga["nz_psum"], b + 1)
                if after(b, 2):
                    dve.wait_ge(ga["sf_used"], b - 1)
                for k in range(K):
                    stt(sfT[par][:, k, :], PS[1][:, 0:NTOK], qpart[:, k, bass.ds(b, 1)], sfA[:, k, :],
                        ALU.mult, ALU.add).then_inc(ga["sfT_ready"], 1)
                dve.wait_ge(ga["sfT_ready"], K * (b + 1))
                if after(b, 1):
                    dve.wait_ge(ga["v_psum"], b)
                dve.tensor_copy(kvrep, sfT[par][:, :, 0:NONGT].unsqueeze(2).broadcast_to([P, K, HPC, NONGT]))\
                   .then_inc(ga["kvrep_ready"], 1)

            def gat_KB(b, par):
                dve.wait_ge(ga["k_psum"], b + 1)
                if after(b, 2):
                    dve.wait_ge(ga["s_psum"], T * (b - 1))
                for g in range(4):
                    stt(KB[par][:, g, :, :],
                        PS[1][:, 256 + g * NONGT:256 + (g + 1) * NONGT].unsqueeze(1).broadcast_to([P, HPK, NONGT]),
                        col("bk", g), head_mask[:, :, :], ALU.add, ALU.mult).then_inc(ga["KB_ready"], 1)

            def gat_VB(b, par):
                dve.wait_ge(ga["v_psum"], b + 1)
                if after(b, 2):
                    dve.wait_ge(S["gat"]["out_psum"], b - 1)
                M = HPC * NONGT
                dve.tensor_tensor(VB[par].rearrange("p d (c n) -> p (d c) n", c=CH),
                                  PS[3][0:M, :].rearrange("p (g n) -> p g n", n=HPC * DH),
                                  v_mask[:, :, :].rearrange("p h e -> p (h e)").unsqueeze(1)
                                  .broadcast_to([M, 2 * CH, HPC * DH]), ALU.mult).then_inc(ga["VB_ready"], 1)

            def gat_bias(b, par, t):
                dve.wait_ge(ga["s_psum"], T * b + (t + 1))
                dve.wait_ge(ga["cb"], b + 1)
                if after(b, 1):
                    dve.wait_ge(ga["exp_done"], T * (b - 1) + (t + 1))
                for d in range(2):
                    ins = dve.tensor_tensor(
                        sco[t][:, d * HEADS:(d + 1) * HEADS, :],
                        PS[4 + d][:, 0:HEADS * NONGT].rearrange("p (h m) -> p h m", m=NONGT),
                        cbias[par][:, d, t, :].unsqueeze(1).broadcast_to([P, HEADS, NONGT]), ALU.add)
                ins.then_inc(ga["s_biased"], 1)
                dve.wait_ge(ga["s_biased"], T * b + (t + 1))
                dve.tensor_reduce(smax[t], sco[t], AX.X, ALU.max).then_inc(ga["smax_done"], 1)

            def gat_sum(b, par, t):
                dve.wait_ge(ga["exp_done"], T * b + (t + 1))
                dve.tensor_reduce(ssum[t], prb[t], AX.X, ALU.add).then_inc(ga["ssum_done"], 1)
                dve.wait_ge(ga["ssum_done"], T * b + (t + 1))
                dve.reciprocal(srec[t], ssum[t]).then_inc(ga["srec_done"], 1)

            def gat_residual(b, par):
                dve.wait_ge(S["gat"]["out_psum"], b + 1)
                o = PS[6][:, :].rearrange("p (t d) -> p t d", t=T)
                dve.tensor_tensor(upd[:, par, :, :], o, bout[:, :].unsqueeze(1).broadcast_to([P, T, D]), ALU.add)\
                   .then_inc(S["gat"]["out_read"], 1)
                dve.wait_ge(S["gat"]["out_read"], b + 1)
                xb = X[:, bass.ds(b * 2, 2), :]
                stt(xb, upd[:, par, :, :], 0.0, xb, ALU.max, ALU.add).then_inc(S["gat"]["x_ready"], 1)

            def att_max(b, par):
                dve.wait_ge(at["s_psum"], b + 1)
                dve.tensor_reduce(amax[:, par, :], PS[4][:, :].rearrange("p (t m) -> p t m", t=T), AX.X, ALU.max)\
                   .then_inc(at["amax_done"], 1)
                dve.wait_ge(at["amax_done"], b + 1)
                if after(b, 2):
                    dve.wait_ge(at["exp_done"], T * (b - 1))
                ts(nmax[:, par, :], amax[:, par, :], -(D ** -0.5)).then_inc(at["nmax_done"], 1)

            def att_v(b, par):
                dve.wait_ge(at["v_psum"], b + 1)
                if after(b, 2):
                    dve.wait_ge(at["v_lo"], b - 1)
                dve.tensor_copy(vp[:, par, :, :].rearrange("p t d -> p (t d)"), PS[5][:, :]).then_inc(at["v_ready"], 1)

            def att_exT(b, par):
                dve.wait_ge(at["exT_psum"], b + 1)
                if after(b, 2):
                    dve.wait_ge(at["exT_lo"], b - 1)
                dve.tensor_copy(exT[:, par, :, :].rearrange("p m n -> p (m n)"), PS[7][:, :])\
                   .then_inc(at["exT_ready"], 1)
                dve.wait_ge(at["exp_done"], T * (b + 1))
                if after(b, 2):
                    dve.wait_ge(S["att"]["out_read"], b - 1)
                dve.reciprocal(arec[:, par, :], asum[:, par, :]).then_inc(at["arec_done"], 1)

            def att_residual(b, par):
                xb = X[:, bass.ds(b * 2, 2), :]
                dve.tensor_tensor(xb, xb, att_row[:, :].unsqueeze(1).broadcast_to([P, T, D]), ALU.add)\
                   .then_inc(at["row_added"], 1)
                dve.wait_ge(S["att"]["out_psum"], b + 1)
                dve.wait_ge(at["arec_done"], b + 1)
                dve.wait_ge(at["row_added"], b + 1)
                for t in range(T):
                    xt = X[:, bass.ds(b * 2 + t, 1), :].rearrange("p o d -> p (o d)")
                    ins = stt(xt, PS[6][:, t * D:(t + 1) * D], arec[:, par, t:t + 1], xt, ALU.mult, ALU.add)
                ins.then_inc(S["att"]["out_read"], 1)

            def begin(n):
                if n in NORMS:
                    for b in range(2):
                        statistics(n, b, b)
                        normalise(n, b, b)
                    if n != "s5":
                        modulate(n, 0, 0)
                    if n in SPLIT:
                        modulate(n, 1, 1)
                        statistics(n, 2, 0)
                        normalise(n, 2, 0)
                        statistics(n, 3, 1)
                if n == "gat":
                    gat_nz(0, 0)
                    gat_nz(1, 1)

            def phase(n, follow):
                if n == "gat":
                    gat_labels(0, 0)
                    gat_sfT(0, 0)
                    gat_KB(0, 0)
                    gat_VB(0, 0)
                    gat_nz(2, 0)
                if n == "att":
                    att_v(0, 0)

                def one(b, par):
                    more = before_end(b, 1)
                    if n == "att":
                        att_max(b, par)
                        if after(b, 2):
                            att_residual(b - 2, par)
                    if n == "s5" and before_end(b, 2):
                        statistics(n, b + 2, par)
                    if n in ("s5", *MLPS) and after(b, 2):
                        add_upd(n, b - 2, par)
                    if n == "s5":
                        s5_rotate(b, par)
                    if n in SPLIT and before_end(b, 2):
                        modulate(n, b + 2, par)
                    if n == "ff2":
                        hidden_lo(dve, n, b, par)
                    if n == "att":
                        att_exT(b, par)
                        if more:
                            att_v(b + 1, 1 - par)
                    if n in NORMS and before_end(b, AHEAD[n]):
                        normalise(n, b + AHEAD[n], (par + AHEAD[n]) % 2)
                    if n == "s5":
                        s5_scan(b, par)
                        if isinstance(b, int) and b == LAST:
                            mods23()
                        if isinstance(b, int) and b == LAST + 1:
                            vp_weights()
                    if n in ("s5", *MLPS) and after(b, 1):
                        gate(n, b - 1, 1 - par)
                    if n == "gat":
                        gat_bias(b, par, 0)
                        if more:
                            gat_sfT(b + 1, 1 - par)
                        gat_bias(b, par, 1)
                        gat_sum(b, par, 0)
                        if after(b, 1):
                            gat_residual(b - 1, 1 - par)
                        if more:
                            gat_labels(b + 1, 1 - par)
                        gat_sum(b, par, 1)
                        if more:
                            gat_KB(b + 1, 1 - par)
                            gat_VB(b + 1, 1 - par)
                        if before_end(b, 3):
                            gat_nz(b + 3, 1 - par)
                    if n in SPLIT and before_end(b, 4):
                        statistics(n, b + 4, par)
                steps(dve, one)
                if n == "att":
                    att_residual(B - 2, B % 2)
                if follow:
                    begin(follow)
                last = (B - 1) % 2
                if n in ("s5", *MLPS):
                    add_upd(n, B - 2, 1 - last)
                    gate(n, B - 1, last)
                    add_upd(n, B - 1, last)
                elif n == "gat":
                    gat_residual(B - 1, last)
                else:
                    att_residual(B - 1, last)

            s5_scalars()
            link(dve.memset(sign[0:STATES, :], 1.0))
            link(dve.memset(sign[STATES:P, :], -1.0))
            s5_setup()
            mods0()
            begin("s5")
            silu()
            for n, follow in zip(ORDER, ORDER[1:] + [None]):
                phase(n, follow)


_OUT = ((B, NTOK, D), "float32")


def lay_out(inputs):
    g = {k: np.asarray(v) for k, v in inputs.items()}

    def tiles(w):
        return np.ascontiguousarray(w.reshape(-1, P, w.shape[1]).transpose(1, 0, 2))

    def column(v):
        return v.reshape(-1, P).T

    x = g["x"]
    cond = g["cond_1024"]
    a = {"x": x, "cond": np.ascontiguousarray(cond.T.reshape(K, P, B).transpose(1, 0, 2))}
    a["wmod0"] = tiles(np.concatenate([g["L0_cond_Wm"], g["L0_cond_Wc"]], 1))
    a["wmod23"] = tiles(np.concatenate([g["L2_cond_ada_w"], g["L3_cond_film1_w"], g["L3_cond_film2_w"]], 1))
    mod_bias = np.concatenate([g["L0_cond_bm"], g["L0_cond_bc"], g["L2_cond_ada_b"], g["L3_cond_film1_b"],
                               g["L3_cond_film2_b"]])
    two = lambda v: np.concatenate([v, v])
    parts = {
        "mod": column(mod_bias), "ff0_b1": column(g["L0_cond_b1"]), "ssm_b1": column(g["L2_cond_ssm_b1"]),
        "ff2_b1": column(g["L2_cond_ff_b1"]), "ff3_b1": column(g["L3_cond_mlp_b1"]),
        "b_self": column(g["L1_cond_b_self"]), "bq": column(g["L1_cond_bq"].reshape(-1)),
        "bk": column(g["L1_cond_bk"].reshape(-1)), "q_b": column(g["L3_cond_q_b"]), "k_b": column(g["L3_cond_k_b"]),
        "norm1_w": column(g["L3_cond_norm1_w"]), "norm2_w": column(g["L3_cond_norm2_w"]),
        "D_diag": column(g["L0_cond_D_diag"]), "Lam_re": column(two(g["L0_cond_Lam_re"])),
        "Lam_im": column(two(g["L0_cond_Lam_im"])), "log_step": column(two(g["L0_cond_log_step"])),
        "v_b": column(g["L3_cond_v_b"]),
    }
    a["cols"] = np.ascontiguousarray(np.concatenate([parts[n] for n in COLS], 1))
    bout = g["L1_cond_bout"].reshape(2, D)
    a["rows"] = np.concatenate([bout[0], bout[1], g["L3_cond_proj_b"], g["L3_cond_mlp_b2"], g["L1_cond_w_bias"],
                                g["L1_cond_b_bias"].reshape(1)])
    bias = {n: mod_bias[MOD[n] * P:MOD[n] * P + D] for n in ("gate_a", "gate_ff", "gate_msa", "gate_mlp")}
    a["gate_bias"] = np.concatenate(list(bias.values()))
    a["out_bias"] = np.concatenate([g["L0_cond_b2"], g["L2_cond_ssm_b2"], g["L2_cond_ff_b2"]])
    br, bi, cr, ci = g["L0_cond_B_re"], g["L0_cond_B_im"], g["L0_cond_C_re"].T, g["L0_cond_C_im"].T
    a["s5_bc"] = np.ascontiguousarray(np.stack([np.concatenate(v) for v in ((br, bi), (bi, br), (cr, ci), (ci, cr))], 1))
    w = np.concatenate([tiles(g[n]).reshape(P, -1) for n in (
        "L0_cond_W1", "L0_cond_W2", "L2_cond_ssm_w1", "L2_cond_ssm_w2", "L2_cond_ff_w1", "L2_cond_ff_w2",
        "L3_cond_mlp_w1", "L3_cond_mlp_w2")], 1).reshape(P, -1, PIECE)
    before = PIECES["ff2"]
    order = list(range(before)) + [before + i for i in PIECE_AT[before:]]
    a["w_mlp"] = np.ascontiguousarray(w[:, order]).reshape(P, -1)
    w_self = g["L1_cond_W_self"].T
    wo = g["L1_cond_Wout"].reshape(2, D, D)
    a["w_gat"] = tiles(np.concatenate([w_self[:D], *(w.T for w in g["L1_cond_Wq"]), *(w.T for w in g["L1_cond_Wk"]),
                                       *(w.T for w in wo)], 1))
    a["w_qpart"] = tiles(w_self[D:])
    a["w_att"] = tiles(np.concatenate([g["L3_cond_q_w"], g["L3_cond_k_w"], g["L3_cond_v_w"].T, g["L3_cond_proj_w"]], 1))
    m = g["mask_BxSxSx11_ik0"]
    d0 = m[:, :, :NONGT].reshape(B, T, P, NONGT, LABELS)
    d1 = m[:, :NONGT].transpose(0, 2, 1, 3).reshape(B, T, P, NONGT, LABELS)
    a["adj"] = np.ascontiguousarray(np.stack([d0, d1], 1).transpose(0, 3, 1, 2, 4, 5)).reshape(B, P, -1)
    return a


def kernel(**inputs):
    import concourse.bacc as _bacc
    from concourse.bass_utils import run_bass_kernel_spmd as _run

    nc = _bacc.Bacc("TRN2", target_bir_lowering=False, num_devices=1)
    laid = lay_out(inputs)
    arrays, aps = {}, {}
    for name, a in laid.items():
        arrays[f"in_{name}"] = a
        aps[name] = nc.dram_tensor(f"in_{name}", a.shape, mybir.dt.from_np(a.dtype), kind="ExternalInput").ap()
    out = nc.dram_tensor("out_0", _OUT[0], F32, kind="ExternalOutput").ap()
    build_program(nc, aps, out)
    r = _run(nc, [arrays], core_ids=[0])
    return r.results[0]["out_0"]
```

```python
from contextlib import ExitStack

import numpy as np

import concourse.bass as bass
from concourse import mybir

ALU = mybir.AluOpType
ACT = mybir.ActivationFunctionType
AX = mybir.AxisListType
F32 = mybir.dt.float32
F32R = mybir.dt.float32r
BF16 = mybir.dt.bfloat16
I32 = mybir.dt.int32

P = 128
B = 16
NTOK = 256
T = NTOK // P
D = 256
K = D // P
STATES = 64
HEADS, DH, NONGT, LABELS = 16, 16, 20, 11
HPC = 6
CHUNKS = [(0, 0, 6), (6, 6, 12), (10, 12, 16)]
HPK = P // DH
NEG = -9000000000000000.0
PI = 3.1415925
HALF_PI = float(np.pi / 2)
ROUND = 1.5 * 2 ** 23
TWO_PI_HI = 6.28125
TWO_PI_MID = 1.9340515e-3
TWO_PI_LO = float(2 * np.pi - 6.28125 - np.float64(np.float32(1.9340515e-3)))

MOD0 = ["shift_a", "scale_a", "gate_a", "shift_ff", "scale_ff", "gate_ff", "scale_c", "shift_c"]
MOD2 = ["shift_msa", "scale_msa", "gate_msa", "shift_mlp", "scale_mlp", "gate_mlp"]
MOD3 = ["film1_scale", "film1_shift", "film2_scale", "film2_shift"]
MOD = {name: K * n for n, name in enumerate(MOD0 + MOD2 + MOD3)}
NMOD = K * len(MOD)
NMOD0, NMOD2, NMOD3 = K * len(MOD0), K * len(MOD2), K * len(MOD3)

COLS = {}
for _name, _n in [("mod", NMOD), ("ff0_b1", 8), ("ssm_b1", 2), ("ff2_b1", 4), ("ff3_b1", 8), ("b_self", 2),
                  ("bq", 4), ("bk", 4), ("q_b", 2), ("k_b", 2), ("norm1_w", 2), ("norm2_w", 2), ("D_diag", 2),
                  ("Lam_re", 1), ("Lam_im", 1), ("log_step", 1), ("v_b", 2)]:
    COLS[_name] = sum(n for _, n in COLS.values()), _n
NCOLS = sum(n for _, n in COLS.values())
ROWS = {}
for _name, _n in [("bout0", D), ("bout1", D), ("proj_b", D), ("mlp_b2", D), ("w_bias", LABELS), ("b_bias", 1),
                  ("ssm_b2", D)]:
    ROWS[_name] = sum(n for _, n in ROWS.values()), _n
NROWS = sum(n for _, n in ROWS.values())
BIASED = ["ff0", "ff2"]
GATES = ["s5", "ff0", "ssm", "ff2"]

MLPS = {
    "ff0": (1024, ACT.Gelu_apprx_tanh, "layer", 1e-5),
    "ssm": (256, ACT.Gelu, "layer", 1e-6),
    "ff2": (512, ACT.Gelu_apprx_tanh, "layer", 1e-6),
    "ff3": (1024, ACT.Gelu, "rms", 1e-6),
}
BANKS = {n: v[0] // P // 2 for n, v in MLPS.items()}
PIECE = 1024
WEIGHT_AT = {"ff0": 0, "ssm": 3 * PIECE, "ff2": PIECE, "ff3": 0}
PIECES = {"ff0": 4, "ssm": 5, "ff2": 7, "ff3": 11}
PIECE_AT = [0, 1, 2, 3, 3, 1, 2, 1, 2, 0, 3]
GAT_SQ_AT, GAT_OUT_AT = 0, 2 * PIECE
ATT_QK_AT, ATT_V_AT = 0, 3 * PIECE
NORMS = {"s5": ("layer", 1e-5), "att": ("rms", 1e-6), **{n: v[2:] for n, v in MLPS.items()}}
ORDER = ["s5", "ff0", "gat", "ssm", "ff2", "att", "ff3"]
NORMED = [n for n in ORDER if n in NORMS]

FIRST, TURNS = 3, 4
LAST = FIRST + 2 * TURNS
AHEAD = {n: 2 if n == "s5" else 3 for n in NORMS}
SPLIT = [n for n in ORDER if n in MLPS or n == "att"]
JOINED = {m: n for n, m in zip(ORDER, ORDER[1:]) if n in SPLIT and m in SPLIT}


EARLY_STATS = {B - 3: 0, B - 2: 1, B - 1: 2}
EARLY_NORMS = {B - 2: 0, B - 1: 1}


def early(table, n, follow, b):
    return table.get(b) if isinstance(b, int) and n in ("s5", "gat") and follow in SPLIT else None


def ahead(n, b, lead):
    if not isinstance(b, int) or b + lead < B:
        return n, b + lead
    follow = [m for m, before in JOINED.items() if before == n]
    return (follow[0], b + lead - B) if follow else None


def build_program(nc, A, out):
    with ExitStack() as ctx:
        def sb(name, shape, dt=F32):
            return ctx.enter_context(nc.sbuf_tensor(name, shape, dt))

        def sem(name):
            return ctx.enter_context(nc.semaphore(name))

        PS = [ctx.enter_context(nc.psum_tensor(f"bank{i}", [P, 512], F32)) for i in range(8)]

        X = sb("X", [P, B * T, D])
        cond = sb("cond", [P, K, B])
        cond_silu = sb("cond_silu", [P, K, B])
        sig = sb("sig", [P, K, B])
        cols = sb("cols", [P, NCOLS])
        rows = sb("rows", [P, NROWS])
        mod = sb("mod", [P, NMOD, B])
        MS = sb("MS", [P, len(NORMED), K, B])
        MH = sb("MH", [P, len(NORMED), K, B])
        one_ff = sb("one_ff", [P, K, B])
        ident = sb("ident", [P, P])
        ident_b = sb("ident_b", [P, P], BF16)
        half_neg = sb("half_neg", [P, T])
        ones = sb("ones", [1, P])
        s5_inT = sb("s5_inT", [P, 2, K, P])
        s5_out = sb("s5_out", [P, 2, D])
        s5_diag = sb("s5_diag", [P, K, P])
        cosT = sb("cosT", [P, NTOK])
        sinT = sb("sinT", [P, NTOK])
        decay = sb("decay", [P, NTOK])
        rot = sb("rot", [P, 2, P])
        sc = sb("sc", [P, 40])
        sign = sb("sign", [P, 1])

        w_raw = sb("w_raw", [P, 2, PIECE])
        w_gat = sb("w_gat", [P, K, 7 * D])
        w_qpart = sb("w_qpart", [P, K, D])
        qpart = sb("qpart", [P, K, B])
        w_att = sb("w_att", [P, K, 4 * D])
        w_vp = sb("w_vp", [P, K, D])
        att_row = sb("att_row", [P, D])
        bout = sb("bout", [P, D])

        stats = sb("stats", [P, 2, T, 6])
        mv = sb("mv", [P, 2, 6, T])
        msq = sb("msq", [P, 2, T])
        var_eps = sb("var_eps", [P, 2, T])
        rstd = sb("rstd", [P, 2, T])
        xn = sb("xn", [P, 2, T, D])
        hT = sb("hT", [P, 2, K, NTOK])
        gT = sb("gT", [P, 2, 8, NTOK])
        upd = sb("upd", [P, 2, T, D])
        gates = sb("gates", [P, 2, 2, D])
        exT = sb("exT", [P, 2, T, NTOK])

        s5_bc = upd[:, :, :, :].rearrange("p a t d -> p (a t) d")
        s5_in = exT[:, 0, :, :]
        s5_tmp = exT[:, 1, :, :]

        NW = 2 * K * MLPS["ff0"][0]
        G_COLS, H_COLS = 2 * 8 * NTOK, 2 * K * NTOK
        rooms = (nc.sbuf_usable_end - 8 * (NW + G_COLS + H_COLS)) // 64 * 64
        top = [rooms]

        def place(name, shape, dt, at):
            return nc.alloc_sbuf_tensor_at(name, shape, dt, offset=at)

        def new_room(n):
            top[0] += 4 * n
            return top[0] - 4 * n

        weight_room, split_room, input_room = new_room(2 * NW), new_room(2 * G_COLS), new_room(2 * H_COLS)
        wmod0 = place("wmod0", [P, K, NMOD0 * P], F32, weight_room)
        w_hi = place("w_hi", [P, NW], F32R, weight_room)
        w_lo = place("w_lo", [P, NW], F32R, weight_room + 4 * NW)
        mod_rows = place("mod_rows", [B, NMOD0 * P], F32, weight_room + 4 * (2 * NW - NMOD0 * P))
        g_hi = place("g_hi", [P, 2, 8, NTOK], F32R, split_room)
        g_lo = place("g_lo", [P, 2, 8, NTOK], F32R, split_room + 4 * G_COLS)
        wmod23 = place("wmod23", [P, K, (NMOD2 + NMOD3) * P], F32, split_room)
        bias_at = split_room + 4 * K * (NMOD2 + NMOD3) * P
        gate_bias = place("gate_bias", [B, 4, D], F32, bias_at)
        out_bias = place("out_bias", [B, 3, D], F32, bias_at + 4 * 4 * D)
        assert bias_at + 4 * 7 * D <= input_room
        arena = place("arena", [P, 2 * G_COLS], F32, split_room)
        h_hi = place("h_hi", [P, 2, K, NTOK], F32R, input_room)
        h_lo = place("h_lo", [P, 2, K, NTOK], F32R, input_room + 4 * H_COLS)
        gate_rows = place("gate_rows", [B, 4, 2, D], F32, input_room)

        def w1(part, n, k, m):
            a = WEIGHT_AT[n] + k * MLPS[n][0] + m * P
            return part[:, a:a + P]

        def w2(part, n, m):
            a = WEIGHT_AT[n] + K * MLPS[n][0] + m * D
            return part[:, a:a + D]

        bu = gT[:, :, 0:2, :]
        wrot = gT[:, :, 2, :]
        zst = gT[:, :, 3, :]
        zc = gT[:, :, 4, :]
        zs = gT[:, :, 5, :]

        room = [0]

        def carve(n):
            room[0] += n
            assert room[0] <= 2 * G_COLS
            return arena[:, room[0] - n:room[0]]

        adj = [sb(f"adj{i}", [P, 4 * NONGT, LABELS], I32)[:, :, :] for i in range(2)]
        rsum = sb("rsum", [P, 2, T])
        adj_w = carve(4 * NONGT * LABELS).rearrange("p (g l) -> p g l", l=LABELS)
        cnt = carve(4 * NONGT)
        pen = carve(4 * NONGT)
        lab = carve(4 * NONGT)
        cbias = [carve(4 * NONGT).rearrange("p (d t m) -> p d t m", d=2, t=T) for _ in range(2)]
        sfA = carve(K * NTOK).rearrange("p (k n) -> p k n", k=K)
        sfT = [exT[:, i, :, :] for i in range(2)]
        KB = [carve(4 * HPK * NONGT).rearrange("p (g h m) -> p g h m", g=4, h=HPK) for _ in range(2)]
        VB = [carve(2 * D)[0:HPC * NONGT, :].rearrange("p (d n) -> p d n", d=2) for _ in range(2)]
        sco = [carve(2 * HEADS * NONGT).rearrange("p (g m) -> p g m", m=NONGT) for _ in range(T)]
        prb = [carve(2 * HEADS * NONGT).rearrange("p (g m) -> p g m", m=NONGT) for _ in range(T)]
        smax = [sb(f"smax{t}", [P, 2 * HEADS])[:, :] for t in range(T)]
        ssum = [sb(f"ssum{t}", [P, 2 * HEADS])[:, :] for t in range(T)]
        srec = [sb(f"srec{t}", [P, 2 * HEADS])[:, :] for t in range(T)]
        sf_at, KV = split_room + 4 * room[0], K * HPC * NONGT
        assert room[0] + 2 * (K * NTOK + KV) <= 2 * G_COLS
        sf_hi = place("sf_hi", [P, K, NTOK], F32R, sf_at)
        sf_lo = place("sf_lo", [P, K, NTOK], F32R, sf_at + 4 * K * NTOK)
        kv_hi = place("kv_hi", [P, K, HPC, NONGT], F32R, sf_at + 8 * K * NTOK)
        kv_lo = place("kv_lo", [P, K, HPC, NONGT], F32R, sf_at + 8 * K * NTOK + 4 * KV)
        QT = [gT[:, i, 0:4, :].rearrange("p (d k) n -> p d k n", d=2) for i in range(2)]
        wT = gT[:, :, 4:8, :].rearrange("p a (c2 c) n -> p a c2 (c n)", c2=2)
        nz = sb("nz", [P, 2, T], BF16)
        head_mask = sb("head_mask", [P, HPK, NONGT])
        v_mask = sb("v_mask", [HPC * NONGT, HPC, DH])

        qT = gT[:, :, 0:2, :]
        kT = gT[:, :, 2:4, :]
        vp = gT[:, :, 4:6, :]
        ex = gT[:, :, 6:8, :]
        Q, KK, V, E = (slice(2 * i, 2 * i + 2) for i in range(4))
        amax = sb("amax", [P, 2, T])
        nmax = sb("nmax", [P, 2, T])
        asum = sb("asum", [P, 2, T])
        arec = sb("arec", [P, 2, T])

        assert nc.sbuf_base <= rooms

        gate_dram = nc.dram_tensor("gate_dram", (B, len(GATES) * 2 * D), F32, kind="Internal").ap()

        def col(name, n=0):
            return cols[:, COLS[name][0] + n:COLS[name][0] + n + 1]

        def row(name):
            return rows[:, ROWS[name][0]:ROWS[name][0] + ROWS[name][1]]

        L = {n: sem(f"loaded_{n}") for n in ("small", "x0", "x", "wmod0", "s5", "wmod23", "w_gat", "w_att")}
        piece_loaded = [sem(f"piece_loaded_{i}") for i in range(2)]
        w_hi_ready, w_lo_ready = sem("w_hi_ready"), sem("w_lo_ready")
        h_hi_ready, h_lo_ready, g_hi_ready, g_lo_ready = (
            sem(k) for k in ("h_hi_ready", "h_lo_ready", "g_hi_ready", "g_lo_ready"))
        consts_done = sem("consts_done")
        const_step = sem("const_step")
        setup_step = sem("setup_step")
        act_setup = sem("act_setup")
        silu_ready = sem("silu_ready")
        mod0_rows_psum, mod0_rows_ready = sem("mod0_rows_psum"), sem("mod0_rows_ready")
        MOD0_BANKS = (2, 3, 5, 6)[:NMOD0 * P // 512]
        mod0_psum = sem("mod0_psum")
        mod0_ready = sem("mod0_ready")
        s5_in_ready = sem("s5_in_ready")
        s5_inT_psum = sem("s5_inT_psum")
        s5_ready = sem("s5_ready")
        mod23_psum = sem("mod23_psum")
        gates0_ready = sem("gates0_ready")
        gates2_ready = sem("gates2_ready")
        gates_stored = sem("gates_stored")
        gates2_stored = sem("gates2_stored")
        stored = sem("stored")

        S = {}
        for n in ORDER:
            names = ["xT_psum", "out_psum", "out_read"]
            if n != "gat":
                names += ["hT_ready"]
            if n != "att":
                names += ["x_ready"]
            if n in NORMS and NORMS[n][0] == "rms":
                names += ["msq_done"]
            if n in MLPS:
                names += ["hid_psum"]
            if n in BIASED:
                names += ["upd_ready"]
            S[n] = {k: sem(f"{n}_{k}") for k in names}
        gate_loaded = [sem(f"gate_loaded_{i}") for i in range(2)]
        adj_loaded = [sem(f"adj_loaded_{i}") for i in range(2)]
        stats_done, aggr_done, var_ready, rstd_ready, xn_ready = (
            sem(k) for k in ("stats_done", "aggr_done", "var_ready", "rstd_ready", "xn_ready"))
        for n in ("s5", "ssm", "ff3"):
            S[n]["upd_ready"] = S[n]["out_read"]
        S["att"]["x_ready"] = S["att"]["out_read"]
        s5 = {k: sem(f"s5_{k}") for k in
            ("bu_psum", "u_used", "bu_ready", "rot_ready", "scan_ready", "zs_ready", "zc_ready")}
        ga = {k: sem(f"gat_{k}") for k in
            ("adj_used", "adj_w", "lab", "pen", "cb", "xs_ready", "nz_ready", "nz_psum", "w_hi", "w_lo", "h_hi",
             "h_lo", "sf_hi", "sf_lo", "sf_psum", "sf_used", "sfA_ready", "sfT_ready", "kvrep_ready", "q_psum",
             "q_ready", "k_psum", "KB_ready", "v_psum", "VB_ready", "s_psum", "s_biased", "smax_done", "s_shifted",
             "exp_done", "ssum_done", "srec_done", "w_ready", "wT_psum", "wT_ready")}
        at = {k: sem(f"att_{k}") for k in
            ("w_hi", "w_lo", "q_psum", "q_hi", "k_psum", "k_hi", "qk_lo", "v_psum", "v_ready", "v_hi", "v_lo",
             "s_psum", "amax_done", "nmax_done", "exp_done", "arec_done", "exT_psum", "exT_ready", "exT_hi",
             "exT_lo", "row_added")}
        ws_psum = sem("ws_psum")
        ws_ready = sem("ws_ready")
        block = ctx.enter_context(nc.Block())

        def prev(n):
            return S[ORDER[ORDER.index(n) - 1]]

        def wait_x(eng, n, b):
            if n == "s5":
                if isinstance(b, int) and b < 2:
                    eng.wait_ge(L["x0"], 16)
                else:
                    eng.wait_ge(L["x"], 16 * (B // 2 - 1))
            else:
                eng.wait_ge(prev(n)["x_ready"], b + 1)

        def steps(eng, one):
            for b in range(FIRST):
                one(b, b % 2)
            with eng.Fori(0, TURNS) as i:
                for j in range(2):
                    one(i * 2 + (FIRST + j), (FIRST + j) % 2)
            for b in range(LAST, B):
                one(b, b % 2)

        def hid_bank(banks, par, j):
            return j if banks == 4 else banks * par + j

        def loads(b, par):
            return (b - par) * 8 + 16

        def nth(n, b):
            return b + B * NORMED.index(n)

        def mth(n, b):
            return b + B * SPLIT.index(n)

        def hidden_count(n, b, j=0):
            earlier = list(MLPS)[:list(MLPS).index(n)]
            return b * BANKS[n] + (j + B * sum(BANKS[e] for e in earlier))

        def after(b, lag):
            return not isinstance(b, int) or b >= lag

        def before_end(b, ahead):
            return not isinstance(b, int) or b + ahead < B

        def piece_at(i):
            return PIECE * PIECE_AT[i]

        def pieces_at(n, b):
            at = {"s5": {1: [0], 2: [1], LAST: [2], LAST + 1: [3]}, "gat": {0: [4]}, "ssm": {1: [5], 2: [6]},
                  "att": {1: [7], 2: [8], B - 1: [9, 10]}}
            return at[n][b] if isinstance(b, int) and n in at and b in at[n] else []

        def last_pieces(n, b):
            return isinstance(b, int) and (n, b) == ("att", B - 1)

        def gat_weights():
            return (GAT_SQ_AT, w_gat[:, :, 0:3 * D]), (GAT_OUT_AT, w_gat[:, :, 5 * D:7 * D])

        def att_weights():
            return (ATT_QK_AT, w_att[:, :, 0:2 * D]), (ATT_V_AT, w_vp[:, :, :])

        def hidden_lo(eng, n, b, par):
            for j in range(BANKS[n]):
                eng.wait_ge(g_hi_ready, 2 * hidden_count(n, b, j + 1))
                eng.tensor_tensor(g_lo[:, par, 2 * j:2 * j + 2, :], gT[:, par, 2 * j:2 * j + 2, :],
                                  g_hi[:, par, 2 * j:2 * j + 2, :], ALU.subtract).then_inc(g_lo_ready, 1)

        @block.sync
        def _(sp):
            def load(dst, src, s):
                sp.dma_start(dst, src).then_inc(s, 16)

            load(cols[:, :], A["cols"], L["small"])
            load(cond[:, :, :], A["cond"], L["small"])
            load(rows[:, :], A["rows"].partition_broadcast(P), L["small"])
            load(gate_bias[:, :, :].rearrange("b g d -> b (g d)"), A["gate_bias"].partition_broadcast(B), L["small"])
            load(out_bias[:, :, :].rearrange("b g d -> b (g d)"), A["out_bias"].partition_broadcast(B), L["small"])
            load(s5_bc[:, :, :], A["s5_bc"], L["s5"])
            xv = A["x"].rearrange("b (t p) d -> p (b t) d", p=P)
            load(X[:, 0:4, :], xv[:, 0:4, :], L["x0"])
            load(wmod0[:, :, :], A["wmod0"], L["wmod0"])
            for c in range(1, B // 2):
                load(X[:, 4 * c:4 * c + 4, :], xv[:, 4 * c:4 * c + 4, :], L["x"])

            def load_piece(i):
                if i >= 2:
                    sp.wait_ge(w_lo_ready, i - 1)
                load(w_raw[:, i % 2, :], A["w_mlp"][:, i * PIECE:(i + 1) * PIECE], piece_loaded[i % 2])

            load_piece(0)
            load_piece(1)
            load(wmod23[:, :, :], A["wmod23"], L["wmod23"])
            load(w_gat[:, :, :], A["w_gat"], L["w_gat"])
            load(w_qpart[:, :, :], A["w_qpart"], L["w_gat"])
            load(w_att[:, :, :], A["w_att"], L["w_att"])

            def load_gate(n, g):
                def one(b, par):
                    if after(b, 2):
                        sp.wait_ge(S[n]["x_ready"], b - 1)
                    src = gate_dram[bass.ds(b, 1), 2 * D * g:2 * D * (g + 1)]
                    sp.dma_start(gates[:, par, :, :].rearrange("p a d -> p (a d)"),
                                 src.broadcast_to([P, 2 * D])).then_inc(gate_loaded[par], 16)
                    if n == "s5" and isinstance(b, int) and b == FIRST - 1:
                        load_piece(2)
                        load_piece(3)
                steps(sp, one)

            sp.wait_ge(gates0_ready, 1)
            sp.dma_start(gate_dram[:, 0:4 * D], gate_rows[:, 0:2, :, :].rearrange("b g a d -> b (g a d)"))\
              .then_inc(gates_stored, 16)
            sp.wait_ge(gates_stored, 16)
            load_gate("s5", 0)
            sp.wait_ge(gates2_ready, 1)
            sp.dma_start(gate_dram[:, 4 * D:8 * D], gate_rows[:, 2:4, :, :].rearrange("b g a d -> b (g a d)"))\
              .then_inc(gates2_stored, 16)
            def load_adj(b, par):
                if after(b, 2):
                    sp.wait_ge(ga["adj_used"], b - 1)
                src = A["adj"][b] if isinstance(b, int) else A["adj"][bass.ds(b, 1)].rearrange("o p n -> (o p) n")
                sp.dma_start(adj[par].rearrange("p g l -> p (g l)"), src).then_inc(adj_loaded[par], 16)

            load_adj(0, 0)
            load_adj(1, 1)
            sp.wait_ge(S["s5"]["x_ready"], B)
            load_piece(4)
            load_piece(5)
            load_gate("ff0", 1)

            def gat_loads(b, par):
                if after(b, 2):
                    load_adj(b, par)
                if isinstance(b, int) and b == FIRST - 1:
                    load_piece(6)

            steps(sp, gat_loads)
            sp.wait_ge(S["ff0"]["x_ready"], B)
            load_gate("ssm", 2)
            load_piece(7)
            load_piece(8)
            sp.wait_ge(S["ssm"]["x_ready"], B)
            load_gate("ff2", 3)
            load_piece(9)
            load_piece(10)

            ov = out.rearrange("b (t p) d -> p (b t) d", p=P)

            def store(b, par):
                sp.wait_ge(S["ff3"]["x_ready"], b + 1)
                if isinstance(b, int):
                    sp.dma_start(ov[:, 2 * b:2 * b + 2, :], X[:, 2 * b:2 * b + 2, :]).then_inc(stored, 16)
                else:
                    sp.dma_start(ov[:, bass.ds(b * 2, 2), :], X[:, bass.ds(b * 2, 2), :]).then_inc(stored, 16)

            steps(sp, store)
            sp.wait_ge(stored, 16 * B)

        @block.gpsimd
        def _(pool):
            pool.memset(ident[:, :], 0.0).then_inc(const_step, 1)
            pool.memset(ident_b[:, :], 0.0).then_inc(const_step, 1)
            pool.memset(half_neg[:, :], -0.5).then_inc(const_step, 1)
            pool.memset(ones[:, :], 1.0).then_inc(const_step, 1)
            pool.memset(head_mask[:, :, :], DH ** -0.5).then_inc(const_step, 1)
            pool.memset(v_mask[:, :, :], 1.0).then_inc(const_step, 1)
            pool.wait_ge(const_step, 6)
            for m in (ident, ident_b):
                pool.affine_select(out=m[:, :], in_=m[:, :], compare_op=ALU.not_equal, fill=1.0, base=0,
                                   pattern=[[-1, P]], channel_multiplier=1).then_inc(const_step, 1)
            pool.affine_select(out=head_mask[:, :, :], in_=head_mask[:, :, :], compare_op=ALU.is_ge, fill=0.0, base=0,
                               pattern=[[-DH, HPK], [0, NONGT]], channel_multiplier=1).then_inc(const_step, 1)
            pool.affine_select(out=v_mask[:, :, :], in_=v_mask[:, :, :], compare_op=ALU.is_ge, fill=0.0, base=0,
                               pattern=[[-NONGT, HPC], [0, DH]], channel_multiplier=1).then_inc(const_step, 1)
            pool.wait_ge(const_step, 10)
            pool.affine_select(out=head_mask[:, :, :], in_=head_mask[:, :, :], compare_op=ALU.is_ge, fill=0.0,
                               base=DH - 1, pattern=[[DH, HPK], [0, NONGT]], channel_multiplier=-1)\
                .then_inc(consts_done, 1)
            pool.affine_select(out=v_mask[:, :, :], in_=v_mask[:, :, :], compare_op=ALU.is_ge, fill=0.0,
                               base=NONGT - 1, pattern=[[NONGT, HPC], [0, DH]], channel_multiplier=-1)\
                .then_inc(consts_done, 1)

            def inv_std(n, b, par):
                s = S[n]
                pool.wait_ge(var_ready, nth(n, b) + 1)
                pool.tensor_tensor(rstd[:, par, :], var_eps[:, par, :], half_neg[:, :], ALU.pow)\
                    .then_inc(rstd_ready, 1)

            def add_bias(n, b, par):
                pool.wait_ge(S[n]["out_read"], b + 1)
                pool.tensor_tensor(upd[:, par, :, :], upd[:, par, :, :],
                                   gates[:, par, 1:2, :].broadcast_to([P, T, D]), ALU.add)\
                    .then_inc(S[n]["upd_ready"], 1)

            def s5_step(b, par):
                pool.wait_ge(s5["bu_ready"], 2 * (b + 1))
                pool.tensor_tensor(wrot[:, par, :], bu[:, par, 0, :], bu[:, par, 1, :], ALU.add)\
                    .then_inc(s5["rot_ready"], 1)
                pool.wait_ge(s5["scan_ready"], b + 1)
                if after(b, 2):
                    pool.wait_ge(S["s5"]["out_psum"], b - 1)
                pool.tensor_tensor(zc[:, par, :], zst[:, par, :], cosT[:, :], ALU.mult).then_inc(s5["zc_ready"], 1)

            def piece_lo(i):
                a = piece_at(i)
                pool.wait_ge(w_hi_ready, i + 1)
                pool.tensor_tensor(w_lo[:, a:a + PIECE], w_raw[:, i % 2, :], w_hi[:, a:a + PIECE], ALU.subtract)\
                    .then_inc(w_lo_ready, 1)

            def input_lo(n, b, par):
                pool.wait_ge(h_hi_ready, mth(n, b) + 1)
                pool.tensor_tensor(h_lo[:, par, :, :], hT[:, par, :, :], h_hi[:, par, :, :], ALU.subtract)\
                    .then_inc(h_lo_ready, 1)

            def att_weights_lo():
                pool.wait_ge(at["w_hi"], 2)
                for a, raw in att_weights():
                    n = raw.shape[1] * raw.shape[2]
                    view = lambda w: w[:, a:a + n].rearrange("p (k n) -> p k n", k=K)
                    pool.tensor_tensor(view(w_lo), raw, view(w_hi), ALU.subtract).then_inc(at["w_lo"], 1)

            def att_lo(b, par, what, raw, hi, lo):
                pool.wait_ge(hi, b + 1)
                pool.tensor_tensor(g_lo[:, par, what, :], raw[:, par, :, :], g_hi[:, par, what, :], ALU.subtract)\
                    .then_inc(lo, 1)

            def att_qk_lo(b, par):
                att_lo(b, par, Q, qT, at["q_hi"], at["qk_lo"])
                att_lo(b, par, KK, kT, at["k_hi"], at["qk_lo"])

            def begin(n):
                if n in JOINED:
                    return
                if n == "s5":
                    inv_std(n, 0, 0)
                    inv_std(n, 1, 1)
                if n == "gat":
                    gat_input_lo(0, 0)
                if n in SPLIT:
                    input_lo(n, 0, 0)
                    input_lo(n, 1, 1)
                    inv_std(n, 3, 1)

            def phase(n, follow):
                if n == "att":
                    att_qk_lo(0, 0)
                if n == "gat":
                    gat_self_lo(0, 0)
                    gat_input_lo(1, 1)

                def one(b, par):
                    if n == "s5" and before_end(b, 2):
                        inv_std(n, b + 2, par)
                    if n == "s5":
                        s5_step(b, par)
                    if n == "ff2" and isinstance(b, int) and b == 2:
                        att_weights_lo()
                    if n == "att":
                        att_lo(b, par, V, vp, at["v_hi"], at["v_lo"])
                        if after(b, 1):
                            att_lo(b - 1, 1 - par, E, exT, at["exT_hi"], at["exT_lo"])
                        if before_end(b, 1):
                            att_qk_lo(b + 1, 1 - par)
                    if n in SPLIT:
                        if n in ("ff0", "ssm", "ff3"):
                            hidden_lo(pool, n, b, par)
                        head = ahead(n, b, 2)
                        if head:
                            input_lo(*head, par)
                    for i in pieces_at(n, b) if not last_pieces(n, b) else []:
                        piece_lo(i)
                    if n in BIASED and after(b, 1):
                        add_bias(n, b - 1, 1 - par)
                    if n in JOINED and JOINED[n] in BIASED and not after(b, 1):
                        add_bias(JOINED[n], B - 1, 1 - par)
                    head = ahead(n, b, 4) if n in SPLIT else None
                    if head:
                        inv_std(*head, par)
                    if n == "gat":
                        gat_step(b, par)
                    first = early(EARLY_STATS, n, follow, b)
                    if first is not None:
                        inv_std(follow, first, first % 2)
                steps(pool, one)
                if n == "att":
                    att_lo(B - 1, (B - 1) % 2, E, exT, at["exT_hi"], at["exT_lo"])
                if follow:
                    begin(follow)
                if n in BIASED and follow not in JOINED:
                    add_bias(n, B - 1, (B - 1) % 2)

            def gat_shift(b, t):
                pool.wait_ge(ga["smax_done"], T * b + (t + 1))
                pool.tensor_tensor(sco[t], sco[t], smax[t].unsqueeze(2).broadcast_to([P, 2 * HEADS, NONGT]),
                                   ALU.subtract).then_inc(ga["s_shifted"], 1)

            def gat_soft(b, t):
                pool.wait_ge(ga["srec_done"], T * b + (t + 1))
                pool.tensor_tensor(prb[t], prb[t], srec[t].unsqueeze(2).broadcast_to([P, 2 * HEADS, NONGT]),
                                   ALU.mult).then_inc(ga["w_ready"], 1)

            def gat_input_lo(b, par):
                pool.wait_ge(ga["h_hi"], b + 1)
                pool.tensor_tensor(h_lo[:, par, :, :], hT[:, par, :, :], h_hi[:, par, :, :], ALU.subtract)\
                    .then_inc(ga["h_lo"], 1)

            def gat_self_lo(b, par):
                pool.wait_ge(ga["sf_hi"], b + 1)
                pool.tensor_tensor(sf_lo[:, :, :], sfT[par], sf_hi[:, :, :], ALU.subtract).then_inc(ga["sf_lo"], 1)

            def gat_step(b, par):
                gat_shift(b, 0)
                if before_end(b, 1):
                    gat_self_lo(b + 1, 1 - par)
                gat_shift(b, 1)
                if before_end(b, 2):
                    gat_input_lo(b + 2, par)
                gat_soft(b, 0)
                gat_soft(b, 1)

            begin("s5")
            for n, follow in zip(ORDER, ORDER[1:] + [None]):
                phase(n, follow)

        @block.scalar
        def _(act):
            act.wait_ge(L["small"], 16 * 5)
            act.activation(sc[:, 0:1], col("log_step"), ACT.Exp).then_inc(act_setup, 1)
            act.wait_ge(setup_step, 1)
            act.activation(sc[:, 2:3], sc[:, 1:2], ACT.Exp).then_inc(act_setup, 1)
            act.activation(sig[:, :, :], cond[:, :, :], ACT.Exp, scale=-1.0).then_inc(silu_ready, 1)
            act.wait_ge(setup_step, 10)
            act.activation(sc[:, 9:10], sc[:, 7:8], ACT.Sin).then_inc(act_setup, 1)
            act.activation(sc[:, 10:11], sc[:, 8:9], ACT.Sin).then_inc(act_setup, 1)

            def modulate(n, b, par):
                s, j = S[n], NORMED.index(n)
                act.wait_ge(s["xT_psum"], b + 1)
                if after(b, 2):
                    act.wait_ge(s5["u_used"], b - 1)
                for k in range(K):
                    act.activation(hT[:, par, k, :], PS[par][:, k * NTOK:(k + 1) * NTOK], ACT.Identity,
                                   bias=MH[:, j, k, bass.ds(b, 1)], scale=MS[:, j, k, bass.ds(b, 1)])\
                        .then_inc(s["hT_ready"], 1)

            def input_hi(n, b, par):
                act.wait_ge(S[n]["hT_ready"], K * (b + 1))
                if n == "ff0" and not after(b, 2):
                    act.wait_ge(gates2_stored, 16)
                if after(b, 2):
                    if n in MLPS:
                        act.wait_ge(S[n]["hid_psum"], (b - 1) * BANKS[n])
                    else:
                        act.wait_ge(at["v_psum"], b - 1)
                act.activation(h_hi[:, par, :, :], hT[:, par, :, :], ACT.Copy).then_inc(h_hi_ready, 1)

            def piece_hi(i):
                a = piece_at(i)
                act.wait_ge(piece_loaded[i % 2], 16 * (i // 2 + 1))
                for n, first in (("ff0", 4), ("gat", 5), ("ff2", 7)):
                    if i == first:
                        act.wait_ge(S[n]["out_psum"], B)
                if i >= 9:
                    act.wait_ge(at["v_psum"], B)
                act.activation(w_hi[:, a:a + PIECE], w_raw[:, i % 2, :], ACT.Copy).then_inc(w_hi_ready, 1)

            def hidden(n, b, par):
                s, (H, fn, _, _) = S[n], MLPS[n]
                banks = BANKS[n]
                if after(b, 2):
                    act.wait_ge(s["out_psum"], b - 1)
                for j in range(banks):
                    act.wait_ge(s["hid_psum"], b * banks + (j + 1))
                    bank = PS[2 + hid_bank(banks, par, j)]
                    for i in range(2):
                        m = 2 * j + i
                        act.activation(gT[:, par, m, :], bank[:, i * NTOK:(i + 1) * NTOK], fn,
                                       bias=col(f"{n}_b1", m))
                        act.activation(g_hi[:, par, m, :], bank[:, i * NTOK:(i + 1) * NTOK], fn,
                                       bias=col(f"{n}_b1", m)).then_inc(g_hi_ready, 1)

            def gat_copy(b, par):
                wait_x(act, "gat", b)
                if not after(b, 2):
                    act.wait_ge(prev("gat")["xT_psum"], B)
                if after(b, 2):
                    act.wait_ge(S["gat"]["xT_psum"], b - 1)
                    act.wait_ge(ga["nz_ready"], b - 1)
                for t in range(T):
                    act.activation(xn[:, par, t, :], X[:, bass.ds(b * 2 + t, 1), :].rearrange("p o d -> p (o d)"),
                                   ACT.Copy, accum_out=rsum[:, par, t:t + 1]).then_inc(ga["xs_ready"], 1)

            def gat_weights_hi(i):
                act.wait_ge(*((S["ff0"]["hid_psum"], B * BANKS["ff0"]), (S["ff0"]["out_psum"], B))[i])
                a, raw = gat_weights()[i]
                n = raw.shape[1] * raw.shape[2]
                act.activation(w_hi[:, a:a + n].rearrange("p (k n) -> p k n", k=K), raw, ACT.Copy)\
                   .then_inc(ga["w_hi"], 1)

            def gat_xT(b, par):
                act.wait_ge(S["gat"]["xT_psum"], b + 1)
                if after(b, 2):
                    act.wait_ge(ga["sf_psum"], b - 1)
                act.activation(hT[:, par, :, :].rearrange("p k n -> p (k n)"), PS[0][:, :], ACT.Copy)
                act.activation(h_hi[:, par, :, :].rearrange("p k n -> p (k n)"), PS[0][:, :], ACT.Copy)\
                    .then_inc(ga["h_hi"], 1)

            def gat_self_hi(b, par):
                act.wait_ge(ga["sfT_ready"], K * (b + 1))
                if after(b, 1):
                    act.wait_ge(ga["v_psum"], b)
                act.activation(sf_hi[:, :, :], sfT[par], ACT.Copy).then_inc(ga["sf_hi"], 1)

            def gat_self(b, par):
                act.wait_ge(ga["sf_psum"], b + 1)
                if after(b, 1):
                    act.wait_ge(ga["sfT_ready"], K * b)
                for k in range(K):
                    act.activation(sfA[:, k, :], PS[2][:, k * NTOK:(k + 1) * NTOK], ACT.Identity,
                                   bias=col("b_self", k)).then_inc(ga["sfA_ready"], 1)

            def gat_q(b, par):
                if after(b, 2):
                    act.wait_ge(ga["s_psum"], T * (b - 1))
                for d in range(2):
                    act.wait_ge(ga["q_psum"], 2 * b + (d + 1))
                    for k in range(K):
                        act.activation(QT[par][:, d, k, :], PS[3 - d][:, k * NTOK:(k + 1) * NTOK], ACT.Identity,
                                       bias=col("bq", 2 * d + k)).then_inc(ga["q_ready"], 1)

            def gat_exp(b, par, t):
                act.wait_ge(ga["s_shifted"], T * b + (t + 1))
                if after(b, 1):
                    act.wait_ge(ga["wT_psum"], 4 * b - 2 * (T - 1 - t))
                act.activation(prb[t], sco[t], ACT.Exp).then_inc(ga["exp_done"], 1)

            def gat_wT(b, par, t):
                if after(b, 1) and t == 0:
                    act.wait_ge(S["gat"]["out_psum"], b)
                for d in range(2):
                    act.wait_ge(ga["wT_psum"], 4 * b + (2 * t + d + 1))
                    n = len(CHUNKS) * P
                    act.activation(wT[0:HPC * NONGT, t, d, 0:n], PS[7 - 7 * d][0:HPC * NONGT, 0:n], ACT.Copy)\
                        .then_inc(ga["wT_ready"], 1)

            def att_weights_hi():
                act.wait_ge(S["ssm"]["out_psum"], B)
                act.wait_ge(ws_ready, 2)
                for a, raw in att_weights():
                    n = raw.shape[1] * raw.shape[2]
                    act.activation(w_hi[:, a:a + n].rearrange("p (k n) -> p k n", k=K), raw, ACT.Copy)\
                       .then_inc(at["w_hi"], 1)

            def att_qk(b, par):
                for what, hi, psum, dst, bank, bias in ((Q, at["q_hi"], at["q_psum"], qT, PS[2], "q_b"),
                                                        (KK, at["k_hi"], at["k_psum"], kT, PS[3], "k_b")):
                    act.wait_ge(psum, b + 1)
                    if after(b, 2) and what is Q:
                        act.wait_ge(at["s_psum"], b - 1)
                    if not after(b, 2) and what is Q:
                        act.wait_ge(prev("att")["out_psum"], b + (B - 1))
                    for to in (dst[:, par, :, :], g_hi[:, par, what, :]):
                        for k in range(K):
                            ins = act.activation(to[:, k, :], bank[:, k * NTOK:(k + 1) * NTOK], ACT.Identity,
                                                 bias=col(bias, k))
                    ins.then_inc(hi, 1)

            def att_v_hi(b, par):
                act.wait_ge(at["v_ready"], b + 1)
                if after(b, 2):
                    act.wait_ge(S["att"]["out_psum"], b - 1)
                act.activation(g_hi[:, par, V, :], vp[:, par, :, :], ACT.Copy).then_inc(at["v_hi"], 1)

            def att_exT_hi(b, par):
                act.wait_ge(at["exT_ready"], b + 1)
                if after(b, 2):
                    act.wait_ge(S["att"]["out_psum"], b - 1)
                act.activation(g_hi[:, par, E, :], exT[:, par, :, :], ACT.Copy).then_inc(at["exT_hi"], 1)

            def att_exp(b, par):
                act.wait_ge(at["nmax_done"], b + 1)
                if after(b, 2):
                    act.wait_ge(at["exT_psum"], b - 1)
                    act.wait_ge(at["arec_done"], b - 1)
                for t in range(T):
                    act.activation(ex[:, par, t, :], PS[4][:, t * NTOK:(t + 1) * NTOK], ACT.Exp,
                                   bias=nmax[:, par, t:t + 1], scale=D ** -0.5, accum_out=asum[:, par, t:t + 1])\
                        .then_inc(at["exp_done"], 1)

            def begin(n):
                if n == "s5":
                    act.wait_ge(mod0_ready, 1)
                    modulate(n, 0, 0)
                if n in JOINED:
                    return
                if n in SPLIT:
                    input_hi(n, 0, 0)
                    input_hi(n, 1, 1)
                if n == "gat":
                    gat_copy(0, 0)
                    gat_copy(1, 1)
                    gat_xT(0, 0)
                    gat_weights_hi(0)

            def phase(n, follow):
                if n == "gat":
                    gat_xT(1, 1)
                    gat_copy(2, 0)
                    gat_self(0, 0)
                    gat_self_hi(0, 0)
                    gat_weights_hi(1)
                    gat_q(0, 0)
                if n == "att":
                    att_qk(0, 0)

                def one(b, par):
                    if n == "s5" and before_end(b, 1):
                        modulate(n, b + 1, 1 - par)
                    for i in pieces_at(n, b) if n != "att" else []:
                        piece_hi(i)
                    if n in MLPS:
                        hidden(n, b, par)
                        if n == "ff2" and isinstance(b, int) and b == 2:
                            att_weights_hi()
                    if n == "gat":
                        if after(b, 1):
                            gat_wT(b - 1, 1 - par, 0)
                        if before_end(b, 1):
                            gat_self(b + 1, 1 - par)
                        if after(b, 1):
                            gat_wT(b - 1, 1 - par, 1)
                        if before_end(b, 1):
                            gat_self_hi(b + 1, 1 - par)
                        gat_exp(b, par, 0)
                        if before_end(b, 2):
                            gat_xT(b + 2, par)
                        gat_exp(b, par, 1)
                        if before_end(b, 1):
                            gat_q(b + 1, 1 - par)
                        if before_end(b, 3):
                            gat_copy(b + 3, 1 - par)
                    if n == "att":
                        att_v_hi(b, par)
                        if after(b, 1):
                            att_exT_hi(b - 1, 1 - par)
                        att_exp(b, par)
                        if before_end(b, 1):
                            att_qk(b + 1, 1 - par)
                    head = ahead(n, b, 2) if n in SPLIT else None
                    if head:
                        input_hi(*head, par)
                    if n == "att":
                        for i in pieces_at(n, b):
                            piece_hi(i)
                steps(act, one)
                if n == "att":
                    att_exT_hi(B - 1, (B - 1) % 2)
                if n == "gat":
                    gat_wT(B - 1, (B - 1) % 2, 0)
                    gat_wT(B - 1, (B - 1) % 2, 1)
                if follow:
                    begin(follow)

            for j, bank in enumerate(MOD0_BANKS):
                act.wait_ge(mod0_rows_psum, j + 1)
                act.activation(mod_rows[:, j * 512:(j + 1) * 512], PS[bank][0:B, :], ACT.Copy)\
                   .then_inc(mod0_rows_ready, 1)
            begin("s5")
            for n, follow in zip(ORDER, ORDER[1:] + [None]):
                phase(n, follow)

        @block.tensor
        def _(pe):
            def group(dst, pairs, inc=None):
                for i, (l, r) in enumerate(pairs):
                    mm = pe.matmul(dst, l, r, start=(i == 0), stop=(i == len(pairs) - 1))
                if inc is not None:
                    mm.then_inc(inc, 1)

            pe.wait_ge(s5_in_ready, 2)
            pe.wait_ge(consts_done, 2)
            for i in range(2):
                for k in range(K):
                    tr = pe.transpose(PS[4][:, (2 * i + k) * P:(2 * i + k + 1) * P], s5_in[:, i, k * P:(k + 1) * P],
                                      ident[:, :])
            tr.then_inc(s5_inT_psum, 1)

            pe.wait_ge(L["small"], 16 * 5)
            pe.wait_ge(L["wmod0"], 16)
            for j, bank in enumerate(MOD0_BANKS):
                group(PS[bank][0:B, :], [(cond[:, k, :], wmod0[:, k, j * 512:(j + 1) * 512]) for k in range(K)],
                      mod0_rows_psum)
            pe.wait_ge(mod0_rows_ready, len(MOD0_BANKS))
            for j in range(NMOD0):
                tr = pe.transpose(PS[2][:, j * B:(j + 1) * B], mod_rows[:, j * P:(j + 1) * P], ident[0:B, 0:B])
            tr.then_inc(mod0_psum, 1)

            def transposes(n, b, par):
                s = S[n]
                if n == "gat":
                    pe.wait_ge(ga["xs_ready"], T * (b + 1))
                    bank = PS[0]
                    if after(b, 1):
                        pe.wait_ge(ga["h_hi"], b)
                    if after(b, 3):
                        pe.wait_ge(ga["wT_ready"], 4 * (b - 2))
                else:
                    pe.wait_ge(xn_ready, T * (nth(n, b) + 1))
                    bank = PS[par]
                    if prev(n) is S["gat"] and not after(b, 1):
                        pe.wait_ge(ga["wT_ready"], 4 * B)
                for k in range(K):
                    for t in range(T):
                        tr = pe.transpose(bank[:, k * NTOK + t * P:k * NTOK + (t + 1) * P],
                                          xn[:, par, t, k * P:(k + 1) * P], ident[:, :])
                tr.then_inc(s["xT_psum"], 1)

            def gat_zero_rows(b, par):
                pe.wait_ge(ga["nz_ready"], b + 1)
                if after(b, 1):
                    pe.wait_ge(ga["KB_ready"], 4 * b)
                for t in range(T):
                    mm = pe.matmul(PS[1][:, t * P:(t + 1) * P], nz[:, par, t:t + 1].broadcast_to([P, P]),
                                   ident_b[:, :], start=True, stop=True)
                mm.then_inc(ga["nz_psum"], 1)

            def out_bank(n, b, par):
                if after(b, 2):
                    pe.wait_ge(S[n]["out_read"], b - 1)
                elif n != "s5":
                    pe.wait_ge(prev(n)["out_read"], B)
                return PS[6 + par]

            def s5_in_mm(b, par):
                s = S["s5"]
                pe.wait_ge(s["hT_ready"], K * (b + 1))
                if after(b, 2):
                    pe.wait_ge(s5["bu_ready"], 2 * (b - 1))
                for i in range(2):
                    group(PS[2 + par][:, i * NTOK:(i + 1) * NTOK],
                          [(s5_inT[:, i, k, :], hT[:, par, k, :]) for k in range(K)], s5["bu_psum"] if i else None)
                bank = out_bank("s5", b, par)
                for t in range(T):
                    for k in range(K):
                        mm = pe.matmul(bank[:, t * D + k * P:t * D + (k + 1) * P], hT[:, par, k, t * P:(t + 1) * P],
                                  s5_diag[:, k, :], start=(t == 0 and k == 0), stop=False, skip_group_check=True)
                mm.then_inc(s5["u_used"], 1)

            def s5_out_mm(b, par):
                bank = PS[6 + par]
                pe.wait_ge(s5["zc_ready"], b + 1)
                pe.wait_ge(s5["zs_ready"], b + 1)
                for t in range(T):
                    tok = slice(t * P, (t + 1) * P)
                    pe.matmul(bank[:, t * D:(t + 1) * D], zc[:, par, tok], s5_out[:, 0, :], start=False, stop=False,
                              skip_group_check=True)
                    mm = pe.matmul(bank[:, t * D:(t + 1) * D], zs[:, par, tok], s5_out[:, 1, :], start=False,
                                   stop=True, skip_group_check=True)
                mm.then_inc(S["s5"]["out_psum"], 1)

            def up(n, b, par):
                s, banks = S[n], BANKS[n]
                pe.wait_ge(h_lo_ready, mth(n, b) + 1)
                for j in range(banks):
                    if banks == 4 and after(b, 1):
                        pe.wait_ge(g_hi_ready, 2 * hidden_count(n, b - 1, j + 1))
                    if banks < 4 and after(b, 2) and j == 0:
                        pe.wait_ge(g_hi_ready, 2 * hidden_count(n, b - 1))
                    if n == "ff2" and not after(b, 1) and j == 0:
                        pe.wait_ge(g_hi_ready, 2 * hidden_count(n, 0))
                    if n == "ff3" and not after(b, 1) and j == 0:
                        pe.wait_ge(at["v_ready"], B)
                    for i in range(2):
                        m = 2 * j + i
                        group(PS[2 + hid_bank(banks, par, j)][:, i * NTOK:(i + 1) * NTOK],
                              [(w1(w, n, k, m), h[:, par, k, :]) for k in range(K)
                               for w, h in ((w_lo, h_hi), (w_hi, h_hi), (w_hi, h_lo))],
                              s["hid_psum"] if i else None)

            def down(n, b, par):
                s, H = S[n], MLPS[n][0]
                M = H // P
                bank = out_bank(n, b, par)
                pe.wait_ge(g_lo_ready, hidden_count(n, b + 1))
                bias = [(ones[:, :], row("ssm_b2")[0:1, :])] if n == "ssm" else []
                for t in range(T):
                    group(bank[:, t * D:(t + 1) * D],
                          bias + [(g[:, par, m, t * P:(t + 1) * P], w2(w, n, m)) for m in range(M)
                           for g, w in ((g_lo, w_hi), (g_hi, w_hi), (g_hi, w_lo))],
                          s["out_psum"] if t == T - 1 else None)

            def three(pairs):
                return [p(*part) for p in pairs for part in ((1, 0), (0, 0), (0, 1))]

            HL, WL, GL = (h_hi, h_lo), (w_hi, w_lo), (g_hi, g_lo)
            SF, KV_ = (sf_hi, sf_lo), (kv_hi, kv_lo)

            def gat_self(b, par):
                pe.wait_ge(ga["h_lo"], b + 1)
                if after(b, 1):
                    pe.wait_ge(ga["q_ready"], 4 * b)
                for m in range(K):
                    a = GAT_SQ_AT + m * P
                    group(PS[2][:, m * NTOK:(m + 1) * NTOK],
                          three([lambda x, y, k=k, a=a: (WL[x][:, a + k * 3 * D:a + k * 3 * D + P],
                                                         HL[y][:, par, k, :]) for k in range(K)]),
                          ga["sf_psum"] if m == K - 1 else None)

            def gat_q(b, par, d):
                pe.wait_ge(ga["sf_lo"], b + 1)
                if d == 0 and after(b, 1):
                    pe.wait_ge(ga["VB_ready"], b)
                for m in range(K):
                    a = GAT_SQ_AT + (1 + d) * D + m * P
                    group(PS[3 - d][:, m * NTOK:(m + 1) * NTOK],
                          three([lambda x, y, k=k, a=a: (WL[x][:, a + k * 3 * D:a + k * 3 * D + P],
                                                         SF[y][:, k, :]) for k in range(K)]),
                          ga["q_psum"] if m == K - 1 else None)

            def gat_k(b, par):
                for d in range(2):
                    for m in range(K):
                        g = 2 * d + m
                        a = (3 + d) * D + m * P
                        group(PS[1][:, 256 + g * NONGT:256 + (g + 1) * NONGT],
                              [(w_gat[:, k, a:a + P], sfT[par][:, k, 0:NONGT]) for k in range(K)],
                              ga["k_psum"] if g == 3 else None)

            def gat_v(b, par):
                pe.wait_ge(ga["kvrep_ready"], b + 1)
                if not after(b, 1):
                    pe.wait_ge(ga["w_lo"], 2)
                pe.wait_ge(ga["q_ready"], 4 * b + 2)
                group(PS[3][0:HPC * NONGT, :],
                      three([lambda x, y, k=k: (KV_[x][:, k, :, :].rearrange("p h m -> p (h m)"),
                                                WL[y][:, GAT_OUT_AT + k * 2 * D:GAT_OUT_AT + (k + 1) * 2 * D])
                             for k in range(K)]), ga["v_psum"])

            def gat_scores(b, par, t):
                if t == 0:
                    pe.wait_ge(ga["KB_ready"], 4 * (b + 1))
                    pe.wait_ge(ga["q_ready"], 4 * (b + 1))
                    if after(b, 1):
                        pe.wait_ge(ga["s_biased"], T * b)
                else:
                    pe.wait_ge(ga["s_biased"], T * b + t)
                for d in range(2):
                    for k in range(K):
                        mm = pe.matmul(PS[4 + d][:, k * HPK * NONGT:(k + 1) * HPK * NONGT],
                                       QT[par][:, d, k, t * P:(t + 1) * P],
                                       KB[par][:, 2 * d + k, :, :].rearrange("p h m -> p (h m)"),
                                       start=True, stop=True)
                mm.then_inc(ga["s_psum"], 1)

            def gat_wT(b, par, t):
                pe.wait_ge(ga["w_ready"], T * b + (t + 1))
                for d in range(2):
                    bank = PS[7 - 7 * d]
                    if t:
                        pe.wait_ge(ga["wT_ready"], 4 * b + (2 * t + d - 1))
                    elif not d:
                        if after(b, 1):
                            pe.wait_ge(ga["wT_ready"], 4 * b)
                        else:
                            pe.wait_ge(prev("gat")["out_read"], B)
                    elif before_end(b, 2):
                        pe.wait_ge(ga["h_hi"], b + 3)
                    for c, (start, _, _) in enumerate(CHUNKS):
                        h0 = d * HEADS + start
                        tr = pe.transpose(bank[0:HPC * NONGT, c * P:(c + 1) * P],
                                          prb[t][:, h0:h0 + HPC, :].rearrange("p h m -> p (h m)"), ident[:, :])
                    tr.then_inc(ga["wT_psum"], 1)

            def gat_open(b, par):
                if after(b, 1):
                    pe.wait_ge(S["gat"]["out_read"], b)
                else:
                    pe.wait_ge(prev("gat")["out_read"], B)
                for t in range(T):
                    for k in range(K):
                        mm = pe.matmul(PS[6][:, t * D + k * P:t * D + (k + 1) * P], sfT[par][:, k, t * P:(t + 1) * P],
                                       ident[:, :], start=(t == 0 and k == 0), stop=False, skip_group_check=True)
                mm.then_inc(ga["sf_used"], 1)

            def gat_out(b, par):
                for t in range(T):
                    pe.wait_ge(ga["wT_ready"], 4 * b + (2 * t + 2))
                    for d in range(2):
                        for c, (_, h, end) in enumerate(CHUNKS):
                            mm = pe.matmul(PS[6][:, t * D + h * DH:t * D + end * DH],
                                           wT[0:HPC * NONGT, t, d, c * P:(c + 1) * P],
                                           VB[par][:, d, h * DH:end * DH],
                                           start=False, stop=(d == 1), skip_group_check=True)
                mm.then_inc(S["gat"]["out_psum"], 1)

            def att_qk(b, par):
                pe.wait_ge(h_lo_ready, mth("att", b) + 1)
                for i, (psum, hi, bank) in enumerate(((at["q_psum"], at["q_hi"], PS[2]),
                                                      (at["k_psum"], at["k_hi"], PS[3]))):
                    if after(b, 1):
                        pe.wait_ge(hi, b)
                    for m in range(K):
                        a = ATT_QK_AT + i * D + m * P
                        group(bank[:, m * NTOK:(m + 1) * NTOK],
                              three([lambda x, y, k=k, a=a: (WL[x][:, a + k * 2 * D:a + k * 2 * D + P],
                                                             HL[y][:, par, k, :]) for k in range(K)]),
                              psum if m == K - 1 else None)

            def att_v(b, par):
                if after(b, 1):
                    pe.wait_ge(at["v_ready"], b)
                for t in range(T):
                    group(PS[5][:, t * D:(t + 1) * D],
                          three([lambda x, y, k=k, t=t: (HL[x][:, par, k, t * P:(t + 1) * P],
                                                         WL[y][:, ATT_V_AT + k * D:ATT_V_AT + (k + 1) * D])
                                 for k in range(K)]),
                          at["v_psum"] if t == T - 1 else None)

            def att_scores(b, par):
                pe.wait_ge(at["qk_lo"], 2 * (b + 1))
                if after(b, 1):
                    pe.wait_ge(at["exp_done"], T * b)
                for t in range(T):
                    group(PS[4][:, t * NTOK:(t + 1) * NTOK],
                          three([lambda x, y, k=k, t=t: (GL[x][:, par, Q.start + k, t * P:(t + 1) * P],
                                                         GL[y][:, par, KK.start + k, :]) for k in range(K)]),
                          at["s_psum"] if t == T - 1 else None)

            def att_exT(b, par):
                pe.wait_ge(at["exp_done"], T * (b + 1))
                if after(b, 1):
                    pe.wait_ge(at["exT_ready"], b)
                else:
                    pe.wait_ge(prev("att")["out_read"], B)
                for m in range(T):
                    for t in range(T):
                        tr = pe.transpose(PS[7][:, m * NTOK + t * P:m * NTOK + (t + 1) * P],
                                          ex[:, par, t, m * P:(m + 1) * P], ident[:, :])
                tr.then_inc(at["exT_psum"], 1)

            def att_out(b, par):
                pe.wait_ge(at["v_lo"], b + 1)
                pe.wait_ge(at["exT_lo"], b + 1)
                if after(b, 1):
                    pe.wait_ge(S["att"]["out_read"], b)
                for t in range(T):
                    group(PS[6][:, t * D:(t + 1) * D],
                          three([lambda x, y, m=m, t=t: (GL[x][:, par, E.start + m, t * P:(t + 1) * P],
                                                         GL[y][:, par, V.start + m, :]) for m in range(T)]),
                          S["att"]["out_psum"] if t == T - 1 else None)

            def setup23(part):
                pe.wait_ge(L["wmod23"], 16)
                pe.wait_ge(silu_ready, 3)
                pe.wait_ge(s5_ready, 1)
                for j in range(NMOD2) if part == 0 else range(NMOD2, NMOD2 + NMOD3):
                    c = cond_silu if j < NMOD2 else cond
                    group(PS[4][:, j * B:(j + 1) * B],
                          [(wmod23[:, k, j * P:(j + 1) * P], c[:, k, :]) for k in range(K)])
                if part == 0:
                    return
                pe.wait_ge(L["w_gat"], 32)
                for m in range(K):
                    a = NMOD2 + NMOD3 + m
                    group(PS[4][:, a * B:(a + 1) * B],
                          [(w_qpart[:, k, m * P:(m + 1) * P], cond[:, k, :]) for k in range(K)],
                          mod23_psum if m == K - 1 else None)
                for g, name in enumerate(("gate_msa", "gate_mlp")):
                    a = (MOD[name] - NMOD0) * P
                    group(PS[5][0:B, g * D:(g + 1) * D],
                          [(cond_silu[:, k, :], wmod23[:, k, a:a + D]) for k in range(K)], mod23_psum if g else None)

            def setup_vp():
                pe.wait_ge(L["w_att"], 16)
                pe.wait_ge(gates2_ready, 1)
                for m in range(K):
                    group(PS[4][:, m * D:(m + 1) * D],
                          [(w_att[:, k, 2 * D + m * P:2 * D + (m + 1) * P], w_att[:, k, 3 * D:4 * D])
                           for k in range(K)])
                group(PS[5][:, 0:D], [(col("v_b", k).broadcast_to([P, P]), w_att[:, k, 3 * D:4 * D]) for k in range(K)],
                      ws_psum)

            def begin(n):
                if n in JOINED:
                    return
                transposes(n, 0, 0)
                if n in SPLIT:
                    transposes(n, 1, 1)

            def phase(n, follow):
                if n == "s5":
                    pe.wait_ge(s5_ready, 1)
                if n in MLPS:
                    pe.wait_ge(w_lo_ready, PIECES[n])
                if n == "ff0":
                    pe.wait_ge(ws_ready, 2)
                if n == "gat":
                    transposes(n, 1, 1)
                    gat_zero_rows(0, 0)
                    pe.wait_ge(ga["w_lo"], 1)
                    gat_self(0, 0)
                    gat_q(0, 0, 0)
                    gat_q(0, 0, 1)
                    gat_k(0, 0)
                    gat_v(0, 0)
                if n == "att":
                    pe.wait_ge(at["w_lo"], 2)
                    pe.wait_ge(g_hi_ready, 2 * hidden_count("ff2", B))
                    att_qk(0, 0)
                    att_v(0, 0)

                def one(b, par):
                    if n == "s5" or n in MLPS:
                        if n == "s5":
                            s5_in_mm(b, par)
                            if before_end(b, 1):
                                transposes(n, b + 1, 1 - par)
                        else:
                            up(n, b, par)
                            head = ahead(n, b, 2)
                            if head:
                                transposes(*head, par)
                        if n == "s5" and isinstance(b, int) and b in (LAST, LAST + 1):
                            setup23(b - LAST)
                        if n == "s5" and isinstance(b, int) and b == LAST + 2:
                            setup_vp()
                        if after(b, 1):
                            (s5_out_mm if n == "s5" else lambda *a: down(n, *a))(b - 1, 1 - par)
                    more = before_end(b, 1)
                    if n == "gat":
                        gat_scores(b, par, 0)
                        if after(b, 1):
                            gat_wT(b - 1, 1 - par, 0)
                        if more:
                            gat_zero_rows(b + 1, 1 - par)
                            gat_self(b + 1, 1 - par)
                        if after(b, 1):
                            gat_wT(b - 1, 1 - par, 1)
                        gat_scores(b, par, 1)
                        if after(b, 1):
                            gat_out(b - 1, 1 - par)
                        if before_end(b, 2):
                            transposes(n, b + 2, par)
                        if more:
                            gat_q(b + 1, 1 - par, 0)
                            gat_q(b + 1, 1 - par, 1)
                            gat_k(b + 1, 1 - par)
                        gat_open(b, par)
                        if more:
                            gat_v(b + 1, 1 - par)
                    if n in JOINED and not after(b, 1):
                        finish(JOINED[n])
                    if n == "att":
                        att_scores(b, par)
                        head = ahead(n, b, 2)
                        if head:
                            transposes(*head, par)
                        if more:
                            att_qk(b + 1, 1 - par)
                        att_exT(b, par)
                        if more:
                            att_v(b + 1, 1 - par)
                        if after(b, 1):
                            att_out(b - 1, 1 - par)
                steps(pe, one)
                if n == "gat":
                    gat_wT(B - 1, (B - 1) % 2, 0)
                    gat_wT(B - 1, (B - 1) % 2, 1)
                if follow:
                    begin(follow)
                if follow not in JOINED:
                    finish(n)

            def finish(n):
                last = (B - 1) % 2
                if n == "s5":
                    s5_out_mm(B - 1, last)
                elif n in MLPS:
                    down(n, B - 1, last)
                elif n == "gat":
                    gat_out(B - 1, last)
                else:
                    att_out(B - 1, last)

            begin("s5")
            for n, follow in zip(ORDER, ORDER[1:] + [None]):
                phase(n, follow)

        @block.vector
        def _(dve):
            chain = [0]

            def link(ins):
                chain[0] += 1
                ins.then_inc(setup_step, 1)
                dve.wait_ge(setup_step, chain[0])

            def links(*made):
                chain[0] += len(made)
                for ins in made:
                    ins.then_inc(setup_step, 1)
                dve.wait_ge(setup_step, chain[0])

            def ts(out_, in_, s1, s2=None, op0=ALU.mult, op1=None):
                if op1 is None:
                    return dve.tensor_scalar(out_, in_, s1, None, op0)
                return dve.tensor_scalar(out_, in_, s1, s2, op0, op1)

            def stt(out_, in0, scalar, in1, op0, op1):
                return dve.scalar_tensor_tensor(out=out_, in0=in0, scalar=scalar, in1=in1, op0=op0, op1=op1)

            def c(i):
                return sc[:, i:i + 1]

            def s5_scalars():
                dve.wait_ge(L["small"], 16 * 5)
                dve.wait_ge(act_setup, 1)
                link(dve.tensor_tensor(c(1), col("Lam_re"), c(0), ALU.mult))
                link(dve.tensor_tensor(c(3), col("Lam_im"), c(0), ALU.mult))
                link(ts(c(12), c(3), float(1 / (2 * np.pi)), ROUND, ALU.mult, ALU.add))
                link(ts(c(4), c(12), -ROUND, None, ALU.add))
                link(stt(c(5), c(4), -TWO_PI_HI, c(3), ALU.mult, ALU.add))
                link(stt(c(6), c(4), -TWO_PI_MID, c(5), ALU.mult, ALU.add))
                link(stt(c(11), c(4), -TWO_PI_LO, c(6), ALU.mult, ALU.add))
                link(ts(c(7), c(11), PI, -PI, ALU.min, ALU.max))
                link(stt(c(12), c(7), -1.0, c(7), ALU.mult, ALU.max))
                link(ts(c(8), c(12), -1.0, HALF_PI, ALU.mult, ALU.add))

            def s5_setup():
                dve.wait_ge(act_setup, 4)
                link(dve.tensor_tensor(c(13), c(2), c(10), ALU.mult))
                link(ts(c(13), c(13), -1.0, None, ALU.add))
                link(dve.tensor_tensor(c(14), c(2), c(9), ALU.mult))
                re, im = col("Lam_re"), col("Lam_im")
                link(dve.tensor_tensor(c(15), re, re, ALU.mult))
                link(stt(c(16), im, im, c(15), ALU.mult, ALU.add))
                link(dve.reciprocal(c(17), c(16)))
                link(dve.tensor_tensor(c(18), c(13), re, ALU.mult))
                link(stt(c(19), c(14), im, c(18), ALU.mult, ALU.add))
                link(dve.tensor_tensor(c(20), c(19), c(17), ALU.mult))
                link(dve.tensor_tensor(c(21), c(13), im, ALU.mult))
                link(stt(c(22), c(14), re, c(21), ALU.mult, ALU.subtract))
                link(dve.tensor_tensor(c(23), c(22), c(17), ALU.mult))
                link(ts(c(24), c(23), sign[:, 0:1], -1.0, ALU.mult, ALU.mult))
                link(ts(c(25), c(20), sign[:, 0:1]))
                link(ts(c(26), sign[:, 0:1], 2.0))
                dve.wait_ge(L["s5"], 16)
                link(ts(s5_tmp[:, 0, :], s5_bc[:, 0, :], c(20)))
                link(ts(s5_tmp[:, 1, :], s5_bc[:, 0, :], c(23)))
                stt(s5_in[:, 0, :], s5_bc[:, 1, :], c(24), s5_tmp[:, 0, :], ALU.mult, ALU.add).then_inc(s5_in_ready, 1)
                stt(s5_in[:, 1, :], s5_bc[:, 1, :], c(25), s5_tmp[:, 1, :], ALU.mult, ALU.add).then_inc(s5_in_ready, 1)
                begin("s5")
                link(ts(s5_out[:, 0, :], s5_bc[:, 2, :], c(26)))
                link(ts(s5_out[:, 1, :], s5_bc[:, 3, :], -2.0))
                dve.wait_ge(consts_done, 2)
                for k in range(K):
                    link(ts(s5_diag[:, k, :], ident[:, :], col("D_diag", k)))
                link(dve.memset(decay[:, :], 1.0))
                link(ts(decay[:, :], decay[:, :], c(2)))
                link(dve.memset(cosT[:, 0:1], 1.0))
                link(dve.memset(sinT[:, 0:1], 0.0))
                ck, sk = c(10), c(9)
                n = 1
                while n < NTOK:
                    if n == NTOK // 8:
                        s5_inputs()
                        mods0()
                    double = 2 * n < NTOK
                    i = 27 + 3 * (n.bit_length() % 2)
                    first = [ts(rot[:, 0, 0:n], sinT[:, 0:n], sk), ts(rot[:, 1, 0:n], cosT[:, 0:n], sk)]
                    if double:
                        first.append(dve.tensor_tensor(c(i), sk, sk, ALU.mult))
                    links(*first)
                    then = [stt(cosT[:, n:2 * n], cosT[:, 0:n], ck, rot[:, 0, 0:n], ALU.mult, ALU.subtract),
                            stt(sinT[:, n:2 * n], sinT[:, 0:n], ck, rot[:, 1, 0:n], ALU.mult, ALU.add)]
                    if double:
                        then += [stt(c(i + 1), ck, ck, c(i), ALU.mult, ALU.subtract),
                                 stt(c(i + 2), sk, 2.0, ck, ALU.mult, ALU.mult)]
                    links(*then)
                    if double:
                        ck, sk = c(i + 1), c(i + 2)
                    n *= 2

            def s5_inputs():
                dve.wait_ge(s5_inT_psum, 1)
                dve.tensor_copy(s5_inT[:, :, :, :].rearrange("p i k n -> p (i k n)"), PS[4][:, :])\
                   .then_inc(s5_ready, 1)

            def mods0():
                dve.wait_ge(mod0_psum, 1)
                a, m = COLS["mod"][0], mod
                link(dve.tensor_tensor(m[:, 0:NMOD0, :], PS[2][:, 0:NMOD0 * B].rearrange("p (j b) -> p j b", b=B),
                                       cols[:, a:a + NMOD0].unsqueeze(2).broadcast_to([P, NMOD0, B]), ALU.add))
                for g, name in enumerate(("gate_a", "gate_ff")):
                    at_ = MOD[name] * P
                    link(dve.tensor_tensor(gate_rows[:, g, 0, :], mod_rows[:, at_:at_ + D], gate_bias[:, g, :],
                                           ALU.add))
                link(dve.memset(gate_rows[:, 0, 1, :], 0.0))
                dve.tensor_tensor(gate_rows[:, 1, 1, :], gate_rows[:, 1, 0, :], out_bias[:, 0, :], ALU.mult)\
                   .then_inc(gates0_ready, 1)
                v = lambda name: mod[:, MOD[name]:MOD[name] + K, :]
                link(ts(one_ff[:, :, :], v("scale_ff"), 1.0, None, ALU.add))
                link(stt(MS[:, 1, :, :], v("scale_c"), 1.0, one_ff[:, :, :], ALU.add, ALU.mult))
                link(dve.tensor_tensor(MH[:, 1, :, :], v("shift_c"), one_ff[:, :, :], ALU.mult))
                link(dve.tensor_tensor(MH[:, 1, :, :], MH[:, 1, :, :], v("shift_ff"), ALU.add))
                link(dve.tensor_copy(MH[:, 0, :, :], v("shift_a")))
                ts(MS[:, 0, :, :], v("scale_a"), 1.0, None, ALU.add).then_inc(mod0_ready, 1)

            def silu():
                dve.wait_ge(silu_ready, 1)
                ts(sig[:, :, :], sig[:, :, :], 1.0, None, ALU.add).then_inc(silu_ready, 1)
                dve.wait_ge(silu_ready, 2)
                link(dve.reciprocal(sig[:, :, :], sig[:, :, :]))
                dve.tensor_tensor(cond_silu[:, :, :], cond[:, :, :], sig[:, :, :], ALU.mult).then_inc(silu_ready, 1)

            def mods23():
                dve.wait_ge(mod23_psum, 2)
                a, n23 = COLS["mod"][0] + NMOD0, NMOD2 + NMOD3
                link(dve.tensor_tensor(mod[:, NMOD0:, :], PS[4][:, 0:n23 * B].rearrange("p (j b) -> p j b", b=B),
                                       cols[:, a:a + n23].unsqueeze(2).broadcast_to([P, n23, B]), ALU.add))
                link(dve.tensor_copy(qpart[:, :, :],
                                     PS[4][:, n23 * B:(n23 + K) * B].rearrange("p (j b) -> p j b", b=B)))
                link(dve.tensor_tensor(gate_rows[:, 2:4, 0, :], PS[5][0:B, :].rearrange("b (g d) -> b g d", g=2),
                                       gate_bias[:, 2:4, :], ALU.add))
                dve.tensor_tensor(gate_rows[:, 2:4, 1, :], gate_rows[:, 2:4, 0, :], out_bias[:, 1:3, :], ALU.mult)\
                   .then_inc(gates2_ready, 1)
                v = lambda name: mod[:, MOD[name]:MOD[name] + K, :]
                for name, sc_, sh in (("ssm", "scale_msa", "shift_msa"), ("ff2", "scale_mlp", "shift_mlp")):
                    j = NORMED.index(name)
                    link(ts(MS[:, j, :, :], v(sc_), 1.0, None, ALU.add))
                    link(dve.tensor_copy(MH[:, j, :, :], v(sh)))
                for name, w, sc_, sh in (("att", "norm1_w", "film1_scale", "film1_shift"),
                                         ("ff3", "norm2_w", "film2_scale", "film2_shift")):
                    j, a = NORMED.index(name), COLS[w][0]
                    link(stt(MS[:, j, :, :], v(sc_), 1.0, cols[:, a:a + K].unsqueeze(2).broadcast_to([P, K, B]),
                             ALU.add, ALU.mult))
                    link(dve.tensor_copy(MH[:, j, :, :], v(sh)))
                link(dve.tensor_tensor(bout[:, :], row("bout0"), row("bout1"), ALU.add))

            def vp_weights():
                dve.wait_ge(ws_psum, 1)
                dve.tensor_copy(w_vp[:, :, :], PS[4][:, :].rearrange("p (k n) -> p k n", k=K)).then_inc(ws_ready, 1)
                dve.tensor_tensor(att_row[:, :], PS[5][:, 0:D], row("proj_b"), ALU.add).then_inc(ws_ready, 1)

            def statistics(n, b, par):
                s, (kind, eps) = S[n], NORMS[n]
                wait_x(dve, n, b)
                for t in range(T):
                    dve.bn_stats(stats[:, par, t, :], X[:, bass.ds(b * 2 + t, 1), :].rearrange("p o d -> p (o d)"))\
                       .then_inc(stats_done, 1)
                dve.wait_ge(stats_done, T * (nth(n, b) + 1))
                mean_e, m2_e, mean_o, m2_o = (stats[:, par, :, i] for i in (1, 2, 4, 5))
                mean, m2, dif, dif2, mean2, sq = (mv[:, par, i, :] for i in range(6))
                dve.tensor_tensor(dif, mean_e, mean_o, ALU.subtract).then_inc(aggr_done, 1)
                stt(m2, m2_e, D * eps, m2_o, ALU.add, ALU.add).then_inc(aggr_done, 1)
                dve.tensor_tensor(mean2, mean_e, mean_o, ALU.add).then_inc(aggr_done, 1)
                dve.wait_ge(aggr_done, 5 * nth(n, b) + 3)
                stt(dif2, dif, 0.25, dif, ALU.mult, ALU.mult).then_inc(aggr_done, 1)
                if kind == "rms":
                    stt(sq, mean2, 0.25, mean2, ALU.mult, ALU.mult).then_inc(aggr_done, 1)
                    dve.wait_ge(aggr_done, 5 * nth(n, b) + 5)
                    dve.tensor_tensor(msq[:, par, :], dif2, sq, ALU.add).then_inc(s["msq_done"], 1)
                    dve.wait_ge(s["msq_done"], b + 1)
                    stt(var_eps[:, par, :], m2, 1 / D, msq[:, par, :], ALU.mult, ALU.add).then_inc(var_ready, 1)
                else:
                    ts(mean, mean2, 0.5).then_inc(aggr_done, 1)
                    dve.wait_ge(aggr_done, 5 * nth(n, b) + 5)
                    stt(var_eps[:, par, :], m2, 1 / D, dif2, ALU.mult, ALU.add).then_inc(var_ready, 1)

            def normalise(n, b, par):
                s, kind = S[n], NORMS[n][0]
                dve.wait_ge(rstd_ready, nth(n, b) + 1)
                if after(b, 2):
                    dve.wait_ge(s["xT_psum"], b - 1)
                elif n != "s5":
                    dve.wait_ge(prev(n)["xT_psum"], b + (B - 1))
                for t in range(T):
                    xb = X[:, bass.ds(b * 2 + t, 1), :].rearrange("p o d -> p (o d)")
                    r = rstd[:, par, t:t + 1]
                    if kind == "rms":
                        ins = ts(xn[:, par, t, :], xb, r)
                    else:
                        ins = ts(xn[:, par, t, :], xb, mv[:, par, 0, t:t + 1], r, ALU.subtract, ALU.mult)
                    ins.then_inc(xn_ready, 1)

            def modulate(n, b, par):
                s, j = S[n], NORMED.index(n)
                dve.wait_ge(s["xT_psum"], b + 1)
                if after(b, 2):
                    if n in MLPS:
                        dve.wait_ge(s["hid_psum"], (b - 1) * BANKS[n])
                    else:
                        dve.wait_ge(at["v_psum"], b - 1)
                for k in range(K):
                    ts(hT[:, par, k, :], PS[par][:, k * NTOK:(k + 1) * NTOK], MS[:, j, k, bass.ds(b, 1)],
                       MH[:, j, k, bass.ds(b, 1)], ALU.mult, ALU.add).then_inc(s["hT_ready"], 1)

            def gate(n, b, par):
                s = S[n]
                dve.wait_ge(s["out_psum"], b + 1)
                if n in GATES:
                    dve.wait_ge(gate_loaded[par], loads(b, par) + 8 * B * GATES.index(n))
                o = PS[6 + par][:, :].rearrange("p (t d) -> p t d", t=T)
                if n == "ff3":
                    dve.tensor_tensor(upd[:, par, :, :], o, row("mlp_b2").unsqueeze(1).broadcast_to([P, T, D]),
                                      ALU.add).then_inc(s["out_read"], 1)
                else:
                    dve.tensor_tensor(upd[:, par, :, :], o, gates[:, par, 0:1, :].broadcast_to([P, T, D]),
                                      ALU.mult).then_inc(s["out_read"], 1)

            def add_upd(n, b, par):
                xb = X[:, bass.ds(b * 2, 2), :]
                dve.wait_ge(S[n]["upd_ready"], b + 1)
                dve.tensor_tensor(xb, xb, upd[:, par, :, :], ALU.add).then_inc(S[n]["x_ready"], 1)

            def s5_rotate(b, par):
                dve.wait_ge(s5["bu_psum"], b + 1)
                if after(b, 2):
                    dve.wait_ge(s5["rot_ready"], b - 1)
                for i, table in enumerate((cosT, sinT)):
                    dve.tensor_tensor(bu[:, par, i, :], PS[2 + par][:, i * NTOK:(i + 1) * NTOK], table[:, :],
                                      ALU.mult).then_inc(s5["bu_ready"], 1)

            def s5_scan(b, par):
                dve.wait_ge(s5["rot_ready"], b + 1)
                if after(b, 2):
                    dve.wait_ge(s5["zc_ready"], b - 1)
                    dve.wait_ge(S["s5"]["out_psum"], b - 1)
                dve.tensor_tensor_scan(zst[:, par, :], decay[:, :], wrot[:, par, :], 0.0, ALU.mult, ALU.add)\
                   .then_inc(s5["scan_ready"], 1)
                dve.wait_ge(s5["scan_ready"], b + 1)
                dve.tensor_tensor(zs[:, par, :], zst[:, par, :], sinT[:, :], ALU.mult).then_inc(s5["zs_ready"], 1)

            def gat_nz(b, par):
                dve.wait_ge(ga["xs_ready"], T * (b + 1))
                if after(b, 2):
                    dve.wait_ge(ga["nz_psum"], b - 1)
                ts(nz[:, par, :], rsum[:, par, :], 0.0, None, ALU.not_equal).then_inc(ga["nz_ready"], 1)

            def gat_labels(b, par):
                dve.wait_ge(adj_loaded[par], loads(b, par))
                wb = row("w_bias").unsqueeze(1).broadcast_to([P, 4 * NONGT, LABELS])
                dve.tensor_tensor(adj_w, adj[par], wb, ALU.mult).then_inc(ga["adj_w"], 1)
                dve.tensor_reduce(cnt, adj[par], AX.X, ALU.add).then_inc(ga["adj_used"], 1)
                dve.wait_ge(ga["adj_w"], b + 1)
                dve.tensor_reduce(lab, adj_w, AX.X, ALU.add).then_inc(ga["lab"], 1)
                dve.wait_ge(ga["adj_used"], b + 1)
                ts(pen, cnt, 0.0, NEG, ALU.is_le, ALU.mult).then_inc(ga["pen"], 1)
                dve.wait_ge(ga["lab"], b + 1)
                dve.wait_ge(ga["pen"], b + 1)
                stt(cbias[par].rearrange("p d t m -> p (d t m)"), lab, row("b_bias"), pen, ALU.add, ALU.add)\
                    .then_inc(ga["cb"], 1)

            def gat_sfT(b, par):
                dve.wait_ge(ga["sfA_ready"], K * (b + 1))
                dve.wait_ge(ga["nz_psum"], b + 1)
                if after(b, 2):
                    dve.wait_ge(ga["sf_used"], b - 1)
                for k in range(K):
                    stt(sfT[par][:, k, :], PS[1][:, 0:NTOK], qpart[:, k, bass.ds(b, 1)], sfA[:, k, :],
                        ALU.mult, ALU.add).then_inc(ga["sfT_ready"], 1)

            def gat_keys(b, par):
                dve.wait_ge(ga["sf_hi"], b + 1)
                dve.wait_ge(ga["sf_lo"], b + 1)
                if after(b, 1):
                    dve.wait_ge(ga["v_psum"], b)
                for to, part in ((kv_hi, sf_hi), (kv_lo, sf_lo)):
                    ins = dve.tensor_copy(to[:, :, :, :],
                                          part[:, :, 0:NONGT].unsqueeze(2).broadcast_to([P, K, HPC, NONGT]))
                ins.then_inc(ga["kvrep_ready"], 1)

            def gat_weights_lo(i):
                a, raw = gat_weights()[i]
                n = raw.shape[1] * raw.shape[2]
                view = lambda w: w[:, a:a + n].rearrange("p (k n) -> p k n", k=K)
                dve.wait_ge(ga["w_hi"], i + 1)
                dve.tensor_tensor(view(w_lo), raw, view(w_hi), ALU.subtract).then_inc(ga["w_lo"], 1)

            def gat_KB(b, par):
                dve.wait_ge(ga["k_psum"], b + 1)
                if after(b, 2):
                    dve.wait_ge(ga["s_psum"], T * (b - 1))
                for g in range(4):
                    stt(KB[par][:, g, :, :],
                        PS[1][:, 256 + g * NONGT:256 + (g + 1) * NONGT].unsqueeze(1).broadcast_to([P, HPK, NONGT]),
                        col("bk", g), head_mask[:, :, :], ALU.add, ALU.mult).then_inc(ga["KB_ready"], 1)

            def gat_VB(b, par):
                dve.wait_ge(ga["v_psum"], b + 1)
                if after(b, 2):
                    dve.wait_ge(S["gat"]["out_psum"], b - 1)
                for start, h, end in CHUNKS:
                    mask = v_mask[:, h - start:end - start, :].rearrange("p h e -> p (h e)")
                    ins = dve.tensor_tensor(
                        VB[par][:, :, h * DH:end * DH],
                        PS[3][0:HPC * NONGT, :].rearrange("p (d n) -> p d n", d=2)[:, :, h * DH:end * DH],
                        mask.unsqueeze(1).broadcast_to([HPC * NONGT, 2, (end - h) * DH]), ALU.mult)
                ins.then_inc(ga["VB_ready"], 1)

            def gat_bias(b, par, t):
                dve.wait_ge(ga["s_psum"], T * b + (t + 1))
                dve.wait_ge(ga["cb"], b + 1)
                if after(b, 1):
                    dve.wait_ge(ga["exp_done"], T * (b - 1) + (t + 1))
                for d in range(2):
                    ins = dve.tensor_tensor(
                        sco[t][:, d * HEADS:(d + 1) * HEADS, :],
                        PS[4 + d][:, 0:HEADS * NONGT].rearrange("p (h m) -> p h m", m=NONGT),
                        cbias[par][:, d, t, :].unsqueeze(1).broadcast_to([P, HEADS, NONGT]), ALU.add)
                ins.then_inc(ga["s_biased"], 1)
                dve.wait_ge(ga["s_biased"], T * b + (t + 1))
                dve.tensor_reduce(smax[t], sco[t], AX.X, ALU.max).then_inc(ga["smax_done"], 1)

            def gat_sum(b, par, t):
                dve.wait_ge(ga["exp_done"], T * b + (t + 1))
                dve.tensor_reduce(ssum[t], prb[t], AX.X, ALU.add).then_inc(ga["ssum_done"], 1)
                dve.wait_ge(ga["ssum_done"], T * b + (t + 1))
                dve.reciprocal(srec[t], ssum[t]).then_inc(ga["srec_done"], 1)

            def gat_residual(b, par):
                dve.wait_ge(S["gat"]["out_psum"], b + 1)
                o = PS[6][:, :].rearrange("p (t d) -> p t d", t=T)
                dve.tensor_tensor(upd[:, par, :, :], o, bout[:, :].unsqueeze(1).broadcast_to([P, T, D]), ALU.add)\
                   .then_inc(S["gat"]["out_read"], 1)
                dve.wait_ge(S["gat"]["out_read"], b + 1)
                xb = X[:, bass.ds(b * 2, 2), :]
                stt(xb, upd[:, par, :, :], 0.0, xb, ALU.max, ALU.add).then_inc(S["gat"]["x_ready"], 1)

            def att_max(b, par):
                dve.wait_ge(at["s_psum"], b + 1)
                dve.tensor_reduce(amax[:, par, :], PS[4][:, :].rearrange("p (t m) -> p t m", t=T), AX.X, ALU.max)\
                   .then_inc(at["amax_done"], 1)
                dve.wait_ge(at["amax_done"], b + 1)
                if after(b, 2):
                    dve.wait_ge(at["exp_done"], T * (b - 1))
                ts(nmax[:, par, :], amax[:, par, :], -(D ** -0.5)).then_inc(at["nmax_done"], 1)

            def att_v(b, par):
                dve.wait_ge(at["v_psum"], b + 1)
                if after(b, 2):
                    dve.wait_ge(at["v_lo"], b - 1)
                dve.tensor_copy(vp[:, par, :, :].rearrange("p t d -> p (t d)"), PS[5][:, :]).then_inc(at["v_ready"], 1)

            def att_exT(b, par):
                dve.wait_ge(at["exT_psum"], b + 1)
                if after(b, 2):
                    dve.wait_ge(at["exT_lo"], b - 1)
                dve.tensor_copy(exT[:, par, :, :].rearrange("p m n -> p (m n)"), PS[7][:, :])\
                   .then_inc(at["exT_ready"], 1)
                dve.wait_ge(at["exp_done"], T * (b + 1))
                if after(b, 2):
                    dve.wait_ge(S["att"]["out_read"], b - 1)
                dve.reciprocal(arec[:, par, :], asum[:, par, :]).then_inc(at["arec_done"], 1)

            def att_residual(b, par):
                xb = X[:, bass.ds(b * 2, 2), :]
                dve.tensor_tensor(xb, xb, att_row[:, :].unsqueeze(1).broadcast_to([P, T, D]), ALU.add)\
                   .then_inc(at["row_added"], 1)
                dve.wait_ge(S["att"]["out_psum"], b + 1)
                dve.wait_ge(at["arec_done"], b + 1)
                dve.wait_ge(at["row_added"], b + 1)
                for t in range(T):
                    xt = X[:, bass.ds(b * 2 + t, 1), :].rearrange("p o d -> p (o d)")
                    ins = stt(xt, PS[6][:, t * D:(t + 1) * D], arec[:, par, t:t + 1], xt, ALU.mult, ALU.add)
                ins.then_inc(S["att"]["out_read"], 1)

            def piece_lo(i):
                a = piece_at(i)
                dve.wait_ge(w_lo_ready, i)
                dve.wait_ge(w_hi_ready, i + 1)
                dve.tensor_tensor(w_lo[:, a:a + PIECE], w_raw[:, i % 2, :], w_hi[:, a:a + PIECE], ALU.subtract)\
                   .then_inc(w_lo_ready, 1)

            def begin(n):
                if n in JOINED:
                    return
                if n == "s5":
                    for b in range(2):
                        statistics(n, b, b)
                        normalise(n, b, b)
                if n in SPLIT:
                    modulate(n, 0, 0)
                    modulate(n, 1, 1)
                    normalise(n, 2, 0)
                    statistics(n, 3, 1)
                if n == "gat":
                    gat_nz(0, 0)
                    gat_nz(1, 1)
                    gat_weights_lo(0)

            def phase(n, follow):
                if n == "gat":
                    gat_sfT(0, 0)
                    gat_weights_lo(1)
                    gat_keys(0, 0)
                    gat_labels(0, 0)
                    gat_KB(0, 0)
                    gat_VB(0, 0)
                    gat_nz(2, 0)
                if n == "att":
                    att_v(0, 0)

                def one(b, par):
                    more = before_end(b, 1)
                    if n == "att":
                        att_max(b, par)
                        if after(b, 2):
                            att_residual(b - 2, par)
                    if n == "s5" and before_end(b, 2):
                        statistics(n, b + 2, par)
                    if n in ("s5", *MLPS) and after(b, 2):
                        add_upd(n, b - 2, par)
                    if n == "s5":
                        s5_rotate(b, par)
                    if n in JOINED and not after(b, 2) and JOINED[n] in MLPS:
                        add_upd(JOINED[n], B - 2 + b, par)
                    if n in JOINED and not after(b, 1):
                        (gate if JOINED[n] in MLPS else lambda _, *a: att_residual(*a))(JOINED[n], B - 1, 1 - par)
                    head = ahead(n, b, 2) if n in SPLIT else None
                    if head:
                        modulate(*head, par)
                    if n == "ff2":
                        hidden_lo(dve, n, b, par)
                    if n == "att":
                        att_exT(b, par)
                        if more:
                            att_v(b + 1, 1 - par)
                    head = ahead(n, b, AHEAD[n]) if n in NORMS else None
                    if head:
                        normalise(*head, (par + AHEAD[n]) % 2)
                    for i in pieces_at(n, b) if last_pieces(n, b) else []:
                        piece_lo(i)
                    if n == "s5":
                        s5_scan(b, par)
                        if isinstance(b, int) and b == LAST + 1:
                            mods23()
                        if isinstance(b, int) and b == LAST + 2:
                            vp_weights()
                    if n in ("s5", *MLPS) and after(b, 1):
                        gate(n, b - 1, 1 - par)
                    if n == "gat":
                        gat_bias(b, par, 0)
                        if more:
                            gat_sfT(b + 1, 1 - par)
                        gat_bias(b, par, 1)
                        gat_sum(b, par, 0)
                        if more:
                            gat_keys(b + 1, 1 - par)
                        if after(b, 1):
                            gat_residual(b - 1, 1 - par)
                        gat_sum(b, par, 1)
                        if more:
                            gat_KB(b + 1, 1 - par)
                            gat_labels(b + 1, 1 - par)
                            gat_VB(b + 1, 1 - par)
                        if before_end(b, 3):
                            gat_nz(b + 3, 1 - par)
                    head = ahead(n, b, 4) if n in SPLIT else None
                    if head:
                        statistics(*head, par)
                    first = early(EARLY_NORMS, n, follow, b)
                    if first is not None:
                        normalise(follow, first, first % 2)
                    first = early(EARLY_STATS, n, follow, b)
                    if first is not None:
                        statistics(follow, first, first % 2)
                steps(dve, one)
                if n == "att":
                    att_residual(B - 2, B % 2)
                if follow:
                    begin(follow)
                last = (B - 1) % 2
                if follow in JOINED:
                    return
                if n in ("s5", *MLPS):
                    add_upd(n, B - 2, 1 - last)
                    gate(n, B - 1, last)
                    add_upd(n, B - 1, last)
                elif n == "gat":
                    gat_residual(B - 1, last)
                else:
                    att_residual(B - 1, last)

            s5_scalars()
            link(dve.memset(sign[0:STATES, :], 1.0))
            link(dve.memset(sign[STATES:P, :], -1.0))
            s5_setup()
            silu()
            for n, follow in zip(ORDER, ORDER[1:] + [None]):
                phase(n, follow)


_OUT = ((B, NTOK, D), "float32")


def lay_out(inputs):
    g = {k: np.asarray(v) for k, v in inputs.items()}

    def tiles(w):
        return np.ascontiguousarray(w.reshape(-1, P, w.shape[1]).transpose(1, 0, 2))

    def column(v):
        return v.reshape(-1, P).T

    x = g["x"]
    cond = g["cond_1024"]
    a = {"x": x, "cond": np.ascontiguousarray(cond.T.reshape(K, P, B).transpose(1, 0, 2))}
    a["wmod0"] = tiles(np.concatenate([g["L0_cond_Wm"], g["L0_cond_Wc"]], 1))
    a["wmod23"] = tiles(np.concatenate([g["L2_cond_ada_w"], g["L3_cond_film1_w"], g["L3_cond_film2_w"]], 1))
    mod_bias = np.concatenate([g["L0_cond_bm"], g["L0_cond_bc"], g["L2_cond_ada_b"], g["L3_cond_film1_b"],
                               g["L3_cond_film2_b"]])
    two = lambda v: np.concatenate([v, v])
    parts = {
        "mod": column(mod_bias), "ff0_b1": column(g["L0_cond_b1"]), "ssm_b1": column(g["L2_cond_ssm_b1"]),
        "ff2_b1": column(g["L2_cond_ff_b1"]), "ff3_b1": column(g["L3_cond_mlp_b1"]),
        "b_self": column(g["L1_cond_b_self"]), "bq": column(g["L1_cond_bq"].reshape(-1)),
        "bk": column(g["L1_cond_bk"].reshape(-1)), "q_b": column(g["L3_cond_q_b"]), "k_b": column(g["L3_cond_k_b"]),
        "norm1_w": column(g["L3_cond_norm1_w"]), "norm2_w": column(g["L3_cond_norm2_w"]),
        "D_diag": column(g["L0_cond_D_diag"]), "Lam_re": column(two(g["L0_cond_Lam_re"])),
        "Lam_im": column(two(g["L0_cond_Lam_im"])), "log_step": column(two(g["L0_cond_log_step"])),
        "v_b": column(g["L3_cond_v_b"]),
    }
    a["cols"] = np.ascontiguousarray(np.concatenate([parts[n] for n in COLS], 1))
    bout = g["L1_cond_bout"].reshape(2, D)
    a["rows"] = np.concatenate([bout[0], bout[1], g["L3_cond_proj_b"], g["L3_cond_mlp_b2"], g["L1_cond_w_bias"],
                                g["L1_cond_b_bias"].reshape(1), g["L2_cond_ssm_b2"]])
    bias = {n: mod_bias[MOD[n] * P:MOD[n] * P + D] for n in ("gate_a", "gate_ff", "gate_msa", "gate_mlp")}
    a["gate_bias"] = np.concatenate(list(bias.values()))
    a["out_bias"] = np.concatenate([g["L0_cond_b2"], g["L2_cond_ssm_b2"], g["L2_cond_ff_b2"]])
    br, bi, cr, ci = g["L0_cond_B_re"], g["L0_cond_B_im"], g["L0_cond_C_re"].T, g["L0_cond_C_im"].T
    a["s5_bc"] = np.ascontiguousarray(
        np.stack([np.concatenate(v) for v in ((br, bi), (bi, br), (cr, ci), (ci, cr))], 1))
    w = np.concatenate([tiles(g[n]).reshape(P, -1) for n in (
        "L0_cond_W1", "L0_cond_W2", "L2_cond_ssm_w1", "L2_cond_ssm_w2", "L2_cond_ff_w1", "L2_cond_ff_w2",
        "L3_cond_mlp_w1", "L3_cond_mlp_w2")], 1).reshape(P, -1, PIECE)
    before = PIECES["ff2"]
    order = list(range(before)) + [before + i for i in PIECE_AT[before:]]
    a["w_mlp"] = np.ascontiguousarray(w[:, order]).reshape(P, -1)
    w_self = g["L1_cond_W_self"].T
    wo = g["L1_cond_Wout"].reshape(2, D, D)
    a["w_gat"] = tiles(np.concatenate([w_self[:D], *(w.T for w in g["L1_cond_Wq"]), *(w.T for w in g["L1_cond_Wk"]),
                                       *(w.T for w in wo)], 1))
    a["w_qpart"] = tiles(w_self[D:])
    a["w_att"] = tiles(np.concatenate([g["L3_cond_q_w"], g["L3_cond_k_w"], g["L3_cond_v_w"].T, g["L3_cond_proj_w"]], 1))
    m = g["mask_BxSxSx11_ik0"]
    d0 = m[:, :, :NONGT].reshape(B, T, P, NONGT, LABELS)
    d1 = m[:, :NONGT].transpose(0, 2, 1, 3).reshape(B, T, P, NONGT, LABELS)
    a["adj"] = np.ascontiguousarray(np.stack([d0, d1], 1).transpose(0, 3, 1, 2, 4, 5)).reshape(B, P, -1)
    return a


def kernel(**inputs):
    import concourse.bacc as _bacc
    from concourse.bass_utils import run_bass_kernel_spmd as _run

    nc = _bacc.Bacc("TRN2", target_bir_lowering=False, num_devices=1)
    laid = lay_out(inputs)
    arrays, aps = {}, {}
    for name, a in laid.items():
        arrays[f"in_{name}"] = a
        aps[name] = nc.dram_tensor(f"in_{name}", a.shape, mybir.dt.from_np(a.dtype), kind="ExternalInput").ap()
    out = nc.dram_tensor("out_0", _OUT[0], F32, kind="ExternalOutput").ap()
    build_program(nc, aps, out)
    r = _run(nc, [arrays], core_ids=[0])
    return r.results[0]["out_0"]
```
